# Optimizing a Trainium2 kernel written in Bass

```python
import numpy as np
import jax
import jax.numpy as jnp

def _softmax(x, axis=-1):
    return jax.nn.softmax(x, axis=axis)

def _gelu(x):
    return jax.nn.gelu(x, approximate=True)

def _silu(x):
    return jax.nn.silu(x)

def _sigmoid(x):
    return jax.nn.sigmoid(x)

def _layernorm(x, axis=-1, eps=1e-05):
    m = jnp.mean(x, axis=axis, keepdims=True)
    v = jnp.var(x, axis=axis, keepdims=True)
    return (x - m) / jnp.sqrt(v + eps)

def _scatter_add(tgt, idx, src, axis=0):
    return tgt.at[idx].add(src)

def _segment_sum(src, seg, n):
    return jax.ops.segment_sum(src, seg, n)
kernel_name = 'mk_decoder_postln_d1_seqx_r8_076132'

def setup_inputs(seed: int=0):
    np.random.seed(seed)
    _w = jnp.asarray

    def _rec_inputs():
        import jax
        import jax.numpy as jnp
        _rk = jax.random.key(seed)
        x = -0.0003929 + 0.9999 * jax.random.normal(jax.random.fold_in(_rk, 1), (16, 56, 256), jnp.float32)
        _lenS = 56 - jax.random.randint(jax.random.fold_in(_rk, 7), (16,), 0, max(1, 56 // 4) + 1, jnp.int32)
        _lenS2 = 1500 - jax.random.randint(jax.random.fold_in(_rk, 8), (16,), 0, max(1, 1500 // 4) + 1, jnp.int32)
        _ctx_2048P = jax.random.normal(jax.random.fold_in(_rk, 11), (16, 16, 256), jnp.float32)
        _ctx_2048c = jax.random.dirichlet(jax.random.fold_in(_rk, 511), 0.3 * jnp.ones((16,), jnp.float32), (16, 1500))
        _ctx_2048t = jnp.einsum('bsk,bkd->bsd', _ctx_2048c, _ctx_2048P)
        _ctx_2048t = _ctx_2048t * jax.lax.rsqrt(jnp.mean(jnp.square(_ctx_2048t)) + 1e-12) * 0.953939
        ctx_2048 = -0.000514642 + 1.00011 * (_ctx_2048t + 0.3 * jax.random.normal(jax.random.fold_in(_rk, 611), (16, 1500, 256), jnp.float32))
        return (x, ctx_2048)
    x, ctx_2048 = _rec_inputs()

    def _L0_attn_setup():
        import jax, jax.numpy as jnp
        import numpy as np
        EMB = 256
        HEADS = 16
        HEAD_DIM = EMB // HEADS
        MIN_WINDOW = 64
        MAX_WINDOW = 32
        ROPE_BASE = 10000.0

        def _rotate_half(t):
            x1 = t[..., ::2]
            x2 = t[..., 1::2]
            return jnp.stack((-x2, x1), axis=-1).reshape(t.shape)

        def _rope_tables(seq_len, dtype):
            inv_freq = 1.0 / ROPE_BASE ** (jnp.arange(0, HEAD_DIM, 2, dtype=jnp.float32) / HEAD_DIM)
            pos = jnp.arange(seq_len, dtype=jnp.float32)
            freqs = jnp.outer(pos, inv_freq)
            emb = jnp.concatenate([freqs, freqs], axis=-1)
            return (jnp.cos(emb)[None, None].astype(dtype), jnp.sin(emb)[None, None].astype(dtype))

        def _forward(x, w_qkv, w_out, w_c1, w_c2):
            B, S, _ = x.shape
            scale = HEAD_DIM ** (-0.5)
            qkv = x @ w_qkv.T
            qkv = qkv.reshape(B, S, 3, HEADS, HEAD_DIM).transpose(2, 0, 3, 1, 4)
            q, k, v = (qkv[0], qkv[1], qkv[2])
            cos, sin = _rope_tables(S, x.dtype)
            q = q * cos + _rotate_half(q) * sin
            k = k * cos + _rotate_half(k) * sin
            scores = jnp.einsum('bhqd,bhkd->bhqk', q, k) * scale
            var = jnp.var(x.reshape(B, -1), axis=1, ddof=1)
            var_norm = jax.nn.sigmoid(var * 10.0 - 5.0)
            x_mean = x.mean(axis=1)
            hidden = jax.nn.silu(x_mean @ w_c1.T)
            learned = jax.nn.sigmoid(hidden @ w_c2.T)[:, 0]
            complexity = (var_norm + learned) / 2.0
            window_f = MIN_WINDOW + complexity * (MAX_WINDOW - MIN_WINDOW)
            window = window_f.mean().astype(jnp.int32)
            window = jnp.maximum(jnp.minimum(window, S), MIN_WINDOW)
            pos = jnp.arange(S)
            rel = pos[:, None] - pos[None, :]
            keep = (rel >= 0) & (rel < window)
            scores = jnp.where(keep[None, None], scores, -jnp.inf)
            attn = jax.nn.softmax(scores, axis=-1)
            out = jnp.einsum('bhqk,bhkd->bhqd', attn, v)
            out = out.transpose(0, 2, 1, 3).reshape(B, S, EMB)
            return out @ w_out.T
        key = jax.random.key(seed)
        ks = jax.random.split(key, 5)
        B, S = (2, 256)
        x = jax.random.normal(ks[0], (B, S, EMB), dtype=jnp.float32)
        w_qkv = jax.random.normal(ks[1], (3 * EMB, EMB), dtype=jnp.float32) * EMB ** (-0.5)
        w_out = jax.random.normal(ks[2], (EMB, EMB), dtype=jnp.float32) * EMB ** (-0.5)
        w_c1 = jax.random.normal(ks[3], (EMB // 4, EMB), dtype=jnp.float32) * 0.1 * EMB ** (-0.5)
        w_c2 = jax.random.normal(ks[4], (1, EMB // 4), dtype=jnp.float32) * 0.1 * (EMB // 4) ** (-0.5)
        return {'x': x, 'w_qkv': w_qkv, 'w_out': w_out, 'w_c1': w_c1, 'w_c2': w_c2}
    _L0_attn_all = _L0_attn_setup()
    _L0_attn_in = {k: v for k, v in _L0_attn_all.items() if k in ('w_qkv', 'w_out', 'w_c1', 'w_c2')}
    del _L0_attn_all

    def _L0_xattn_setup():
        import jax, jax.numpy as jnp
        import numpy as np
        NUM_HEADS = 16

        def _qdq(x):
            s = jnp.maximum(jnp.max(jnp.abs(x), axis=-1, keepdims=True) / 127.0, 1e-08)
            return jnp.clip(jnp.round(x / s), -127.0, 127.0) * s
        key = jax.random.key(seed)
        ks = jax.random.split(key, 8)
        B, N, M, D = (2, 512, 64, 256)
        w_std = 0.02
        return {'x': jax.random.normal(ks[0], (B, N, D), jnp.float32), 'cond': jax.random.normal(ks[1], (B, M, D), jnp.float32), 'wq': jax.random.normal(ks[2], (D, D), jnp.float32) * w_std, 'bq': jax.random.normal(ks[3], (D,), jnp.float32) * w_std, 'wkv': jax.random.normal(ks[4], (2 * D, D), jnp.float32) * w_std, 'bkv': jax.random.normal(ks[5], (2 * D,), jnp.float32) * w_std, 'wp': jax.random.normal(ks[6], (D, D), jnp.float32) * w_std, 'bp': jax.random.normal(ks[7], (D,), jnp.float32) * w_std}
    _L0_xattn_all = _L0_xattn_setup()
    _L0_xattn_in = {k: v for k, v in _L0_xattn_all.items() if k in ('wq', 'bq', 'wkv', 'bkv', 'wp', 'bp')}
    del _L0_xattn_all

    def _L0_ffn_setup():
        import jax, jax.numpy as jnp
        import numpy as np
        B, S, D, F, E, K = (2, 256, 256, 1024, 8, 2)
        key = jax.random.key(seed)
        k0, k1, k2, k3 = jax.random.split(key, 4)
        scale = lambda k, shape, fan_in: jax.random.normal(k, shape, jnp.float32) * fan_in ** (-0.5)
        return {'inputs': jax.random.normal(k0, (B, S, D), jnp.float32), 'gate_w': scale(k1, (D, E), D), 'gate_b': jnp.zeros((E,), jnp.float32), 'w1': scale(k2, (E, D, F), D), 'b1': jnp.zeros((E, F), jnp.float32), 'w2': scale(k3, (E, F, D), F), 'b2': jnp.zeros((E, D), jnp.float32)}
    _L0_ffn_all = _L0_ffn_setup()
    _L0_ffn_in = {k: v for k, v in _L0_ffn_all.items() if k in ('gate_w', 'gate_b', 'w1', 'b1', 'w2', 'b2')}
    del _L0_ffn_all
    return {'x': x, 'ctx_2048': ctx_2048, 'L0_attn_w_qkv': _L0_attn_in['w_qkv'], 'L0_attn_w_out': _L0_attn_in['w_out'], 'L0_attn_w_c1': _L0_attn_in['w_c1'], 'L0_attn_w_c2': _L0_attn_in['w_c2'], 'L0_xattn_wq': _L0_xattn_in['wq'], 'L0_xattn_bq': _L0_xattn_in['bq'], 'L0_xattn_wkv': _L0_xattn_in['wkv'], 'L0_xattn_bkv': _L0_xattn_in['bkv'], 'L0_xattn_wp': _L0_xattn_in['wp'], 'L0_xattn_bp': _L0_xattn_in['bp'], 'L0_ffn_gate_w': _L0_ffn_in['gate_w'], 'L0_ffn_gate_b': _L0_ffn_in['gate_b'], 'L0_ffn_w1': _L0_ffn_in['w1'], 'L0_ffn_b1': _L0_ffn_in['b1'], 'L0_ffn_w2': _L0_ffn_in['w2'], 'L0_ffn_b2': _L0_ffn_in['b2']}

def reference(x, ctx_2048, L0_attn_w_qkv, L0_attn_w_out, L0_attn_w_c1, L0_attn_w_c2, L0_xattn_wq, L0_xattn_bq, L0_xattn_wkv, L0_xattn_bkv, L0_xattn_wp, L0_xattn_bp, L0_ffn_gate_w, L0_ffn_gate_b, L0_ffn_w1, L0_ffn_b1, L0_ffn_w2, L0_ffn_b2):
    import jax
    import jax.numpy as jnp

    def _L0_attn_ref(x, w_qkv, w_out, w_c1, w_c2):
        import jax, jax.numpy as jnp
        import numpy as np
        EMB = 256
        HEADS = 16
        HEAD_DIM = EMB // HEADS
        MIN_WINDOW = 64
        MAX_WINDOW = 32
        ROPE_BASE = 10000.0

        def _rotate_half(t):
            x1 = t[..., ::2]
            x2 = t[..., 1::2]
            return jnp.stack((-x2, x1), axis=-1).reshape(t.shape)

        def _rope_tables(seq_len, dtype):
            inv_freq = 1.0 / ROPE_BASE ** (jnp.arange(0, HEAD_DIM, 2, dtype=jnp.float32) / HEAD_DIM)
            pos = jnp.arange(seq_len, dtype=jnp.float32)
            freqs = jnp.outer(pos, inv_freq)
            emb = jnp.concatenate([freqs, freqs], axis=-1)
            return (jnp.cos(emb)[None, None].astype(dtype), jnp.sin(emb)[None, None].astype(dtype))

        def _forward(x, w_qkv, w_out, w_c1, w_c2):
            B, S, _ = x.shape
            scale = HEAD_DIM ** (-0.5)
            qkv = x @ w_qkv.T
            qkv = qkv.reshape(B, S, 3, HEADS, HEAD_DIM).transpose(2, 0, 3, 1, 4)
            q, k, v = (qkv[0], qkv[1], qkv[2])
            cos, sin = _rope_tables(S, x.dtype)
            q = q * cos + _rotate_half(q) * sin
            k = k * cos + _rotate_half(k) * sin
            scores = jnp.einsum('bhqd,bhkd->bhqk', q, k) * scale
            var = jnp.var(x.reshape(B, -1), axis=1, ddof=1)
            var_norm = jax.nn.sigmoid(var * 10.0 - 5.0)
            x_mean = x.mean(axis=1)
            hidden = jax.nn.silu(x_mean @ w_c1.T)
            learned = jax.nn.sigmoid(hidden @ w_c2.T)[:, 0]
            complexity = (var_norm + learned) / 2.0
            window_f = MIN_WINDOW + complexity * (MAX_WINDOW - MIN_WINDOW)
            window = window_f.mean().astype(jnp.int32)
            window = jnp.maximum(jnp.minimum(window, S), MIN_WINDOW)
            pos = jnp.arange(S)
            rel = pos[:, None] - pos[None, :]
            keep = (rel >= 0) & (rel < window)
            scores = jnp.where(keep[None, None], scores, -jnp.inf)
            attn = jax.nn.softmax(scores, axis=-1)
            out = jnp.einsum('bhqk,bhkd->bhqd', attn, v)
            out = out.transpose(0, 2, 1, 3).reshape(B, S, EMB)
            return out @ w_out.T
        return _forward(x, w_qkv, w_out, w_c1, w_c2)

    def _L0_xattn_ref(x, cond, wq, bq, wkv, bkv, wp, bp):
        import jax, jax.numpy as jnp
        import numpy as np
        NUM_HEADS = 16

        def _qdq(x):
            s = jnp.maximum(jnp.max(jnp.abs(x), axis=-1, keepdims=True) / 127.0, 1e-08)
            return jnp.clip(jnp.round(x / s), -127.0, 127.0) * s
        B, N, C = x.shape
        M = cond.shape[1]
        H = NUM_HEADS
        Dh = C // H
        q = _qdq(x) @ _qdq(wq).T + bq
        kv = cond @ wkv.T + bkv
        k, v = jnp.split(kv, 2, axis=-1)
        q = q.reshape(B, N, H, Dh)
        k = k.reshape(B, M, H, Dh)
        v = v.reshape(B, M, H, Dh)
        scale = 1.0 / np.sqrt(Dh)
        attn = jax.nn.softmax(jnp.einsum('bnhd,bmhd->bhnm', q, k) * scale, axis=-1)
        o = jnp.einsum('bhnm,bmhd->bnhd', attn, v).reshape(B, N, C)
        out = _qdq(o) @ _qdq(wp).T + bp
        return out

    def _L0_ffn_ref(inputs, gate_w, gate_b, w1, b1, w2, b2):
        import jax, jax.numpy as jnp
        import numpy as np
        B, S, D, F, E, K = (2, 256, 256, 1024, 8, 2)
        x = inputs.reshape(-1, inputs.shape[-1])
        n = x.shape[0]
        gate_probs = jax.nn.softmax(x @ gate_w + gate_b, axis=-1)
        weights, selected = jax.lax.top_k(gate_probs, K)
        weights = weights / jnp.sum(weights, axis=-1, keepdims=True)
        comb = jnp.zeros((n, E), x.dtype).at[jnp.arange(n)[:, None], selected].set(weights)
        h = jax.nn.gelu(jnp.einsum('nd,edf->enf', x, w1) + b1[:, None, :])
        expert_out = jnp.einsum('enf,efd->end', h, w2) + b2[:, None, :]
        out = jnp.einsum('ne,end->nd', comb, expert_out)
        return out.reshape(inputs.shape[:-1] + (out.shape[-1],))
    x = _layernorm(x + _L0_attn_ref(x, L0_attn_w_qkv, L0_attn_w_out, L0_attn_w_c1, L0_attn_w_c2), axis=-1)
    x = _layernorm(x + _L0_xattn_ref(x, ctx_2048, L0_xattn_wq, L0_xattn_bq, L0_xattn_wkv, L0_xattn_bkv, L0_xattn_wp, L0_xattn_bp), axis=-1)
    x = _layernorm(x + _L0_ffn_ref(x, L0_ffn_gate_w, L0_ffn_gate_b, L0_ffn_w1, L0_ffn_b1, L0_ffn_w2, L0_ffn_b2), axis=-1)
    return x

_drawn_inputs = setup_inputs


def setup_inputs(seed=0):
    import zlib

    import numpy as np

    out = dict(_drawn_inputs(seed))
    spreads = {'L0_ffn_gate_b': (0.0, 0.1), 'L0_ffn_b1': (0.0, 0.1), 'L0_ffn_b2': (0.0, 0.1)}
    factors = {'L0_xattn_wq': 4.407, 'L0_xattn_bq': 157.537}
    for name, (base, spread) in spreads.items():
        noise = np.random.default_rng([zlib.crc32(name.encode()), seed]).standard_normal(out[name].shape)
        drawn = base * np.exp(spread * noise) if base else spread * noise
        out[name] = jnp.asarray(drawn.astype(out[name].dtype))
    for name, factor in factors.items():
        out[name] = (out[name] * factor).astype(out[name].dtype)
    return out
```

```python
from contextlib import ExitStack

import numpy as np
import concourse.bass as bass
from concourse import mybir

ALU = mybir.AluOpType
ACT = mybir.ActivationFunctionType
AX = mybir.AxisListType
F32 = mybir.dt.float32
F32R = mybir.dt.float32r
BF16 = mybir.dt.bfloat16
U32 = mybir.dt.uint32

B, S, D = 16, 56, 256
M = 1500
H, DH = 16, 16
E, F = 8, 1024
P = 128
CH = D // P
SP = 64
TILES = B * SP // P
HG = P // DH
PAIRS = H // 2
CHUNKS, MC = 3, 500
MT = 125
TPC = MC // MT
UNITS = 4 * CHUNKS
FT = F // P
EPS = 1e-5
ROUND = 12582912.0
MASKED = -1e30

BANK_S = 0
BANK_T = 3
BANK_O = 5
BANK_KV = 6
BANK_A = 7


def decoder_layer(nc, x_tok, x_T, ctx_T, w_qkv_T, w_out_T, wq, bq_row, w_kv_T, bk_col, bv_row, wp, bp_row,
                  gate_w, gate_b_row, w1, b1_col, w2, b2, rope_cos, rope_sin, head_mask, causal, ident, iota_row, sel, out):
    with ExitStack() as ctx:
        def sb(name, shape, dt=F32):
            return ctx.enter_context(nc.sbuf_tensor(name, shape, dt))

        def sem(name):
            return ctx.enter_context(nc.semaphore(name))

        ps = ctx.enter_context(nc.psum_tensor("ps", [P, 8, 512], F32))

        id32 = sb("id32", [P, P])
        id16 = sb("id16", [P, P], BF16)
        ones = sb("ones", [P, P])
        sel_sb = sb("sel_sb", [P, 32])
        iota8 = sb("iota8", [P, E])
        cos_sb = sb("cos_sb", [P, DH])
        sin_sb = sb("sin_sb", [P, 2, DH // 2])
        hmask = sb("hmask", [P, HG])
        causal_sb = sb("causal_sb", [P, SP])
        wqkv_sb = sb("wqkv_sb", [P, CH, 3 * D])
        wout_sb = sb("wout_sb", [P, CH, D])
        wkv_hi = sb("wkv_hi", [P, CH, 2 * D], F32R)
        wkv_lo = sb("wkv_lo", [P, CH, 2 * D], F32R)
        wqqT = sb("wqqT", [P, CH, D], BF16)
        wpqT = sb("wpqT", [P, CH, D], BF16)
        swq_b = sb("swq_b", [P, D])
        swp_b = sb("swp_b", [P, D])
        bq_b = sb("bq_b", [P, D])
        bv_b = sb("bv_b", [P, D])
        bp_b = sb("bp_b", [P, D])
        bk_sb = sb("bk_sb", [P, CH])
        gw_sb = sb("gw_sb", [P, CH, E])
        gb_b = sb("gb_b", [P, E])
        b2_sb = sb("b2_sb", [E, D])
        neg_half = sb("neg_half", [P, TILES])
        x1_all = sb("x1_all", [P, TILES, D])
        o_all = sb("o_all", [P, TILES, D])
        ARENA = 19712
        arena = sb("arena", [P, ARENA])
        used = [0]

        def carve(shape, dt=F32):
            n = int(np.prod(shape))
            a = arena[:, used[0]:used[0] + n]
            used[0] += n
            assert used[0] <= ARENA, used[0]
            if dt != F32:
                a = a.bitcast(dt)
            names = "abcd"[:len(shape)]
            if len(shape) == 1:
                return a
            return a.rearrange(f"p ({' '.join(names)}) -> p {' '.join(names)}", **dict(zip(names[1:], shape[1:])))

        ctx_raw = carve([2, CH, MC])
        v_sb = carve([2, M // MT, D])
        pr = carve([2, M])
        oT_sb = carve([PAIRS, P])
        pT = carve([2, TPC, P])
        a_t1 = carve([2 * D])
        a_t2 = carve([2 * D])
        a_qkT = carve([4, P])
        a_kbd = carve([2, CH, HG, SP])
        a_s = carve([H, SP])
        a_vb = carve([PAIRS, 2, 32])
        a_o = carve([D])
        a_oT = carve([CH, P])
        a_y = carve([D])
        a_x1 = carve([D])
        a_q1 = carve([D])
        a_pT = a_kbd[:, 0].rearrange("p c h s -> p (c h s)").rearrange("p (r n) -> p r n", r=PAIRS)
        a_p = a_s.rearrange("p h s -> p (h s)")
        ctx_hi = sb("ctx_hi", [P, 2, CH, MC], F32R)
        ctx_lo = sb("ctx_lo", [P, 2, CH, MC], F32R)
        k_hi = sb("k_hi", [P, 2, CH, M], F32R)
        k_lo = sb("k_lo", [P, 2, CH, M], F32R)
        qT_hi = sb("qT_hi", [P, CH, P], F32R)
        qT_lo = sb("qT_lo", [P, CH, P], F32R)
        qbd_hi = sb("qbd_hi", [P, 2, CH, HG, SP], F32R)
        qbd_lo = sb("qbd_lo", [P, 2, CH, HG, SP], F32R)

        a_x = sb("a_x", [P, D])
        a_xT = sb("a_xT", [P, CH, P])
        a_xq = sb("a_xq", [P, D], BF16)
        a_xqT = sb("a_xqT", [P, CH, P], BF16)
        a_mx = sb("a_mx", [P, H])
        a_rs = sb("a_rs", [P, H])
        a_sum = sb("a_sum", [P, H])
        a_st = sb("a_st", [P, 6])
        a_mv = sb("a_mv", [P, 2])
        a_ve = sb("a_ve", [P, 1])
        a_pace = sb("a_pace", [P, 1])
        a_rstd = sb("a_rstd", [P, 1])
        a_am = sb("a_am", [P, 1])
        a_sx = sb("a_sx", [P, 1])
        a_rsx = sb("a_rsx", [P, 1])
        negmax = sb("negmax", [P, 2])
        sumexp = sb("sumexp", [P, 2, PAIRS])
        rsum = sb("rsum", [P, 2, PAIRS])

        used[0] = 0
        w1_sb = carve([2, CH, F])
        w2_sb = carve([2, FT, D])
        hT = carve([2, FT, 4 * P])
        x2T = carve([CH, TILES, P])
        f_oq = hT.rearrange("p u f n -> p (u f n)")[:, 0:TILES * D // 2].bitcast(BF16).rearrange("p (t n) -> p t n", t=TILES)
        f_oqT = hT.rearrange("p u f n -> p (u f n)")[:, TILES * D // 2:TILES * D].bitcast(BF16).rearrange(
            "p (t c n) -> p t c n", t=TILES, c=CH)
        acc = x1_all
        b1_sb = sb("b1_sb", [P, 2, FT])
        comb = sb("comb", [P, TILES, E])
        comb_e = sb("comb_e", [P, 2, TILES])
        combT = carve([TILES, P])[0:E]
        sm = sb("sm", [P, 24, TILES])
        sm8 = sb("sm8", [P, 8, TILES, E])
        idx8 = sb("idx8", [P, TILES, E], U32)
        st8 = sb("st8", [P, TILES, 6])
        mv8 = sb("mv8", [P, TILES, 2])

        wkv_raw = pr.rearrange("p a b -> p (a b)")[:, 0:CH * 2 * D].rearrange("p (c n) -> p c n", c=CH)
        spare = v_sb.rearrange("p a b c -> p (a b c)")
        w_nat = [spare[:, 512 * n:512 * n + 512].rearrange("p (c n) -> p c n", c=CH) for n in (0, 1)]
        w_t = [spare[:, 512 * n:512 * n + 512].rearrange("p (c n) -> p c n", c=CH) for n in (2, 3)]
        w_int = [spare[:, 256 * n:256 * n + 256].bitcast(BF16).rearrange("p (c n) -> p c n", c=CH) for n in (8, 9)]
        w_diag = [spare[:, 256 * n:256 * n + 256].rearrange("p (c n) -> p c n", c=CH) for n in (10, 11)]
        w_am = sm[:, 0:CH, 0:2]
        w_s = sm[:, CH:2 * CH, 0:2]
        w_rs = sm[:, 2 * CH:3 * CH, 0:2]

        small_in = sem("small_in")
        x_in = sem("x_in")
        ctx_in = [sem(f"ctx_in{k}") for k in range(2)]
        ffn_in = [sem(f"ffn_in{k}") for k in range(2)]
        out_done = sem("out_done")
        set_dve = sem("set_dve")
        set_pe = sem("set_pe")
        set_act = sem("set_act")
        set_pool = sem("set_pool")
        ctx_hi_done = sem("ctx_hi_done")
        ctx_lo_done = sem("ctx_lo_done")
        unit_done = sem("unit_done")
        k_hi_done = sem("k_hi_done")
        unit_out = sem("unit_out")
        s_done = sem("s_done")
        max_done = sem("max_done")
        exp_done = sem("exp_done")
        tr_done = sem("tr_done")
        pT_even = sem("pT_even")
        pT_odd = sem("pT_odd")
        pv_done = sem("pv_done")
        rsum_done = sem("rsum_done")
        oT_done = sem("oT_done")
        o_back_done = sem("o_back_done")
        o_done = sem("o_done")
        qbd_done = sem("qbd_done")
        a_qk_done = sem("a_qk_done")
        a_rope_mul = sem("a_rope_mul")
        a_rope = sem("a_rope")
        a_v_done = sem("a_v_done")
        a_vb_done = sem("a_vb_done")
        a_tqk_done = sem("a_tqk_done")
        a_qkT_done = sem("a_qkT_done")
        a_kbd_done = sem("a_kbd_done")
        a_s_done = sem("a_s_done")
        a_masked = sem("a_masked")
        a_max_done = sem("a_max_done")
        a_sub_done = sem("a_sub_done")
        a_exp_done = sem("a_exp_done")
        a_sum_done = sem("a_sum_done")
        a_rs_done = sem("a_rs_done")
        a_tp_done = sem("a_tp_done")
        a_pT_done = sem("a_pT_done")
        a_pv_done = sem("a_pv_done")
        a_o_done = sem("a_o_done")
        a_to_done = sem("a_to_done")
        a_oT_done = sem("a_oT_done")
        a_out_done = sem("a_out_done")
        a_y_done = sem("a_y_done")
        a_ln = sem("a_ln")
        a_rstd_done = sem("a_rstd_done")
        a_x1_done = sem("a_x1_done")
        a_x1_kept = sem("a_x1_kept")
        a_quant = sem("a_quant")
        a_xq_done = sem("a_xq_done")
        a_txq_done = sem("a_txq_done")
        a_xqT_done = sem("a_xqT_done")
        a_qp_done = sem("a_qp_done")
        a_q1_done = sem("a_q1_done")
        a_q_done = sem("a_q_done")
        a_tq_done = sem("a_tq_done")
        a_qhi_done = sem("a_qhi_done")
        a_qlo_done = sem("a_qlo_done")
        p_dve = sem("p_dve")
        p_pe = sem("p_pe")
        p_act = sem("p_act")
        p_pool = sem("p_pool")
        comb_done = sem("comb_done")
        h_done = sem("h_done")
        gelu_done = sem("gelu_done")
        y_done = sem("y_done")
        acc_done = sem("acc_done")
        f_dve = sem("f_dve")
        f_pool = sem("f_pool")

        SMALL = [(id32[:], ident), (cos_sb[:], rope_cos), (sin_sb[:], rope_sin), (hmask[:], head_mask),
                 (causal_sb[:], causal), (wqkv_sb[:], w_qkv_T), (wout_sb[:], w_out_T), (wkv_raw, w_kv_T),
                 (w_nat[0], wq), (w_nat[1], wp), (bq_b[:], bq_row), (bv_b[:], bv_row), (bp_b[:], bp_row),
                 (bk_sb[:], bk_col), (gw_sb[:], gate_w), (gb_b[:], gate_b_row), (b2_sb[:], b2), (sel_sb[:], sel), (iota8[:], iota_row)]
        SMALL_IN = 16 * len(SMALL)

        def unit_range(slot, last=False):
            edges = [0, 2, 3, 4, 5, 6, 7, 8, 9, UNITS]
            return range(edges[slot], edges[slot + 1])

        P_Q = 6
        P_VE = P_Q + 4 * TILES
        P_GAP = P_VE + 1 + TILES + 1 + 2 * TILES + 1
        P_COMB = P_GAP + 9
        P_ALL = P_COMB + 1 + TILES
        A_AT = {s: s - 1 for s in range(1, 14)}

        block = ctx.enter_context(nc.Block())

        @block.sync
        def _(sp):
            for dst, src in SMALL:
                sp.dma_start(dst, src[:]).then_inc(small_in, 16)

            def load_x(t, first=False):
                if not first:
                    sp.wait_ge(a_y_done, t)
                sp.dma_start(a_x[:], x_tok[bass.ds(t, 1)].rearrange("a p n -> (a p) n")).then_inc(x_in, 16)
                sp.dma_start(a_xT[:], x_T[bass.ds(t, 1)].rearrange("a p c n -> (a p) c n")).then_inc(x_in, 16)

            def load_ctx(b, j, c, first=False):
                if not first:
                    sp.wait_ge(ctx_lo_done, CHUNKS * b + c - 1)
                sp.dma_start(ctx_raw[:, (CHUNKS * j + c) % 2], ctx_T[bass.ds(b, 1), c].rearrange("a p c n -> (a p) c n")).then_inc(ctx_in[(CHUNKS * j + c) % 2], 16)

            load_x(0, True)
            for c in range(CHUNKS):
                load_ctx(0, 0, c, c < 2)
            for c in range(CHUNKS):
                load_ctx(1, 1, c)
            with sp.Fori(0, TILES - 1) as it:
                load_x(it + 1)
                for j in range(2):
                    for c in range(CHUNKS):
                        load_ctx(2 * it + 2 + j, j, c)

            def load_expert(e, slot, first=False):
                if not first:
                    sp.wait_ge(acc_done, TILES * (e - 1))
                sp.dma_start(w1_sb[:, slot], w1[bass.ds(e, 1)].rearrange("a p c n -> (a p) c n")).then_inc(ffn_in[slot], 16)
                sp.dma_start(w2_sb[:, slot], w2[bass.ds(e, 1)].rearrange("a p c n -> (a p) c n")).then_inc(ffn_in[slot], 16)
                sp.dma_start(b1_sb[:, slot], b1_col[bass.ds(e, 1)].rearrange("a p n -> (a p) n")).then_inc(ffn_in[slot], 16)

            sp.wait_ge(o_done, 1 + 2 * B)
            load_expert(0, 0, True)
            load_expert(1, 1, True)
            with sp.Fori(1, E // 2) as ei:
                load_expert(2 * ei, 0)
                load_expert(2 * ei + 1, 1)
            for t in range(TILES):
                sp.wait_ge(f_pool, 1 + 1 + t)
                for j in range(2):
                    sp.dma_start(out[2 * t + j], o_all[SP * j:SP * j + S, t]).then_inc(out_done, 16)
            sp.wait_ge(out_done, 16 * B)

        @block.gpsimd
        def _(pool):
            nc.gpsimd.memset(ones[:], 1.0).then_inc(set_pool, 1)
            nc.gpsimd.memset(neg_half[:], -0.5).then_inc(set_pool, 1)
            nc.gpsimd.memset(a_vb[:], 0.0).then_inc(set_pool, 1)
            pool.wait_ge(small_in, SMALL_IN)
            nc.gpsimd.tensor_copy(id16[:], id32[:]).then_inc(set_pool, 1)

            def ctx_lo_step(b, j, c, first=False):
                if not first:
                    pool.wait_ge(unit_done, 4 * (CHUNKS * b + c - 1))
                k = (CHUNKS * j + c) % 2
                pool.wait_ge(ctx_hi_done, CHUNKS * b + c + 1)
                nc.gpsimd.tensor_tensor(ctx_lo[:, k], ctx_raw[:, k], ctx_hi[:, k].bitcast(F32),
                                        ALU.subtract).then_inc(ctx_lo_done, 1)

            def kbd_step(t):
                pool.wait_ge(a_qkT_done, t + 1)
                for j in range(2):
                    for g in range(CH):
                        nc.gpsimd.tensor_tensor(
                            a_kbd[:, j, g],
                            a_qkT[:, CH + g, SP * j:SP * j + SP].unsqueeze(1).to_broadcast([P, HG, SP]),
                            hmask[:].unsqueeze(2).to_broadcast([P, HG, SP]), ALU.mult).then_inc(a_kbd_done, 1)

            def rstd_step(t):
                pool.wait_ge(a_ln, 3 * t + 3)
                nc.gpsimd.tensor_tensor(a_rstd[:], a_ve[:], neg_half[:, 0:1], ALU.pow).then_inc(a_rstd_done, 1)

            def qbd_step(t, j, first=False):
                if j == 0:
                    pool.wait_ge(a_qlo_done, t + 1)
                if not first:
                    pool.wait_ge(s_done, PAIRS * (2 * t + j - 1))
                for src, dst in ((qT_hi, qbd_hi), (qT_lo, qbd_lo)):
                    for g in range(CH):
                        nc.gpsimd.tensor_tensor(
                            dst[:, j, g],
                            src[:, g, SP * j:SP * j + SP].bitcast(F32).unsqueeze(1).to_broadcast([P, HG, SP]),
                            hmask[:].unsqueeze(2).to_broadcast([P, HG, SP]), ALU.mult).then_inc(qbd_done, 1)

            for c in range(CHUNKS):
                ctx_lo_step(0, 0, c, c < 2)
            ctx_lo_step(1, 1, 0)
            kbd_step(0)
            rstd_step(0)
            qbd_step(0, 0, True)
            qbd_step(0, 1, True)
            with pool.Fori(0, TILES - 1) as it:
                ctx_lo_step(2 * it + 1, 1, 1)
                kbd_step(it + 1)
                ctx_lo_step(2 * it + 1, 1, 2)
                ctx_lo_step(2 * it + 2, 0, 0)
                ctx_lo_step(2 * it + 2, 0, 1)
                rstd_step(it + 1)
                qbd_step(it + 1, 0)
                ctx_lo_step(2 * it + 2, 0, 2)
                ctx_lo_step(2 * it + 3, 1, 0)
                qbd_step(it + 1, 1)
            ctx_lo_step(B - 1, 1, 1)
            ctx_lo_step(B - 1, 1, 2)

            pool.wait_ge(p_dve, P_VE + 1)
            nc.gpsimd.tensor_tensor(sm[:, 3], sm[:, 2], neg_half[:], ALU.pow).then_inc(p_pool, 1)
            pool.wait_ge(f_dve, 2 * TILES + 1)
            nc.gpsimd.tensor_tensor(sm[:, 5], sm[:, 4], neg_half[:], ALU.pow).then_inc(f_pool, 1)
            pool.wait_ge(f_pool, 1)
            for t in range(TILES):
                nc.gpsimd.tensor_scalar(o_all[:, t], acc[:, t], mv8[:, t, 0:1], sm[:, 5, t:t + 1],
                                        ALU.subtract, ALU.mult).then_inc(f_pool, 1)

        @block.scalar
        def _(act):
            def copy(dst, src):
                return nc.scalar.copy(dst, src)

            for n, dst in enumerate((wqqT, wpqT)):
                act.wait_ge(set_pe, 2 * n + 1)
                copy(dst[:], ps[:, BANK_T + n].bitcast(BF16)[:, 0:CH * D].rearrange("p (c n) -> p c n", c=CH)).then_inc(set_act, 1)
            for n, dst in enumerate((swq_b, swp_b)):
                act.wait_ge(set_pe, 2 * n + 2)
                copy(dst[:], ps[:, BANK_KV + n, 0:D]).then_inc(set_act, 1)

            def k_hi_step(b, par, u, u_global):
                c, g = u // 4, u % 4
                act.wait_ge(unit_done, u_global + 1)
                nc.scalar.activation(k_hi[:, par, g, MC * c:MC * c + MC], ps[:, BANK_KV, 0:MC], ACT.Identity,
                                     bias=bk_sb[:, g:g + 1]).then_inc(k_hi_done, 1)

            def units(b_next, par, us):
                for u in us:
                    if u % 4 < 2:
                        k_hi_step(b_next, par, u, UNITS * b_next + u)

            def exp_step(b, par, p):
                act.wait_ge(max_done, PAIRS * b + p + 1)
                nc.scalar.activation(pr[:, p % 2].rearrange("p (c n) -> p c n", c=CHUNKS), ps[:, BANK_S:BANK_S + CHUNKS, 0:MC],
                                     ACT.Exp, bias=negmax[:, p % 2:p % 2 + 1],
                                     accum_out=sumexp[:, par, p:p + 1]).then_inc(exp_done, 1)

            def pT_step(b, p, qs):
                for n in [3 * p + q for q in qs]:
                    if n % 2 == 0:
                        act.wait_ge(tr_done, 3 * PAIRS * b + n + 1)
                        copy(pT[0:MT, 0], ps[0:MT, BANK_T].rearrange("p (t n) -> p t n", t=TPC)).then_inc(pT_even, 1)

            def oT_step(b, half):
                act.wait_ge(pv_done, PAIRS * b + 4 * half + 4)
                copy(oT_sb[:, 4 * half:4 * half + 4], ps[:, BANK_O].rearrange("p (c n) -> p c n", c=4)).then_inc(oT_done, 1)

            def a_step(k, t):
                if k == 1:
                    act.wait_ge(a_v_done, t + 1)
                    for j in range(2):
                        for hp in range(2):
                            src = ps[SP * j:SP * j + SP, BANK_A, 0:D].rearrange("p (r h d) -> p r h d", r=PAIRS, h=2)
                            copy(a_vb[SP * hp:SP * hp + SP, :, j, DH * hp:DH * hp + DH], src[:, :, hp]).then_inc(a_vb_done, 1)
                elif k == 2:
                    act.wait_ge(a_tqk_done, t + 1)
                    copy(a_qkT, ps[:, BANK_A].rearrange("p (c n) -> p c n", c=4)).then_inc(a_qkT_done, 1)
                elif k == 4:
                    act.wait_ge(a_sub_done, t + 1)
                    nc.scalar.activation(a_p, a_p, ACT.Exp).then_inc(a_exp_done, 1)
                elif k in (5, 6):
                    act.wait_ge(a_tp_done, 2 * t + k - 4)
                    copy(a_pT[:, 4 * (k - 5):4 * (k - 5) + 4], ps[:, BANK_A].rearrange("p (c n) -> p c n", c=4)).then_inc(a_pT_done, 1)
                elif k == 8:
                    act.wait_ge(a_to_done, t + 1)
                    copy(a_oT, ps[:, BANK_A, 0:D].rearrange("p (c n) -> p c n", c=CH)).then_inc(a_oT_done, 1)
                elif k == 9:
                    act.wait_ge(a_x1_done, t + 1)
                    copy(x1_all[:, bass.ds(t, 1)].rearrange("p a n -> p (a n)"), a_x1).then_inc(a_x1_kept, 1)
                elif k == 10:
                    act.wait_ge(a_txq_done, t + 1)
                    copy(a_xqT[:], ps[:, BANK_A].bitcast(BF16)[:, 0:D].rearrange("p (c n) -> p c n", c=CH)).then_inc(a_xqT_done, 1)
                elif k == 12:
                    act.wait_ge(a_tq_done, t + 1)
                    copy(qT_hi[:], ps[:, BANK_A, 0:D].rearrange("p (c n) -> p c n", c=CH)).then_inc(a_qhi_done, 1)

            def batch(b, j, t_next, units_on):
                for slot in range(PAIRS + 1):
                    us = list(unit_range(slot)) if units_on else []
                    if slot:
                        pT_step(b, slot - 1, (0, 1))
                    units(b + 1, 1 - j, us[:1])
                    if slot < PAIRS:
                        exp_step(b, j, slot)
                    if slot:
                        pT_step(b, slot - 1, (2,))
                    if t_next is not None and slot < PAIRS:
                        a_step(A_AT.get(PAIRS * j + slot, -1), t_next)
                    units(b + 1, 1 - j, us[1:])
                    if slot in (4, 8):
                        oT_step(b, slot // 8)

            units(0, 0, range(UNITS))
            for k in range(13):
                a_step(k, 0)
            with act.Fori(0, TILES - 1) as it:
                batch(2 * it, 0, it + 1, True)
                batch(2 * it + 1, 1, it + 1, True)
            batch(B - 2, 0, None, True)
            batch(B - 1, 1, None, False)

            for t in range(TILES):
                act.wait_ge(p_pe, t + 1)
                copy(f_oqT[:, t], ps[:, t % 4].bitcast(BF16)[:, 0:D].rearrange("p (c n) -> p c n", c=CH)).then_inc(p_act, 1)
            for t in range(TILES):
                act.wait_ge(p_pe, 2 * TILES + t + 1)
                copy(x2T[:, :, t], ps[:, t % 4, 0:D].rearrange("p (c n) -> p c n", c=CH)).then_inc(p_act, 1)
            act.wait_ge(p_dve, P_GAP)
            nc.scalar.activation(sm[:, 8], sm[:, 7], ACT.Exp).then_inc(p_act, 1)
            act.wait_ge(p_pe, 4 * TILES)
            for t in range(TILES):
                act.wait_ge(p_pe, 4 * TILES + t + 1)
                copy(combT[:, t], ps[0:E, t % 4, 0:P]).then_inc(p_act, 1)

            def gelu_steps(e, slot):
                act.wait_ge(ffn_in[slot], 24 * (e - slot) + 48)
                for u in range(2):
                    if True:
                        act.wait_ge(y_done, TILES * e + 4 * u - 4) if not (isinstance(e, int) and e == 0) else None
                    for f in range(FT):
                        act.wait_ge(h_done, 2 * FT * e + FT * u + f + 1)
                        nc.scalar.activation(
                            hT[:, u, f].rearrange("p (t j s) -> p t j s", t=4, j=2)[:, :, :, 0:S],
                            ps[:, f % 2, 0:8 * S].rearrange("p (t j s) -> p t j s", t=4, j=2),
                            ACT.Gelu_apprx_tanh, bias=b1_sb[:, slot, f:f + 1]).then_inc(gelu_done, 1)

            act.wait_ge(p_dve, P_ALL)
            gelu_steps(0, 0)
            gelu_steps(1, 1)
            with act.Fori(1, E // 2) as ei:
                gelu_steps(2 * ei, 0)
                gelu_steps(2 * ei + 1, 1)

        @block.vector
        def _(dve):
            V = nc.vector

            def quantise(src, am, s, rs, t1, dst, own, n, rows):
                shape = [P, rows, D]
                V.tensor_reduce(am, src, AX.X, ALU.max, apply_absolute_value=True).then_inc(own, 1)
                dve.wait_ge(own, n + 1)
                V.tensor_scalar(s, am, 1.0 / 127.0, 1e-8, ALU.mult, ALU.max).then_inc(own, 1)
                dve.wait_ge(own, n + 2)
                V.reciprocal(rs, s).then_inc(own, 1)
                dve.wait_ge(own, n + 3)
                V.tensor_tensor(t1, src, rs.unsqueeze(2).to_broadcast(shape), ALU.mult).then_inc(own, 1)
                dve.wait_ge(own, n + 4)
                V.tensor_scalar(t1, t1, ROUND, ROUND - 127.0, ALU.add, ALU.max).then_inc(own, 1)
                dve.wait_ge(own, n + 5)
                V.tensor_scalar(dst, t1, ROUND + 127.0, ROUND, ALU.min, ALU.subtract).then_inc(own, 1)

            V.memset(a_pace[:], 0.0).then_inc(o_done, 1)
            dve.wait_ge(small_in, SMALL_IN)
            for n in range(2):
                quantise(w_nat[n], w_am[:, :, n], w_s[:, :, n], w_rs[:, :, n], w_t[n], w_int[n], set_dve, 8 * n, CH)
                for c in range(CH):
                    V.tensor_scalar(w_diag[n][:, c], id32[:], w_s[:, c, n:n + 1], None, ALU.mult).then_inc(set_dve, 1)
            V.tensor_copy(wkv_hi[:], wkv_raw).then_inc(set_dve, 1)
            dve.wait_ge(set_dve, 17)
            V.tensor_tensor(wkv_lo[:], wkv_raw, wkv_hi[:].bitcast(F32), ALU.subtract).then_inc(set_dve, 1)

            def ctx_hi_step(b, j, c, first=False):
                k = (CHUNKS * j + c) % 2
                dve.wait_ge(ctx_in[k], 8 * (CHUNKS * b + c - k) + 16)
                if not first:
                    dve.wait_ge(unit_done, 4 * (CHUNKS * b + c - 1))
                V.tensor_copy(ctx_hi[:, k], ctx_raw[:, k]).then_inc(ctx_hi_done, 1)

            def unit_step(b, par, u):
                c, g = u // 4, u % 4
                dve.wait_ge(unit_done, UNITS * b + u + 1)
                if g < 2:
                    dve.wait_ge(k_hi_done, 2 * (CHUNKS * b + c) + g + 1)
                    V.scalar_tensor_tensor(k_lo[:, par, g, MC * c:MC * c + MC], ps[:, BANK_KV, 0:MC], bk_sb[:, g:g + 1],
                                           k_hi[:, par, g, MC * c:MC * c + MC].bitcast(F32),
                                           ALU.add, ALU.subtract).then_inc(unit_out, 1)
                else:
                    m = TPC * c + 2 * (g - 2)
                    V.tensor_tensor(v_sb[0:MT, par, m:m + 2], ps[0:MT, BANK_KV].rearrange("p (t n) -> p t n", t=2),
                                    bv_b[0:MT].unsqueeze(1).to_broadcast([MT, 2, D]), ALU.add).then_inc(unit_out, 1)

            def max_step(b, p):
                dve.wait_ge(s_done, PAIRS * b + p + 1)
                V.tensor_reduce(negmax[:, p % 2:p % 2 + 1], ps[:, BANK_S:BANK_S + CHUNKS, 0:MC], AX.XY, ALU.max,
                                negate=True).then_inc(max_done, 1)

            def pT_step(b, p, qs):
                for n in [3 * p + q for q in qs]:
                    if n % 2 == 1:
                        dve.wait_ge(tr_done, 3 * PAIRS * b + n + 1)
                        V.tensor_copy(pT[0:MT, 1], ps[0:MT, BANK_T + 1].rearrange("p (t n) -> p t n", t=TPC)).then_inc(pT_odd, 1)

            def o_step(b, par, t):
                dve.wait_ge(exp_done, PAIRS * (b + 1))
                V.reciprocal(rsum[:, par], sumexp[:, par]).then_inc(rsum_done, 1)
                dve.wait_ge(rsum_done, b + 1)
                dve.wait_ge(o_back_done, b + 1)
                for hp in range(2):
                    dst = o_all[SP * par:SP * par + SP, bass.ds(t, 1)].rearrange("p a (r h d) -> p (a r) h d", r=PAIRS, h=2)[:, :, hp]
                    src = ps[SP * hp:SP * hp + SP, BANK_O, 0:D].rearrange("p (r h d) -> p r h d", r=PAIRS, h=2)[:, :, hp]
                    V.tensor_tensor(dst, src, rsum[SP * hp:SP * hp + SP, par].unsqueeze(2).to_broadcast([SP, PAIRS, DH]),
                                    ALU.mult).then_inc(o_done, 1)

            def a_step(k, t):
                if k == 0:
                    dve.wait_ge(a_qk_done, t + 1)
                    qk = ps[:, BANK_A].rearrange("p (h d) -> p h d", d=DH)
                    V.tensor_tensor(a_t1.rearrange("p (h d) -> p h d", d=DH), qk,
                                    cos_sb[:].unsqueeze(1).to_broadcast([P, 2 * H, DH]), ALU.mult).then_inc(a_rope_mul, 1)
                    qk2 = ps[:, BANK_A].rearrange("p (h i e) -> p h i e", i=DH // 2, e=2)
                    t2 = a_t2.rearrange("p (h i e) -> p h i e", i=DH // 2, e=2)
                    for e in range(2):
                        V.tensor_tensor(t2[:, :, :, e], qk2[:, :, :, 1 - e],
                                        sin_sb[:, e].unsqueeze(1).to_broadcast([P, 2 * H, DH // 2]), ALU.mult).then_inc(a_rope_mul, 1)
                    dve.wait_ge(a_rope_mul, 3 * t + 3)
                    V.tensor_tensor(a_t1, a_t1, a_t2, ALU.add).then_inc(a_rope, 1)
                elif k in (3, 4):
                    g = k - 3
                    dve.wait_ge(a_s_done, 2 * t + g + 1)
                    V.tensor_tensor(a_s[:, HG * g:HG * g + HG], ps[:, BANK_A].rearrange("p (h s) -> p h s", h=HG),
                                    causal_sb[:].unsqueeze(1).to_broadcast([P, HG, SP]), ALU.add).then_inc(a_masked, 1)
                    if g == 1:
                        dve.wait_ge(a_masked, 2 * t + 2)
                        V.tensor_reduce(a_mx[:], a_s, AX.X, ALU.max).then_inc(a_max_done, 1)
                        dve.wait_ge(a_max_done, t + 1)
                        V.tensor_tensor(a_s, a_s, a_mx[:].unsqueeze(2).to_broadcast([P, H, SP]), ALU.subtract).then_inc(a_sub_done, 1)
                elif k == 5:
                    dve.wait_ge(a_exp_done, t + 1)
                    V.tensor_reduce(a_sum[:], a_p.rearrange("p (h s) -> p h s", h=H), AX.X, ALU.add).then_inc(a_sum_done, 1)
                    dve.wait_ge(a_sum_done, t + 1)
                    V.reciprocal(a_rs[:], a_sum[:]).then_inc(a_rs_done, 1)
                elif k == 7:
                    dve.wait_ge(a_rs_done, t + 1)
                    dve.wait_ge(a_pv_done, t + 1)
                    for j in range(2):
                        rows = slice(SP * j, SP * j + SP)
                        src = ps[rows, BANK_A].rearrange("p (r j x) -> p r j x", r=PAIRS, j=2)[:, :, j]
                        V.tensor_tensor(a_o[rows].rearrange("p (r h d) -> p r h d", r=PAIRS, h=2),
                                        src.rearrange("p r (h d) -> p r h d", h=2),
                                        a_rs[rows].rearrange("p (r h) -> p r h", h=2).unsqueeze(3).to_broadcast([SP, PAIRS, 2, DH]),
                                        ALU.mult).then_inc(a_o_done, 1)
                elif k == 9:
                    dve.wait_ge(a_out_done, t + 1)
                    V.tensor_tensor(a_y, ps[:, BANK_A, 0:D], a_x[:], ALU.add).then_inc(a_y_done, 1)
                    dve.wait_ge(a_y_done, t + 1)
                    V.bn_stats(a_st[:], a_y).then_inc(a_ln, 1)
                    dve.wait_ge(a_ln, 3 * t + 1)
                    V.memset(a_pace[:], 0.0)
                    V.bn_aggr(a_mv[:], a_st[:]).then_inc(a_ln, 1)
                    dve.wait_ge(a_ln, 3 * t + 2)
                    V.tensor_scalar(a_ve[:], a_mv[:, 1:2], EPS, None, ALU.add).then_inc(a_ln, 1)
                    if not (isinstance(t, int) and t == 0):
                        dve.wait_ge(a_x1_kept, t)
                    dve.wait_ge(a_rstd_done, t + 1)
                    V.tensor_scalar(a_x1, a_y, a_mv[:, 0:1], a_rstd[:], ALU.subtract, ALU.mult).then_inc(a_x1_done, 1)
                    dve.wait_ge(a_x1_done, t + 1)
                    V.tensor_reduce(a_am[:], a_x1, AX.X, ALU.max, apply_absolute_value=True).then_inc(a_quant, 1)
                    dve.wait_ge(a_quant, 5 * t + 1)
                    V.tensor_scalar(a_sx[:], a_am[:], 1.0 / 127.0, 1e-8, ALU.mult, ALU.max).then_inc(a_quant, 1)
                    dve.wait_ge(a_quant, 5 * t + 2)
                    V.reciprocal(a_rsx[:], a_sx[:]).then_inc(a_quant, 1)
                    dve.wait_ge(a_quant, 5 * t + 3)
                    V.tensor_scalar(a_q1, a_x1, a_rsx[:], ROUND, ALU.mult, ALU.add).then_inc(a_quant, 1)
                    dve.wait_ge(a_quant, 5 * t + 4)
                    V.tensor_scalar(a_q1, a_q1, ROUND - 127.0, ROUND + 127.0, ALU.max, ALU.min).then_inc(a_quant, 1)
                    dve.wait_ge(a_quant, 5 * t + 5)
                    V.tensor_scalar(a_xq[:], a_q1, ROUND, None, ALU.subtract).then_inc(a_xq_done, 1)
                elif k == 11:
                    dve.wait_ge(a_qp_done, t + 1)
                    V.scalar_tensor_tensor(a_q1, ps[:, BANK_A, 0:D], a_sx[:], swq_b[:], ALU.mult, ALU.mult).then_inc(a_q1_done, 1)
                    dve.wait_ge(a_q1_done, t + 1)
                    V.tensor_tensor(a_q1, a_q1, bq_b[:], ALU.add).then_inc(a_q_done, 1)
                elif k == 12:
                    dve.wait_ge(a_qhi_done, t + 1)
                    V.tensor_tensor(qT_lo[:], ps[:, BANK_A, 0:D].rearrange("p (c n) -> p c n", c=CH),
                                    qT_hi[:].bitcast(F32), ALU.subtract).then_inc(a_qlo_done, 1)

            def unit_steps(b, j, us, ctx_on):
                for u in us:
                    unit_step(b, j, u)
                    if u % 4 == 3:
                        c = u // 4
                        if c == 0:
                            ctx_hi_step(b, j, 2)
                        elif ctx_on:
                            ctx_hi_step(b + 1, 1 - j, c - 1)

            def batch(b, j, t, t_next, units_on):
                ctx_on = t_next is not None
                for slot in range(PAIRS + 1):
                    us = list(unit_range(slot)) if units_on else []
                    if slot < PAIRS:
                        max_step(b, slot)
                    if slot:
                        pT_step(b, slot - 1, (0, 1))
                    unit_steps(b + 1, 1 - j, us[:1], ctx_on)
                    if slot:
                        pT_step(b, slot - 1, (2,))
                    if t_next is not None and slot < PAIRS:
                        a_step(A_AT.get(PAIRS * j + slot, -1), t_next)
                    unit_steps(b + 1, 1 - j, us[1:], ctx_on)
                o_step(b, j, t)

            dve.wait_ge(set_act, 4)
            dve.wait_ge(set_pool, 4)
            ctx_hi_step(0, 0, 0, True)
            ctx_hi_step(0, 0, 1, True)
            unit_steps(0, 0, range(UNITS), True)
            for k in range(13):
                a_step(k, 0)
            with dve.Fori(0, TILES - 1) as it:
                batch(2 * it, 0, it, it + 1, True)
                batch(2 * it + 1, 1, it, it + 1, True)
            batch(B - 2, 0, TILES - 1, None, True)
            batch(B - 1, 1, TILES - 1, None, False)

            n = [0]

            def own(ins):
                ins.then_inc(p_dve, 1)
                n[0] += 1

            def settle():
                dve.wait_ge(p_dve, n[0])

            dve.wait_ge(o_done, 1 + 2 * B)
            quantise(o_all[:], sm[:, 0], sm[:, 1], sm[:, 9], o_all[:], f_oq, p_dve, 0, TILES)
            n[0] = 6
            for t in range(TILES):
                dve.wait_ge(p_pe, TILES + t + 1)
                own(V.scalar_tensor_tensor(o_all[:, t], ps[:, 4 + t % 4, 0:D], sm[:, 1, t:t + 1], swp_b[:], ALU.mult, ALU.mult))
                settle()
                own(V.tensor_tensor(o_all[:, t], o_all[:, t], bp_b[:], ALU.add))
                settle()
                own(V.tensor_tensor(o_all[:, t], o_all[:, t], x1_all[:, t], ALU.add))
                settle()
                own(V.bn_stats(st8[:, t], o_all[:, t]))
            settle()
            for t in range(TILES):
                V.bn_aggr(mv8[:, t], st8[:, t]).then_inc(rsum_done, 1)
            dve.wait_ge(rsum_done, B + TILES)
            V.tensor_scalar(sm[:, 2], mv8[:, :, 1], EPS, None, ALU.add).then_inc(p_dve, 1)
            n[0] += 1
            assert n[0] == P_VE + 1
            dve.wait_ge(p_pool, 1)
            for t in range(TILES):
                own(V.tensor_scalar(acc[:, t], o_all[:, t], mv8[:, t, 0:1], sm[:, 3, t:t + 1], ALU.subtract, ALU.mult))
            dve.wait_ge(p_pe, 4 * TILES)
            own(V.tensor_tensor(sm8[:, 0], ps[:, 4, 0:TILES * E].rearrange("p (t e) -> p t e", e=E),
                                gb_b[:].unsqueeze(1).to_broadcast([P, TILES, E]), ALU.add))
            settle()
            for t in range(TILES):
                own(V.max(sm8[:, 1, t], sm8[:, 0, t]))
            settle()
            for t in range(TILES):
                own(V.max_index(idx8[:, t], sm8[:, 1, t], sm8[:, 0, t]))
            own(V.tensor_tensor(sm[:, 7], sm8[:, 1, :, 1], sm8[:, 1, :, 0], ALU.subtract))
            gap_at = n[0]
            settle()
            own(V.tensor_copy(sm8[:, 2], idx8[:]))
            dve.wait_ge(p_act, 2 * TILES + 1)
            own(V.tensor_scalar(sm[:, 10], sm[:, 8], 1.0, None, ALU.add))
            settle()
            own(V.reciprocal(sm[:, 11], sm[:, 10]))
            settle()
            own(V.tensor_tensor(sm[:, 12], sm[:, 8], sm[:, 11], ALU.mult))
            for i in range(2):
                own(V.tensor_tensor(sm8[:, 3 + i], iota8[:].unsqueeze(1).to_broadcast([P, TILES, E]),
                                    sm8[:, 2, :, i:i + 1].to_broadcast([P, TILES, E]), ALU.is_equal))
            settle()
            for i in range(2):
                own(V.tensor_tensor(sm8[:, 5 + i], sm8[:, 3 + i], sm[:, 11 + i].unsqueeze(2).to_broadcast([P, TILES, E]), ALU.mult))
            settle()
            own(V.tensor_tensor(comb[:], sm8[:, 5], sm8[:, 6], ALU.add))
            comb_at = n[0]
            own(V.memset(hT, 0.0))
            for t in range(TILES):
                dve.wait_ge(p_pe, 5 * TILES + t + 1)
                own(V.tensor_tensor(acc[:, t], ps[:, 4 + t % 4, 0:D], acc[:, t], ALU.add))
            settle()
            assert (gap_at, comb_at, n[0]) == (P_GAP, P_COMB, P_ALL), (gap_at, comb_at, n[0])

            def expert(e, slot):
                V.tensor_copy(comb_e[:, slot], comb[:, :, bass.ds(e, 1)].rearrange("p t a -> p (t a)")).then_inc(comb_done, 1)
                dve.wait_ge(comb_done, e + 1)
                for t in range(TILES):
                    dve.wait_ge(y_done, TILES * e + t + 1)
                    if not (isinstance(e, int) and e == 0):
                        dve.wait_ge(acc_done, TILES * (e - 1) + t + 1)
                    V.scalar_tensor_tensor(acc[:, t], ps[:, 4 + t % 2, 0:D], comb_e[:, slot, t:t + 1], acc[:, t],
                                           ALU.mult, ALU.add).then_inc(acc_done, 1)

            expert(0, 0)
            expert(1, 1)
            with dve.Fori(1, E // 2) as ei:
                expert(2 * ei, 0)
                expert(2 * ei + 1, 1)
            dve.wait_ge(acc_done, TILES * E)
            for t in range(TILES):
                V.bn_stats(st8[:, t], acc[:, t]).then_inc(f_dve, 1)
            dve.wait_ge(f_dve, TILES)
            for t in range(TILES):
                V.bn_aggr(mv8[:, t], st8[:, t]).then_inc(f_dve, 1)
            dve.wait_ge(f_dve, 2 * TILES)
            V.tensor_scalar(sm[:, 4], mv8[:, :, 1], EPS, None, ALU.add).then_inc(f_dve, 1)

        @block.tensor
        def _(pe):
            mm = nc.tensor.matmul

            def transpose(dst, src, n):
                return nc.tensor.transpose(dst, src, (id16 if src.dtype == BF16 else id32)[0:n, 0:n])

            pe.wait_ge(small_in, SMALL_IN)
            pe.wait_ge(set_pool, 4)
            for n in range(2):
                pe.wait_ge(set_dve, 8 * n + 6)
                for g in range(CH):
                    for c in range(CH):
                        last = transpose(ps[:, BANK_T + n].bitcast(BF16)[:, c * D + g * P:c * D + g * P + P],
                                         w_int[n][:, g, c * P:c * P + P], P)
                last.then_inc(set_pe, 1)
                pe.wait_ge(set_dve, 8 * n + 8)
                mm(ps[:, BANK_KV + n, 0:D], ones[:], w_diag[n].rearrange("p c n -> p (c n)"), start=True, stop=True).then_inc(set_pe, 1)
            pe.wait_ge(set_dve, 18)
            pe.wait_ge(set_act, 4)

            SPLIT = ((0, 0), (0, 1), (1, 0))

            def unit(b, j, u, first=False):
                c, g = u // 4, u % 4
                place = (CHUNKS * j + c) % 2
                cs, ws = (ctx_hi, ctx_lo), (wkv_hi, wkv_lo)
                pe.wait_ge(ctx_lo_done, CHUNKS * b + c + 1)
                if not first:
                    pe.wait_ge(unit_out, UNITS * b + u)
                if g < 2:
                    for i, (x, w) in enumerate(SPLIT):
                        for k in range(CH):
                            last = mm(ps[:, BANK_KV, 0:MC], ws[w][:, k, P * g:P * g + P], cs[x][:, place, k, :],
                                      start=(i == 0 and k == 0), stop=(i == 2 and k == CH - 1))
                else:
                    for m in range(2):
                        a = MT * (2 * (g - 2) + m)
                        for i, (x, w) in enumerate(SPLIT):
                            for k in range(CH):
                                last = mm(ps[0:MT, BANK_KV, D * m:D * m + D], cs[x][:, place, k, a:a + MT], ws[w][:, k, D:2 * D],
                                          start=(i == 0 and k == 0), stop=(i == 2 and k == CH - 1))
                last.then_inc(unit_done, 1)

            def scores(b, j, p):
                g, r = p // (PAIRS // CH), p % (PAIRS // CH)
                if p > 0:
                    pe.wait_ge(exp_done, PAIRS * b + p)
                ks, qs = (k_hi, k_lo), (qbd_hi, qbd_lo)
                for i, (kk, qq) in enumerate(SPLIT):
                    q = qs[qq][:, j, g, 2 * r:2 * r + 2, :].rearrange("p h s -> p (h s)")
                    for c in range(CHUNKS):
                        last = mm(ps[:, BANK_S + c, 0:MC], q, ks[kk][:, j, g, MC * c:MC * c + MC], start=(i == 0), stop=(i == 2))
                last.then_inc(s_done, 1)

            def tr(b, p, q):
                n = 3 * p + q
                pe.wait_ge(exp_done, PAIRS * b + p + 1)
                if n > 1:
                    pe.wait_ge((pT_even, pT_odd)[n % 2], 12 * b + n // 2)
                for i in range(TPC):
                    a = MC * q + MT * i
                    last = transpose(ps[0:MT, BANK_T + n % 2, P * i:P * i + P], pr[:, p % 2, a:a + MT], P)
                last.then_inc(tr_done, 1)

            def pv(b, j, p, q):
                n = 3 * p + q
                if q == 0 and p == 0:
                    pe.wait_ge(o_done, 2 * b + 1)
                if q == 0 and p == PAIRS // 2:
                    pe.wait_ge(oT_done, 2 * b + 1)
                pe.wait_ge((pT_even, pT_odd)[n % 2], 12 * b + n // 2 + 1)
                for i in range(TPC):
                    last = mm(ps[32 * i:32 * i + 32, BANK_O, P * (p % 4):P * (p % 4) + P],
                              v_sb[0:MT, j, TPC * q + i, 32 * p:32 * p + 32], pT[0:MT, n % 2, i],
                              start=(q == 0), stop=(q == 2))
                if q == 2:
                    last.then_inc(pv_done, 1)

            def o_back(b):
                pe.wait_ge(oT_done, 2 * b + 2)
                for p in range(PAIRS):
                    last = mm(ps[:, BANK_O, 32 * p:32 * p + 32], oT_sb[:, p], sel_sb[:], start=True, stop=True)
                last.then_inc(o_back_done, 1)

            def a_step(k, t, first=False):
                A = ps[:, BANK_A]
                if k == 0:
                    pe.wait_ge(x_in, 32 * (t + 1))
                    if not first:
                        pe.wait_ge(a_qlo_done, t)
                    for c in range(CH):
                        last = mm(A, a_xT[:, c], wqkv_sb[:, c, 0:2 * D], start=(c == 0), stop=(c == CH - 1))
                    last.then_inc(a_qk_done, 1)
                elif k == 1:
                    pe.wait_ge(a_rope_mul, 3 * t + 3)
                    for c in range(CH):
                        last = mm(A[:, 0:D], a_xT[:, c], wqkv_sb[:, c, 2 * D:3 * D], start=(c == 0), stop=(c == CH - 1))
                    last.then_inc(a_v_done, 1)
                elif k == 2:
                    pe.wait_ge(a_rope, t + 1)
                    pe.wait_ge(a_vb_done, 4 * t + 4)
                    for c in range(4):
                        last = transpose(A[:, P * c:P * c + P], a_t1[:, P * c:P * c + P], P)
                    last.then_inc(a_tqk_done, 1)
                elif k in (3, 4):
                    g = k - 3
                    pe.wait_ge(a_kbd_done, 4 * t + 4)
                    if g == 1:
                        pe.wait_ge(a_masked, 2 * t + 1)
                    for j in range(2):
                        last = mm(ps[SP * j:SP * j + SP, BANK_A], a_qkT[:, g, SP * j:SP * j + SP],
                                  a_kbd[:, j, g].rearrange("p h s -> p (h s)"), start=True, stop=True)
                    last.then_inc(a_s_done, 1)
                elif k in (5, 6):
                    pe.wait_ge(a_exp_done, t + 1)
                    if k == 6:
                        pe.wait_ge(a_pT_done, 2 * t + 1)
                    for r in range(4):
                        a = P * (4 * (k - 5) + r)
                        last = transpose(A[:, P * r:P * r + P], a_p[:, a:a + P], P)
                    last.then_inc(a_tp_done, 1)
                elif k == 7:
                    pe.wait_ge(a_pT_done, 2 * t + 2)
                    for r in range(PAIRS):
                        last = mm(A[:, 64 * r:64 * r + 64], a_pT[:, r], a_vb[:, r].rearrange("p j d -> p (j d)"), start=True, stop=True)
                    last.then_inc(a_pv_done, 1)
                elif k == 8:
                    pe.wait_ge(a_o_done, 2 * t + 2)
                    for c in range(CH):
                        last = transpose(A[:, P * c:P * c + P], a_o[:, P * c:P * c + P], P)
                    last.then_inc(a_to_done, 1)
                elif k == 9:
                    pe.wait_ge(a_oT_done, t + 1)
                    for c in range(CH):
                        last = mm(A[:, 0:D], a_oT[:, c], wout_sb[:, c], start=(c == 0), stop=(c == CH - 1))
                    last.then_inc(a_out_done, 1)
                elif k == 10:
                    pe.wait_ge(a_xq_done, t + 1)
                    for c in range(CH):
                        last = transpose(A.bitcast(BF16)[:, P * c:P * c + P], a_xq[:, P * c:P * c + P], P)
                    last.then_inc(a_txq_done, 1)
                elif k == 11:
                    pe.wait_ge(a_xqT_done, t + 1)
                    for c in range(CH):
                        last = mm(A[:, 0:D], a_xqT[:, c], wqqT[:, c], start=(c == 0), stop=(c == CH - 1))
                    last.then_inc(a_qp_done, 1)
                elif k == 12:
                    pe.wait_ge(a_q_done, t + 1)
                    for c in range(CH):
                        last = transpose(A[:, P * c:P * c + P], a_q1[:, P * c:P * c + P], P)
                    last.then_inc(a_tq_done, 1)

            def batch(b, j, t_next, units_on):
                pe.wait_ge(unit_out, UNITS * (b + 1))
                pe.wait_ge(qbd_done, 4 * (b + 1))
                for slot in range(PAIRS + 1):
                    if slot < PAIRS:
                        scores(b, j, slot)
                    us = list(unit_range(slot)) if units_on else []
                    if slot:
                        tr(b, slot - 1, 0)
                        tr(b, slot - 1, 1)
                    for u in us[:1]:
                        unit(b + 1, 1 - j, u)
                    if slot:
                        pv(b, j, slot - 1, 0)
                        tr(b, slot - 1, 2)
                        pv(b, j, slot - 1, 1)
                    if t_next is not None and slot < PAIRS:
                        a_step(A_AT.get(PAIRS * j + slot, -1), t_next)
                    if slot:
                        pv(b, j, slot - 1, 2)
                    for u in us[1:]:
                        unit(b + 1, 1 - j, u)
                o_back(b)

            for u in range(UNITS):
                unit(0, 0, u, u == 0)
            for k in range(13):
                a_step(k, 0, True)
            with pe.Fori(0, TILES - 1) as it:
                batch(2 * it, 0, it + 1, True)
                batch(2 * it + 1, 1, it + 1, True)
            batch(B - 2, 0, None, True)
            batch(B - 1, 1, None, False)

            pe.wait_ge(p_dve, 6)
            for t in range(TILES):
                if t >= 4:
                    pe.wait_ge(p_act, t - 3)
                for c in range(CH):
                    last = transpose(ps[:, t % 4].bitcast(BF16)[:, P * c:P * c + P], f_oq[:, t, P * c:P * c + P], P)
                last.then_inc(p_pe, 1)
            for t in range(TILES):
                pe.wait_ge(p_act, t + 1)
                if t >= 4:
                    pe.wait_ge(p_dve, 6 + 4 * (t - 3))
                for c in range(CH):
                    last = mm(ps[:, 4 + t % 4, 0:D], f_oqT[:, t, c], wpqT[:, c], start=(c == 0), stop=(c == CH - 1))
                last.then_inc(p_pe, 1)
            for t in range(TILES):
                pe.wait_ge(p_dve, P_VE + 1 + t + 1)
                pe.wait_ge(p_act, TILES + max(0, t - 3))
                for c in range(CH):
                    last = transpose(ps[:, t % 4, P * c:P * c + P], acc[:, t, P * c:P * c + P], P)
                last.then_inc(p_pe, 1)
            for t in range(TILES):
                pe.wait_ge(p_act, TILES + t + 1)
                for c in range(CH):
                    last = mm(ps[:, 4, E * t:E * t + E], x2T[:, c, t], gw_sb[:, c], start=(c == 0), stop=(c == CH - 1))
                last.then_inc(p_pe, 1)
            for t in range(TILES):
                pe.wait_ge(p_dve, P_COMB)
                pe.wait_ge(p_act, 2 * TILES + 1 + max(0, t - 3))
                transpose(ps[0:E, t % 4, 0:P], comb[:, t], P).then_inc(p_pe, 1)
            for t in range(TILES):
                pe.wait_ge(p_act, 2 * TILES + 1 + t + 1)
                if t >= 4:
                    pe.wait_ge(p_dve, P_COMB + 1 + t - 3)
                mm(ps[:, 4 + t % 4, 0:D], combT[:, t], b2_sb[:], start=True, stop=True).then_inc(p_pe, 1)
            pe.wait_ge(p_dve, P_ALL)

            def expert(e, slot):
                first = isinstance(e, int) and e == 0
                pe.wait_ge(ffn_in[slot], 24 * (e - slot) + 48)
                for u in range(2):
                    for f in range(FT):
                        if not (first and u == 0 and f < 2):
                            pe.wait_ge(gelu_done, 2 * FT * e + FT * u + f - 1)
                        for c in range(CH):
                            last = mm(ps[:, f % 2, 0:8 * S], w1_sb[:, slot, c, P * f:P * f + P],
                                      x2T[:, c, 4 * u:4 * u + 4].rearrange("p t (j s) -> p (t j) s", j=2)[:, :, 0:S],
                                      start=(c == 0), stop=(c == CH - 1))
                        last.then_inc(h_done, 1)
                for u in range(2):
                    for tt in range(4):
                        t = 4 * u + tt
                        if tt == 0:
                            pe.wait_ge(gelu_done, 2 * FT * e + FT * (u + 1))
                        if not (first and t < 2):
                            pe.wait_ge(acc_done, TILES * e + t - 1)
                        for f in range(FT):
                            last = mm(ps[:, 4 + t % 2, 0:D], hT[:, u, f, P * tt:P * tt + P], w2_sb[:, slot, f],
                                      start=(f == 0), stop=(f == FT - 1))
                        last.then_inc(y_done, 1)

            expert(0, 0)
            expert(1, 1)
            with pe.Fori(1, E // 2) as ei:
                expert(2 * ei, 0)
                expert(2 * ei + 1, 1)


def tables():
    pos = (np.arange(P) % SP).astype(np.float32)
    inv = (1.0 / 10000.0 ** (np.arange(0, DH, 2, dtype=np.float32) / DH)).astype(np.float32)
    freqs = np.outer(pos, inv).astype(np.float32)
    emb = np.concatenate([freqs, freqs], axis=-1)
    cos, sin = np.cos(emb).astype(np.float32), np.sin(emb).astype(np.float32)
    sin_pair = np.stack([-sin[:, 0::2], sin[:, 1::2]], axis=1)
    head = (np.arange(P)[:, None] // DH == np.arange(HG)[None, :]).astype(np.float32) * np.float32(DH ** -0.5)
    causal = np.where(np.arange(SP)[None, :] <= (np.arange(P) % SP)[:, None], 0.0, MASKED).astype(np.float32)
    return {"rope_cos": cos, "rope_sin": np.ascontiguousarray(sin_pair), "head_mask": head, "causal": causal,
            "ident": np.eye(P, dtype=np.float32), "sel": np.tile(np.eye(32, dtype=np.float32), (P // 32, 1)),
            "iota_row": np.ascontiguousarray(np.broadcast_to(np.arange(E, dtype=np.float32), (P, E)))}


def kernel(x, ctx_2048, L0_attn_w_qkv, L0_attn_w_out, L0_attn_w_c1, L0_attn_w_c2, L0_xattn_wq, L0_xattn_bq,
           L0_xattn_wkv, L0_xattn_bkv, L0_xattn_wp, L0_xattn_bp, L0_ffn_gate_w, L0_ffn_gate_b, L0_ffn_w1, L0_ffn_b1,
           L0_ffn_w2, L0_ffn_b2):
    import concourse.bacc as bacc
    from concourse.bass_utils import run_bass_kernel_spmd

    def halves(a):
        return a.reshape(-1, P, a.shape[-1]).transpose(1, 0, 2)

    def rows(v):
        return np.broadcast_to(v.reshape(1, -1), (P, v.size))

    xp = np.zeros((B, SP, D), np.asarray(x).dtype)
    xp[:, :S] = np.asarray(x)
    xp = xp.reshape(TILES, P, D)
    ct = np.asarray(ctx_2048).reshape(B, CHUNKS, MC, CH, P).transpose(0, 1, 4, 3, 2)
    wkv, bkv = np.asarray(L0_xattn_wkv), np.asarray(L0_xattn_bkv)
    arrays = {
        "x_tok": xp, "x_T": xp.reshape(TILES, P, CH, P).transpose(0, 3, 2, 1), "ctx_T": ct,
        "w_qkv_T": halves(np.asarray(L0_attn_w_qkv).T), "w_out_T": halves(np.asarray(L0_attn_w_out).T),
        "wq": halves(np.asarray(L0_xattn_wq)), "bq_row": rows(np.asarray(L0_xattn_bq)),
        "w_kv_T": halves(wkv.T), "bk_col": bkv[:D].reshape(CH, P).T, "bv_row": rows(bkv[D:]),
        "wp": halves(np.asarray(L0_xattn_wp)), "bp_row": rows(np.asarray(L0_xattn_bp)),
        "gate_w": halves(np.asarray(L0_ffn_gate_w)), "gate_b_row": rows(np.asarray(L0_ffn_gate_b)),
        "w1": np.asarray(L0_ffn_w1).reshape(E, CH, P, F).transpose(0, 2, 1, 3),
        "b1_col": np.asarray(L0_ffn_b1).reshape(E, FT, P).transpose(0, 2, 1),
        "w2": np.asarray(L0_ffn_w2).reshape(E, FT, P, D).transpose(0, 2, 1, 3), "b2": np.asarray(L0_ffn_b2),
    }
    arrays.update(tables())
    arrays = {k: np.ascontiguousarray(v) for k, v in arrays.items()}
    nc = bacc.Bacc("TRN2", target_bir_lowering=False, num_devices=1)
    args = {k: nc.dram_tensor(k, v.shape, mybir.dt.from_np(v.dtype), kind="ExternalInput").ap() for k, v in arrays.items()}
    out = nc.dram_tensor("out", (B, S, D), F32, kind="ExternalOutput").ap()
    decoder_layer(nc, **args, out=out)
    r = run_bass_kernel_spmd(nc, [arrays], core_ids=[0])
    return r.results[0]["out"]
```

```python
from contextlib import ExitStack

import numpy as np
import concourse.bass as bass
from concourse import mybir

ALU = mybir.AluOpType
ACT = mybir.ActivationFunctionType
AX = mybir.AxisListType
F32 = mybir.dt.float32
F32R = mybir.dt.float32r
BF16 = mybir.dt.bfloat16
U32 = mybir.dt.uint32
I32 = mybir.dt.int32

B, S, D = 16, 56, 256
M = 1500
H, DH = 16, 16
E, F = 8, 1024
P = 128
CH = D // P
SP = 64
TILES = B * SP // P
HG = P // DH
PAIRS = H // 2
CHUNKS, MC = 3, 500
MT = 125
TPC = MC // MT
UNITS = 4 * CHUNKS
FT = F // P
A_STEPS = 14
GT = 2 * B * S // P + E - 1
DUMP = GT * P
EPS = 1e-5
ROUND = 12582912.0
MASKED = -1e30

BANK_S = 0
BANK_T = 3
BANK_O = 5
BANK_KV = 6
XG_BANK, Y_BANK = 0, 1
H_BANK, TH_BANK = 2, 4
BANK_A = 7


def decoder_layer(nc, x_tok, x_T, ctx_T, w_qkv_T, w_out_T, wq, bq_row, w_kv_T, bk_col, bv_row, wp, bp_row,
                  gate_w, gate_b_row, w1, b1, w2, b2, rope_cos, rope_sin, head_mask, causal, ident, iota_row, sel,
                  before, valid, dump, iota_tiles, out):
    with ExitStack() as ctx:
        def sb(name, shape, dt=F32):
            return ctx.enter_context(nc.sbuf_tensor(name, shape, dt))[:]

        def sem(name):
            return ctx.enter_context(nc.semaphore(name))

        ps = ctx.enter_context(nc.psum_tensor("ps", [P, 8, 512], F32))

        id32 = sb("id32", [P, P])
        id16 = sb("id16", [P, P], BF16)
        ones = sb("ones", [P, P])
        iota8 = sb("iota8", [P, E])
        swp_b = sb("swp_b", [P, D])
        wpqT = sb("wpqT", [P, CH, D], BF16)
        bp_b = sb("bp_b", [P, D])
        gw_sb = sb("gw_sb", [P, CH, E])
        gb_b = sb("gb_b", [P, E])
        before16 = sb("before16", [P, P], BF16)
        ones16 = sb("ones16", [P, P], BF16)
        valid_sb = sb("valid_sb", [P, 1])
        dump_sb = sb("dump_sb", [P, TILES, 2])
        iota_t = sb("iota_t", [P, GT])
        neg_half = sb("neg_half", [P, TILES])
        x1_all = sb("x1_all", [P, TILES, D])
        o_all = sb("o_all", [P, TILES, D])
        acc = x1_all
        comb = sb("comb", [P, 2, TILES])
        slot_gather = sb("slot_gather", [P, TILES, 2], U32)
        slot_scatter = sb("slot_scatter", [P, TILES, 2], U32)
        e_tab = sb("e_tab", [P, GT], I32)
        sm = sb("sm", [P, 16, TILES])
        zeros = sb("zeros", [P, D])

        whole = sb
        attention = ExitStack()

        def sb(name, shape, dt=F32):
            return attention.enter_context(nc.sbuf_tensor(name, shape, dt))[:]

        cos_sb = sb("cos_sb", [P, DH])
        sin_sb = sb("sin_sb", [P, 2, DH // 2])
        hmask = sb("hmask", [P, HG])
        causal_sb = sb("causal_sb", [P, SP])
        sel_sb = sb("sel_sb", [P, 32])
        wqkv_sb = sb("wqkv_sb", [P, CH, 3 * D])
        wout_sb = sb("wout_sb", [P, CH, D])
        wkv_hi = sb("wkv_hi", [P, CH, 2 * D], F32R)
        wkv_lo = sb("wkv_lo", [P, CH, 2 * D], F32R)
        wqqT = sb("wqqT", [P, CH, D], BF16)
        swq_b = sb("swq_b", [P, D])
        bq_b = sb("bq_b", [P, D])
        bv_b = sb("bv_b", [P, D])
        bk_sb = sb("bk_sb", [P, CH])
        ctx_raw = sb("ctx_raw", [P, 2, CH, MC])
        v_sb = sb("v_sb", [P, 2, M // MT, D])
        pr = sb("pr", [P, 2, M])
        oT_sb = sb("oT_sb", [P, PAIRS, P])
        pT = sb("pT", [P, 2, TPC, P])
        a_t1 = sb("a_t1", [P, 2 * D])
        a_t2 = sb("a_t2", [P, 2 * D])
        a_qkT = sb("a_qkT", [P, 4, P])
        a_kbd = sb("a_kbd", [P, 2, CH, HG, SP])
        a_s = sb("a_s", [P, H, SP])
        a_p = a_s[:].rearrange("p h s -> p (h s)")
        a_vb = sb("a_vb", [P, PAIRS, 2, 32])
        a_o = sb("a_o", [P, D])
        a_oT = sb("a_oT", [P, CH, P])
        a_y = sb("a_y", [P, D])
        a_x1 = sb("a_x1", [P, D])
        a_q1 = sb("a_q1", [P, D])
        a_pT = a_kbd[:, 0].rearrange("p c h s -> p (c h s)").rearrange("p (r n) -> p r n", r=PAIRS)
        ctx_hi = sb("ctx_hi", [P, 2, CH, MC], F32R)
        ctx_lo = sb("ctx_lo", [P, 2, CH, MC], F32R)
        k_hi = sb("k_hi", [P, 2, CH, M], F32R)
        k_lo = sb("k_lo", [P, 2, CH, M], F32R)
        qT_hi = sb("qT_hi", [P, CH, P], F32R)
        qT_lo = sb("qT_lo", [P, CH, P], F32R)
        qbd_hi = sb("qbd_hi", [P, 2, CH, HG, SP], F32R)
        qbd_lo = sb("qbd_lo", [P, 2, CH, HG, SP], F32R)
        a_x = sb("a_x", [P, D])
        a_xT = sb("a_xT", [P, CH, P])
        a_xq = sb("a_xq", [P, D], BF16)
        a_xqT = sb("a_xqT", [P, CH, P], BF16)
        a_mx = sb("a_mx", [P, H])
        a_rs = sb("a_rs", [P, H])
        a_sum = sb("a_sum", [P, H])
        a_st = sb("a_st", [P, 6])
        a_mv = sb("a_mv", [P, 2])
        a_ve = sb("a_ve", [P, 1])
        a_pace = sb("a_pace", [P, 1])
        a_rstd = sb("a_rstd", [P, 1])
        a_am = sb("a_am", [P, 1])
        a_sx = sb("a_sx", [P, 1])
        a_rsx = sb("a_rsx", [P, 1])
        negmax = sb("negmax", [P, 2])
        sumexp = sb("sumexp", [P, 2, PAIRS])
        rsum = sb("rsum", [P, 2, PAIRS])
        wkv_raw = pr[:].rearrange("p a b -> p (a b)")[:, 0:CH * 2 * D].rearrange("p (c n) -> p c n", c=CH)
        spare = v_sb[:, 1].rearrange("p b c -> p (b c)")
        w_nat = [spare[:, 512 * n:512 * n + 512].rearrange("p (c n) -> p c n", c=CH) for n in (0, 1)]
        w_t = [spare[:, 512 * n:512 * n + 512].rearrange("p (c n) -> p c n", c=CH) for n in (2, 3)]
        w_int = [spare[:, 256 * n:256 * n + 256].bitcast(BF16).rearrange("p (c n) -> p c n", c=CH) for n in (8, 9)]
        w_diag = [spare[:, 256 * n:256 * n + 256].rearrange("p (c n) -> p c n", c=CH) for n in (10, 11)]
        before32 = pr[:].rearrange("p a b -> p (a b)")[:, CH * 2 * D:CH * 2 * D + P]
        w_am = sm[:, 0:CH, 0:2]
        w_s = sm[:, CH:2 * CH, 0:2]
        w_rs = sm[:, 2 * CH:3 * CH, 0:2]

        attention.close()
        sb = whole
        w1_sb = sb("w1_sb", [P, E, CH, F])
        w2_sb = sb("w2_sb", [P, E, FT, D])
        f_oq = sb("f_oq", [P, TILES, D], BF16)
        f_oqT = sb("f_oqT", [P, TILES, CH, P], BF16)
        x2T = sb("x2T", [P, CH, TILES, P])
        sm8 = sb("sm8", [P, 16, TILES, E])
        e_cmp = sb("e_cmp", [P, GT, E])
        e_sum = sb("e_sum", [P, GT])
        oh16 = sb("oh16", [P, TILES, E], BF16)
        idx8 = sb("idx8", [P, TILES, E], U32)
        st8 = sb("st8", [P, TILES, 6])
        mv8 = sb("mv8", [P, TILES, 2])
        xg = sb("xg", [P, D])
        xgT = sb("xgT", [P, CH, P])
        b1_row = sb("b1_row", [P, F])
        b2_row = sb("b2_row", [P, D])
        hb = sb("hb", [P, F])
        hg = sb("hg", [P, F])
        y_sb = sb("y_sb", [P, D])
        hT = x2T[:].rearrange("p c t n -> p (c t n)")[:, 0:F].rearrange("p (f n) -> p f n", f=FT)
        got = w1_sb[:, 0:2].rearrange("p e c f -> p (e c f)").rearrange("p (k t n) -> p k t n", k=2, t=TILES)

        kv_in = sem("kv_in")
        dec_in = sem("dec_in")
        small_in = sem("small_in")
        x_in = sem("x_in")
        ctx_in = [sem(f"ctx_in{k}") for k in range(2)]
        out_done = sem("out_done")
        set_dve = sem("set_dve")
        set_pe = sem("set_pe")
        set_act = sem("set_act")
        set_pool = sem("set_pool")
        ctx_hi_done = sem("ctx_hi_done")
        ctx_lo_done = sem("ctx_lo_done")
        unit_done = sem("unit_done")
        k_hi_done = sem("k_hi_done")
        unit_out = sem("unit_out")
        s_done = sem("s_done")
        max_done = sem("max_done")
        exp_done = sem("exp_done")
        tr_done = sem("tr_done")
        pT_outer = sem("pT_outer")
        pT_inner = sem("pT_inner")
        pv_done = sem("pv_done")
        rsum_done = sem("rsum_done")
        oT_done = sem("oT_done")
        o_back_done = sem("o_back_done")
        o_done = sem("o_done")
        qbd_done = sem("qbd_done")
        a_qk_done = sem("a_qk_done")
        a_rope_mul = sem("a_rope_mul")
        a_rope = sem("a_rope")
        a_v_done = sem("a_v_done")
        a_vb_done = sem("a_vb_done")
        a_tqk_done = sem("a_tqk_done")
        a_qkT_done = sem("a_qkT_done")
        a_kbd_done = sem("a_kbd_done")
        a_s_done = sem("a_s_done")
        a_masked = sem("a_masked")
        a_max_done = sem("a_max_done")
        a_sub_done = sem("a_sub_done")
        a_exp_done = sem("a_exp_done")
        a_sum_done = sem("a_sum_done")
        a_rs_done = sem("a_rs_done")
        a_tp_done = sem("a_tp_done")
        a_pT_done = sem("a_pT_done")
        a_pv_done = sem("a_pv_done")
        a_o_done = sem("a_o_done")
        a_to_done = sem("a_to_done")
        a_oT_done = sem("a_oT_done")
        a_out_done = sem("a_out_done")
        a_y_done = sem("a_y_done")
        a_ln = sem("a_ln")
        a_rstd_done = sem("a_rstd_done")
        a_x1_done = sem("a_x1_done")
        a_x1_kept = sem("a_x1_kept")
        a_quant = sem("a_quant")
        a_xq_done = sem("a_xq_done")
        a_txq_done = sem("a_txq_done")
        a_xqT_done = sem("a_xqT_done")
        a_qp_done = sem("a_qp_done")
        a_q1_done = sem("a_q1_done")
        a_q_done = sem("a_q_done")
        a_tq_done = sem("a_tq_done")
        a_qhi_done = sem("a_qhi_done")
        a_qlo_done = sem("a_qlo_done")
        p_dve = sem("p_dve")
        p_pe = sem("p_pe")
        p_act = sem("p_act")
        p_pool = sem("p_pool")
        w_in = sem("w_in")
        zeroed = sem("zeroed")
        scattered = sem("scattered")
        xg_in = sem("xg_in")
        b1_in = sem("b1_in")
        b2_in = sem("b2_in")
        y_out = sem("y_out")
        tx_done = sem("tx_done")
        xgT_done = sem("xgT_done")
        m1_done = sem("m1_done")
        hb_done = sem("hb_done")
        gelu_done = sem("gelu_done")
        th_done = sem("th_done")
        hT_act = sem("hT_act")
        hT_dve = sem("hT_dve")
        m2_done = sem("m2_done")
        y_ready = sem("y_ready")
        gathered = [sem(f"gathered{t}") for t in range(TILES)]
        f_dve = sem("f_dve")
        f_pool = sem("f_pool")

        xs = nc.dram_tensor("xs", (DUMP + 2 * TILES * P, D), F32).ap()
        ys = nc.dram_tensor("ys", (GT * P, D), F32).ap()
        xs_tiles = xs[0:DUMP].rearrange("(g p) n -> g p n", p=P)
        ys_tiles = ys.rearrange("(g p) n -> g p n", p=P)

        FOR_KV = [(wkv_raw, w_kv_T), (bk_sb[:], bk_col), (bv_b[:], bv_row)]
        FOR_DEC = [(wqkv_sb[:], w_qkv_T), (cos_sb[:], rope_cos), (sin_sb[:], rope_sin), (id32[:], ident),
                   (hmask[:], head_mask), (causal_sb[:], causal), (wout_sb[:], w_out_T)]
        SMALL = [(w_nat[0], wq), (w_nat[1], wp), (bq_b[:], bq_row), (bp_b[:], bp_row), (gw_sb[:], gate_w),
                 (gb_b[:], gate_b_row), (sel_sb[:], sel), (before32, before), (valid_sb[:], valid),
                 (dump_sb[:], dump), (iota_t[:], iota_tiles), (iota8[:], iota_row)]

        def unit_slots(slot):
            edges = [0, 2, 3, 5, 6, 8, 10, 11, UNITS]
            us = list(range(edges[slot - 1], edges[slot]))
            return (us[:1], us[1:]) if slot < PAIRS else ([], us)

        A_AT = {s: s - 1 for s in range(1, 1 + A_STEPS)}

        block = ctx.enter_context(nc.Block())
        at = {}

        @block.vector
        def _(dve):
            V = nc.vector

            def quantise(src, am, s, rs, t1, dst, own, n, rows):
                shape = [P, rows, D]
                V.tensor_reduce(am, src, AX.X, ALU.max, apply_absolute_value=True).then_inc(own, 1)
                dve.wait_ge(own, n + 1)
                V.tensor_scalar(s, am, 1.0 / 127.0, 1e-8, ALU.mult, ALU.max).then_inc(own, 1)
                dve.wait_ge(own, n + 2)
                V.reciprocal(rs, s).then_inc(own, 1)
                dve.wait_ge(own, n + 3)
                V.tensor_tensor(t1, src, rs.unsqueeze(2).to_broadcast(shape), ALU.mult).then_inc(own, 1)
                dve.wait_ge(own, n + 4)
                V.tensor_scalar(t1, t1, ROUND, ROUND - 127.0, ALU.add, ALU.max).then_inc(own, 1)
                dve.wait_ge(own, n + 5)
                V.tensor_scalar(dst, t1, ROUND + 127.0, ROUND, ALU.min, ALU.subtract).then_inc(own, 1)

            V.memset(a_pace[:], 0.0).then_inc(o_done, 1)
            dve.wait_ge(kv_in, 16 * len(FOR_KV))
            V.tensor_copy(wkv_hi[:], wkv_raw).then_inc(set_dve, 1)
            dve.wait_ge(set_dve, 1)
            V.tensor_tensor(wkv_lo[:], wkv_raw, wkv_hi[:].bitcast(F32), ALU.subtract).then_inc(set_dve, 1)

            def weights_to_int8(n):
                quantise(w_nat[n], w_am[:, :, n], w_s[:, :, n], w_rs[:, :, n], w_t[n], w_int[n], set_dve, 2 + 8 * n, CH)
                for c in range(CH):
                    V.tensor_scalar(w_diag[n][:, c], id32[:], w_s[:, c, n:n + 1], None, ALU.mult).then_inc(set_dve, 1)

            def ctx_hi_step(b, j, c, first=False):
                k = (CHUNKS * j + c) % 2
                dve.wait_ge(ctx_in[k], 8 * (CHUNKS * b + c - k) + 16)
                if not first:
                    dve.wait_ge(unit_done, 4 * (CHUNKS * b + c - 1))
                V.tensor_copy(ctx_hi[:, k], ctx_raw[:, k]).then_inc(ctx_hi_done, 1)

            def unit_step(b, par, u):
                c, g = u // 4, u % 4
                dve.wait_ge(unit_done, UNITS * b + u + 1)
                if g < 2:
                    dve.wait_ge(k_hi_done, 2 * (CHUNKS * b + c) + g + 1)
                    V.scalar_tensor_tensor(k_lo[:, par, g, MC * c:MC * c + MC], ps[:, BANK_KV, 0:MC], bk_sb[:, g:g + 1],
                                           k_hi[:, par, g, MC * c:MC * c + MC].bitcast(F32),
                                           ALU.add, ALU.subtract).then_inc(unit_out, 1)
                else:
                    m = TPC * c + 2 * (g - 2)
                    V.tensor_tensor(v_sb[0:MT, par, m:m + 2], ps[0:MT, BANK_KV].rearrange("p (t n) -> p t n", t=2),
                                    bv_b[0:MT].unsqueeze(1).to_broadcast([MT, 2, D]), ALU.add).then_inc(unit_out, 1)

            def max_step(b, p):
                dve.wait_ge(s_done, PAIRS * b + p + 1)
                V.tensor_reduce(negmax[:, p % 2:p % 2 + 1], ps[:, BANK_S:BANK_S + CHUNKS, 0:MC], AX.XY, ALU.max,
                                negate=True).then_inc(max_done, 1)

            def pT_step(b, p):
                n = (3 * p + 1) % 2
                dve.wait_ge(tr_done, 3 * PAIRS * b + 3 * p + 2)
                V.tensor_copy(pT[0:MT, n], ps[0:MT, BANK_T + n].rearrange("p (t n) -> p t n", t=TPC)).then_inc(pT_inner, 1)

            def o_step(b, par, t):
                dve.wait_ge(exp_done, PAIRS * (b + 1))
                V.reciprocal(rsum[:, par], sumexp[:, par]).then_inc(rsum_done, 1)
                dve.wait_ge(rsum_done, b + 1)
                dve.wait_ge(o_back_done, b + 1)
                for hp in range(2):
                    dst = o_all[SP * par:SP * par + SP, bass.ds(t, 1)].rearrange("p a (r h d) -> p (a r) h d", r=PAIRS, h=2)[:, :, hp]
                    src = ps[SP * hp:SP * hp + SP, BANK_O, 0:D].rearrange("p (r h d) -> p r h d", r=PAIRS, h=2)[:, :, hp]
                    V.tensor_tensor(dst, src, rsum[SP * hp:SP * hp + SP, par].unsqueeze(2).to_broadcast([SP, PAIRS, DH]),
                                    ALU.mult).then_inc(o_done, 1)

            def a_step(k, t):
                if k == 0:
                    dve.wait_ge(a_qk_done, t + 1)
                    qk = ps[:, BANK_A].rearrange("p (h d) -> p h d", d=DH)
                    V.tensor_tensor(a_t1.rearrange("p (h d) -> p h d", d=DH), qk,
                                    cos_sb[:].unsqueeze(1).to_broadcast([P, 2 * H, DH]), ALU.mult).then_inc(a_rope_mul, 1)
                    qk2 = ps[:, BANK_A].rearrange("p (h i e) -> p h i e", i=DH // 2, e=2)
                    t2 = a_t2.rearrange("p (h i e) -> p h i e", i=DH // 2, e=2)
                    for e in range(2):
                        V.tensor_tensor(t2[:, :, :, e], qk2[:, :, :, 1 - e],
                                        sin_sb[:, e].unsqueeze(1).to_broadcast([P, 2 * H, DH // 2]), ALU.mult).then_inc(a_rope_mul, 1)
                    dve.wait_ge(a_rope_mul, 3 * t + 3)
                    V.tensor_tensor(a_t1, a_t1, a_t2, ALU.add).then_inc(a_rope, 1)
                elif k in (3, 4):
                    g = k - 3
                    dve.wait_ge(a_s_done, 2 * t + g + 1)
                    V.tensor_tensor(a_s[:, HG * g:HG * g + HG], ps[:, BANK_A].rearrange("p (h s) -> p h s", h=HG),
                                    causal_sb[:].unsqueeze(1).to_broadcast([P, HG, SP]), ALU.add).then_inc(a_masked, 1)
                    if g == 1:
                        dve.wait_ge(a_masked, 2 * t + 2)
                        V.tensor_reduce(a_mx[:], a_s, AX.X, ALU.max).then_inc(a_max_done, 1)
                        dve.wait_ge(a_max_done, t + 1)
                        V.tensor_tensor(a_s, a_s, a_mx[:].unsqueeze(2).to_broadcast([P, H, SP]), ALU.subtract).then_inc(a_sub_done, 1)
                elif k == 5:
                    dve.wait_ge(a_exp_done, t + 1)
                    V.tensor_reduce(a_sum[:], a_p.rearrange("p (h s) -> p h s", h=H), AX.X, ALU.add).then_inc(a_sum_done, 1)
                    dve.wait_ge(a_sum_done, t + 1)
                    V.reciprocal(a_rs[:], a_sum[:]).then_inc(a_rs_done, 1)
                elif k == 7:
                    dve.wait_ge(a_rs_done, t + 1)
                    dve.wait_ge(a_pv_done, t + 1)
                    for j in range(2):
                        rows = slice(SP * j, SP * j + SP)
                        src = ps[rows, BANK_A].rearrange("p (r j x) -> p r j x", r=PAIRS, j=2)[:, :, j]
                        V.tensor_tensor(a_o[rows].rearrange("p (r h d) -> p r h d", r=PAIRS, h=2),
                                        src.rearrange("p r (h d) -> p r h d", h=2),
                                        a_rs[rows].rearrange("p (r h) -> p r h", h=2).unsqueeze(3).to_broadcast([SP, PAIRS, 2, DH]),
                                        ALU.mult).then_inc(a_o_done, 1)
                elif k == 9:
                    dve.wait_ge(a_out_done, t + 1)
                    V.tensor_tensor(a_y, ps[:, BANK_A, 0:D], a_x[:], ALU.add).then_inc(a_y_done, 1)
                    dve.wait_ge(a_y_done, t + 1)
                    V.bn_stats(a_st[:], a_y).then_inc(a_ln, 1)
                    dve.wait_ge(a_ln, 3 * t + 1)
                    V.memset(a_pace[:], 0.0)
                    V.bn_aggr(a_mv[:], a_st[:]).then_inc(a_ln, 1)
                    dve.wait_ge(a_ln, 3 * t + 2)
                    V.tensor_scalar(a_ve[:], a_mv[:, 1:2], EPS, None, ALU.add).then_inc(a_ln, 1)
                    if not (isinstance(t, int) and t == 0):
                        dve.wait_ge(a_x1_kept, t)
                    dve.wait_ge(a_rstd_done, t + 1)
                    V.tensor_scalar(a_x1, a_y, a_mv[:, 0:1], a_rstd[:], ALU.subtract, ALU.mult).then_inc(a_x1_done, 1)
                elif k == 10:
                    dve.wait_ge(a_x1_done, t + 1)
                    V.tensor_reduce(a_am[:], a_x1, AX.X, ALU.max, apply_absolute_value=True).then_inc(a_quant, 1)
                    dve.wait_ge(a_quant, 5 * t + 1)
                    V.tensor_scalar(a_sx[:], a_am[:], 1.0 / 127.0, 1e-8, ALU.mult, ALU.max).then_inc(a_quant, 1)
                    dve.wait_ge(a_quant, 5 * t + 2)
                    V.reciprocal(a_rsx[:], a_sx[:]).then_inc(a_quant, 1)
                    dve.wait_ge(a_quant, 5 * t + 3)
                    V.tensor_scalar(a_q1, a_x1, a_rsx[:], ROUND, ALU.mult, ALU.add).then_inc(a_quant, 1)
                    dve.wait_ge(a_quant, 5 * t + 4)
                    V.tensor_scalar(a_q1, a_q1, ROUND - 127.0, ROUND + 127.0, ALU.max, ALU.min).then_inc(a_quant, 1)
                    dve.wait_ge(a_quant, 5 * t + 5)
                    V.tensor_scalar(a_xq[:], a_q1, ROUND, None, ALU.subtract).then_inc(a_xq_done, 1)
                elif k == 12:
                    dve.wait_ge(a_qp_done, t + 1)
                    V.scalar_tensor_tensor(a_q1, ps[:, BANK_A, 0:D], a_sx[:], swq_b[:], ALU.mult, ALU.mult).then_inc(a_q1_done, 1)
                    dve.wait_ge(a_q1_done, t + 1)
                    V.tensor_tensor(a_q1, a_q1, bq_b[:], ALU.add).then_inc(a_q_done, 1)
                elif k == 13:
                    dve.wait_ge(a_qhi_done, t + 1)
                    V.tensor_tensor(qT_lo[:], ps[:, BANK_A, 0:D].rearrange("p (c n) -> p c n", c=CH),
                                    qT_hi[:].bitcast(F32), ALU.subtract).then_inc(a_qlo_done, 1)

            def kbd_part(j):
                dve.wait_ge(a_qkT_done, 1)
                for g in range(CH):
                    V.tensor_tensor(a_kbd[:, j, g], a_qkT[:, CH + g, SP * j:SP * j + SP].unsqueeze(1).to_broadcast([P, HG, SP]),
                                    hmask[:].unsqueeze(2).to_broadcast([P, HG, SP]), ALU.mult).then_inc(a_kbd_done, 1)

            def unit_steps(b, j, us, ctx_on):
                for u in us:
                    unit_step(b, j, u)
                    if u % 4 == 3:
                        c = u // 4
                        if c == 0:
                            ctx_hi_step(b, j, 2)
                        elif ctx_on:
                            ctx_hi_step(b + 1, 1 - j, c - 1)

            def batch(b, j, t, t_next, units_on):
                ctx_on = t_next is not None
                for slot in range(1, PAIRS + 1):
                    early, late = unit_slots(slot) if units_on else ([], [])
                    if slot < PAIRS:
                        max_step(b, slot)
                    elif units_on:
                        max_step(b + 1, 0)
                    pT_step(b, slot - 1)
                    unit_steps(b + 1, 1 - j, early, ctx_on)
                    if t_next is not None:
                        a_step(A_AT.get(PAIRS * j + slot, -1), t_next)
                    unit_steps(b + 1, 1 - j, late, ctx_on)
                o_step(b, j, t)

            ctx_hi_step(0, 0, 0, True)
            dve.wait_ge(ctx_hi_done, 1)
            V.tensor_tensor(ctx_lo[:, 0], ctx_raw[:, 0], ctx_hi[:, 0].bitcast(F32), ALU.subtract).then_inc(ctx_lo_done, 1)
            ctx_hi_step(0, 0, 1, True)
            dve.wait_ge(dec_in, 16 * len(FOR_DEC))
            for k in range(A_STEPS):
                if k < UNITS:
                    unit_steps(0, 0, [k], True)
                a_step(k, 0)
                if k == 2:
                    kbd_part(0)
                elif k == 3:
                    dve.wait_ge(small_in, 16 * len(SMALL))
                    weights_to_int8(0)
                elif k == 5:
                    weights_to_int8(1)
                elif k == 7:
                    dve.wait_ge(set_dve, 18)
                    dve.wait_ge(set_act, 4)
                    dve.wait_ge(set_pool, 7)
            dve.wait_ge(a_qlo_done, 1)
            for g in range(CH):
                V.tensor_tensor(qbd_lo[:, 0, g], qT_lo[:, g, 0:SP].bitcast(F32).unsqueeze(1).to_broadcast([P, HG, SP]),
                                hmask[:].unsqueeze(2).to_broadcast([P, HG, SP]), ALU.mult).then_inc(qbd_done, 1)
            max_step(0, 0)
            with dve.Fori(0, TILES - 1) as it:
                batch(2 * it, 0, it, it + 1, True)
                batch(2 * it + 1, 1, it, it + 1, True)
            batch(B - 2, 0, TILES - 1, None, True)
            batch(B - 1, 1, TILES - 1, None, False)

            n = [0]

            def own(ins):
                ins.then_inc(p_dve, 1)
                n[0] += 1

            def settle(k=None):
                dve.wait_ge(p_dve, n[0] if k is None else k)

            dve.wait_ge(o_done, 1 + 2 * B)
            quantise(o_all[:], sm[:, 0], sm[:, 1], sm[:, 9], o_all[:], f_oq[:], p_dve, 0, TILES)
            n[0] = at["integers"] = 6
            for t in range(TILES):
                dve.wait_ge(p_pe, TILES + t + 1)
                own(V.scalar_tensor_tensor(o_all[:, t], ps[:, 4 + t % 4, 0:D], sm[:, 1, t:t + 1], swp_b[:], ALU.mult, ALU.mult))
            settle()
            own(V.tensor_tensor(o_all[:], o_all[:], bp_b[:].unsqueeze(1).to_broadcast([P, TILES, D]), ALU.add))
            settle()
            own(V.tensor_tensor(o_all[:], o_all[:], x1_all[:], ALU.add))
            settle()
            for t in range(TILES):
                own(V.bn_stats(st8[:, t], o_all[:, t]))
            settle()
            for t in range(TILES):
                own(V.bn_aggr(mv8[:, t], st8[:, t]))
            settle()
            own(V.tensor_scalar(sm[:, 2], mv8[:, :, 1], EPS, None, ALU.add))
            at["variances"] = n[0]
            dve.wait_ge(p_pool, 1)
            for t in range(TILES):
                own(V.tensor_scalar(acc[:, t], o_all[:, t], mv8[:, t, 0:1], sm[:, 3, t:t + 1], ALU.subtract, ALU.mult))
            dve.wait_ge(p_pe, 4 * TILES)
            lg, top, sel1, sel2, slots = sm8[:, 0], sm8[:, 1], sm8[:, 3], sm8[:, 4], sm8[:, 5]
            own(V.tensor_tensor(lg, ps[:, 4, 0:TILES * E].rearrange("p (t e) -> p t e", e=E),
                                gb_b[:].unsqueeze(1).to_broadcast([P, TILES, E]), ALU.add))
            settle()
            for t in range(TILES):
                own(V.max(top[:, t], lg[:, t]))
            settle()
            for t in range(TILES):
                own(V.max_index(idx8[:, t], top[:, t], lg[:, t]))
            own(V.tensor_tensor(sm[:, 7], top[:, :, 1], top[:, :, 0], ALU.subtract))
            at["gaps"] = n[0]
            settle()
            own(V.tensor_copy(sm8[:, 2], idx8[:]))
            settle()
            for i, dst in enumerate((sel1, sel2)):
                own(V.tensor_tensor(dst, iota8[:].unsqueeze(1).to_broadcast([P, TILES, E]),
                                    sm8[:, 2, :, i:i + 1].to_broadcast([P, TILES, E]), ALU.is_equal))
            settle()
            for dst in (sel1, sel2):
                own(V.tensor_scalar(dst, dst, valid_sb[:], None, ALU.mult))
            settle()
            own(V.tensor_tensor(oh16[:], sel1, sel2, ALU.add))
            at["choices"] = n[0]
            dve.wait_ge(p_act, 2 * TILES + 1)
            own(V.tensor_scalar(sm[:, 10], sm[:, 8], 1.0, None, ALU.add))
            settle()
            own(V.reciprocal(comb[:, 0], sm[:, 10]))
            settle()
            own(V.tensor_tensor(comb[:, 1], sm[:, 8], comb[:, 0], ALU.mult))
            dve.wait_ge(p_pe, 4 * TILES + 2)
            tot = ps[:, 6, 0:TILES * E].rearrange("p (t e) -> p t e", e=E)
            rank = ps[:, 5, 0:TILES * E].rearrange("p (t e) -> p t e", e=E)
            tots, cum = sm8[:, 6], sm8[:, 7]
            own(V.tensor_copy(tots, tot))
            own(V.memset(cum[:, 0], 0.0))
            settle()
            for t in range(1, TILES):
                own(V.tensor_tensor(cum[:, t], cum[:, t - 1], tots[:, t - 1], ALU.add))
                settle()
            count, tiles, ends, first = (sm8[:, 8, i] for i in range(4))
            own(V.tensor_tensor(count, cum[:, TILES - 1], tots[:, TILES - 1], ALU.add))
            settle()
            own(V.tensor_scalar(tiles, count, 1.0 / P, (P - 1.0) / P - 0.5 + 0.5 / P, ALU.mult, ALU.add))
            settle()
            own(V.tensor_scalar(tiles, tiles, ROUND, ROUND, ALU.add, ALU.subtract))
            settle()
            own(V.tensor_copy(ends[:, 0:1], tiles[:, 0:1]))
            settle()
            for e in range(1, E):
                own(V.tensor_tensor(ends[:, e:e + 1], ends[:, e - 1:e], tiles[:, e:e + 1], ALU.add))
                settle()
            own(V.tensor_tensor(first, ends, tiles, ALU.subtract))
            own(V.tensor_tensor(e_cmp[:], iota_t[:].unsqueeze(2).to_broadcast([P, GT, E]),
                                ends.unsqueeze(1).to_broadcast([P, GT, E]), ALU.is_ge))
            settle()
            own(V.tensor_reduce(e_sum[:], e_cmp[:], AX.X, ALU.add))
            own(V.tensor_scalar(first, first, float(P), None, ALU.mult))
            settle()
            own(V.tensor_scalar(e_tab[:], e_sum[:], E - 1.0, None, ALU.min))
            at["tiles known"] = n[0]
            own(V.tensor_tensor(slots, rank, cum, ALU.add))
            settle()
            own(V.tensor_tensor(slots, slots, first.unsqueeze(1).to_broadcast([P, TILES, E]), ALU.add))
            settle()
            for i, dst in enumerate((sel1, sel2)):
                own(V.tensor_tensor(dst, dst, slots, ALU.mult))
            settle()
            slot_f = sm8[:, 9].rearrange("p t e -> p (t e)")[:, 0:2 * TILES].rearrange("p (t k) -> p t k", k=2)
            for i, src in enumerate((sel1, sel2)):
                own(V.tensor_reduce(slot_f[:, :, i], src, AX.X, ALU.add))
            settle()
            own(V.tensor_tensor(slot_scatter[:], slot_f, dump_sb[:], ALU.add))
            at["slots"] = n[0]
            own(V.tensor_copy(slot_gather[:], slot_f))

            def bias_step(g, first=False):
                for i in range(2):
                    dve.wait_ge(m1_done, 2 * g + i + 1)
                    if i == 0:
                        dve.wait_ge(b1_in, 16 * (g + 1))
                        if not first:
                            dve.wait_ge(gelu_done, g)
                    V.tensor_tensor(hb[:, 512 * i:512 * i + 512], ps[:, H_BANK + i], b1_row[:, 512 * i:512 * i + 512],
                                    ALU.add).then_inc(hb_done, 1)

            def around(g, left=GT, first=False):
                if left > 1:
                    pass
                dve.wait_ge(th_done, 2 * g + 2)
                V.tensor_copy(hT[:, 4:8], ps[:, TH_BANK + 1].rearrange("p (f n) -> p f n", f=4)).then_inc(hT_dve, 1)
                if left > 1:
                    bias_step(g + 1)
                dve.wait_ge(m2_done, g + 1)
                dve.wait_ge(b2_in, 16 * (g + 1))
                if not first:
                    dve.wait_ge(y_out, 16 * g)
                V.tensor_tensor(y_sb[:], ps[:, Y_BANK, 0:D], b2_row[:], ALU.add).then_inc(y_ready, 1)

            bias_step(0, True)
            around(0, first=True)
            with dve.Fori(1, GT - 3) as g:
                around(g)
            for left in (3, 2, 1):
                around(GT - left, left)

            for t in range(TILES):
                dve.wait_ge(gathered[t], 32)
                for k in range(2):
                    V.scalar_tensor_tensor(acc[:, t], got[:, k, t], comb[:, k, t:t + 1], acc[:, t], ALU.mult, ALU.add).then_inc(f_dve, 1)
                    dve.wait_ge(f_dve, 3 * t + k + 1)
                V.bn_stats(st8[:, t], acc[:, t]).then_inc(f_dve, 1)
            dve.wait_ge(f_dve, 3 * TILES)
            for t in range(TILES):
                V.bn_aggr(mv8[:, t], st8[:, t]).then_inc(f_dve, 1)
            dve.wait_ge(f_dve, 4 * TILES)
            V.tensor_scalar(sm[:, 4], mv8[:, :, 1], EPS, None, ALU.add).then_inc(f_dve, 1)

        @block.sync
        def _(sp):
            for dst, src in FOR_KV:
                sp.dma_start(dst, src[:]).then_inc(kv_in, 16)

            def load_x(t, first=False):
                if not first:
                    sp.wait_ge(a_y_done, t)
                sp.dma_start(a_x[:], x_tok[bass.ds(t, 1)].rearrange("a p n -> (a p) n")).then_inc(x_in, 16)
                sp.dma_start(a_xT[:], x_T[bass.ds(t, 1)].rearrange("a p c n -> (a p) c n")).then_inc(x_in, 16)

            def load_ctx(b, j, c, first=False):
                if not first:
                    sp.wait_ge(ctx_lo_done, CHUNKS * b + c - 1)
                sp.dma_start(ctx_raw[:, (CHUNKS * j + c) % 2], ctx_T[bass.ds(b, 1), c].rearrange("a p c n -> (a p) c n")).then_inc(ctx_in[(CHUNKS * j + c) % 2], 16)

            load_ctx(0, 0, 0, True)
            load_x(0, True)
            for dst, src in FOR_DEC:
                sp.dma_start(dst, src[:]).then_inc(dec_in, 16)
            load_ctx(0, 0, 1, True)
            for dst, src in SMALL:
                sp.dma_start(dst, src[:]).then_inc(small_in, 16)
            load_ctx(0, 0, 2)
            load_ctx(1, 1, 0)
            load_ctx(1, 1, 1)
            sp.wait_ge(set_pool, 5)
            sp.dma_start(xs_tiles.rearrange("g p n -> p g n"), zeros[:].unsqueeze(1).to_broadcast([P, GT, D])).then_inc(zeroed, 16)
            load_ctx(1, 1, 2)
            with sp.Fori(0, TILES - 1) as it:
                load_x(it + 1)
                for j in range(2):
                    for c in range(CHUNKS):
                        load_ctx(2 * it + 2 + j, j, c)

            sp.wait_ge(o_done, 1 + 2 * B)
            for e in range(E):
                sp.dma_start(w1_sb[:, e], w1[e]).then_inc(w_in, 16)
                sp.dma_start(w2_sb[:, e], w2[e]).then_inc(w_in, 16)

            def load_xg(g):
                sp.dma_start(xg[:], xs_tiles[bass.ds(g, 1)].rearrange("a p n -> (a p) n")).then_inc(xg_in, 16)

            def load_b1(g):
                e = sp.value_load(e_tab[0:1, bass.ds(g, 1)], min_val=0, max_val=E - 1)
                sp.dma_start(b1_row[:], b1[bass.ds(e, 1)].to_broadcast([P, F])).then_inc(b1_in, 16)

            def load_b2(g):
                e = sp.value_load(e_tab[0:1, bass.ds(g, 1)], min_val=0, max_val=E - 1)
                sp.dma_start(b2_row[:], b2[bass.ds(e, 1)].to_broadcast([P, D])).then_inc(b2_in, 16)

            sp.wait_ge(p_dve, at["tiles known"])
            load_b1(0)
            load_b2(0)
            sp.wait_ge(scattered, 16 * 2 * TILES)
            load_xg(0)
            sp.wait_ge(tx_done, 1)
            load_xg(1)
            sp.wait_ge(hb_done, 2)
            load_b1(1)
            sp.wait_ge(tx_done, 2)
            load_xg(2)

            def around(g, left=GT):
                if left > 2:
                    sp.wait_ge(hb_done, 2 * g + 4)
                    load_b1(g + 2)
                if left > 3:
                    sp.wait_ge(tx_done, g + 3)
                    load_xg(g + 3)
                sp.wait_ge(y_ready, g + 1)
                sp.dma_start(ys_tiles[bass.ds(g, 1)].rearrange("a p n -> (a p) n"), y_sb[:]).then_inc(y_out, 16)
                if left > 1:
                    load_b2(g + 1)

            with sp.Fori(0, GT - 3) as g:
                around(g)
            for left in (3, 2, 1):
                around(GT - left, left)

            for t in range(TILES):
                sp.wait_ge(f_pool, 1 + 1 + t)
                for j in range(2):
                    sp.dma_start(out[2 * t + j], o_all[SP * j:SP * j + S, t]).then_inc(out_done, 16)
            sp.wait_ge(out_done, 16 * B)

        @block.gpsimd
        def _(pool):
            nc.gpsimd.memset(ones[:], 1.0).then_inc(set_pool, 1)
            nc.gpsimd.memset(neg_half[:], -0.5).then_inc(set_pool, 1)
            nc.gpsimd.memset(a_vb[:], 0.0).then_inc(set_pool, 1)
            nc.gpsimd.memset(ones16[:], 1.0).then_inc(set_pool, 1)
            nc.gpsimd.memset(zeros[:], 0.0).then_inc(set_pool, 1)

            def ctx_lo_step(b, j, c, first=False):
                if not first:
                    pool.wait_ge(unit_done, 4 * (CHUNKS * b + c - 1))
                k = (CHUNKS * j + c) % 2
                pool.wait_ge(ctx_hi_done, CHUNKS * b + c + 1)
                nc.gpsimd.tensor_tensor(ctx_lo[:, k], ctx_raw[:, k], ctx_hi[:, k].bitcast(F32),
                                        ALU.subtract).then_inc(ctx_lo_done, 1)

            def kbd_step(t, batches=(0, 1)):
                pool.wait_ge(a_qkT_done, t + 1)
                for j in batches:
                    for g in range(CH):
                        nc.gpsimd.tensor_tensor(
                            a_kbd[:, j, g],
                            a_qkT[:, CH + g, SP * j:SP * j + SP].unsqueeze(1).to_broadcast([P, HG, SP]),
                            hmask[:].unsqueeze(2).to_broadcast([P, HG, SP]), ALU.mult).then_inc(a_kbd_done, 1)

            def rstd_step(t):
                pool.wait_ge(a_ln, 3 * t + 3)
                nc.gpsimd.tensor_tensor(a_rstd[:], a_ve[:], neg_half[:, 0:1], ALU.pow).then_inc(a_rstd_done, 1)

            def qbd_step(t, j, first=False, parts=((qT_hi, qbd_hi), (qT_lo, qbd_lo))):
                if j == 0:
                    pool.wait_ge(a_qlo_done, t + 1)
                if not first:
                    pool.wait_ge(s_done, PAIRS * (2 * t + j - 1))
                for src, dst in parts:
                    for g in range(CH):
                        nc.gpsimd.tensor_tensor(
                            dst[:, j, g],
                            src[:, g, SP * j:SP * j + SP].bitcast(F32).unsqueeze(1).to_broadcast([P, HG, SP]),
                            hmask[:].unsqueeze(2).to_broadcast([P, HG, SP]), ALU.mult).then_inc(qbd_done, 1)

            ctx_lo_step(0, 0, 1, True)
            pool.wait_ge(dec_in, 16 * len(FOR_DEC))
            nc.gpsimd.tensor_copy(id16[:], id32[:]).then_inc(set_pool, 1)
            kbd_step(0, (1,))
            pool.wait_ge(small_in, 16 * len(SMALL))
            nc.gpsimd.tensor_copy(before16[:], before32).then_inc(set_pool, 1)
            ctx_lo_step(0, 0, 2)
            ctx_lo_step(1, 1, 0)
            rstd_step(0)
            qbd_step(0, 0, True, ((qT_hi, qbd_hi),))
            pool.wait_ge(qbd_done, 4)
            qbd_step(0, 1, True)
            with pool.Fori(0, TILES - 1) as it:
                ctx_lo_step(2 * it + 1, 1, 1)
                kbd_step(it + 1)
                ctx_lo_step(2 * it + 1, 1, 2)
                ctx_lo_step(2 * it + 2, 0, 0)
                ctx_lo_step(2 * it + 2, 0, 1)
                rstd_step(it + 1)
                ctx_lo_step(2 * it + 2, 0, 2)
                qbd_step(it + 1, 0)
                ctx_lo_step(2 * it + 3, 1, 0)
                qbd_step(it + 1, 1)
            ctx_lo_step(B - 1, 1, 1)
            ctx_lo_step(B - 1, 1, 2)

            pool.wait_ge(p_dve, at["variances"])
            nc.gpsimd.tensor_tensor(sm[:, 3], sm[:, 2], neg_half[:], ALU.pow).then_inc(p_pool, 1)
            pool.wait_ge(zeroed, 16)
            pool.wait_ge(p_dve, at["slots"])
            for t in range(TILES):
                for k in range(2):
                    nc.gpsimd.indirect_dma_start(
                        out=xs, out_offset=bass.IndirectOffsetOnAxis(ap=slot_scatter[:, t, k:k + 1], axis=0),
                        in_=acc[:, t], in_offset=None).then_inc(scattered, 16)
            pool.wait_ge(y_out, 16 * GT)
            for t in range(TILES):
                for k in range(2):
                    nc.gpsimd.indirect_dma_start(
                        out=got[:, k, t], out_offset=None, in_=ys,
                        in_offset=bass.IndirectOffsetOnAxis(ap=slot_gather[:, t, k:k + 1], axis=0)).then_inc(gathered[t], 16)
            pool.wait_ge(f_dve, 4 * TILES + 1)
            nc.gpsimd.tensor_tensor(sm[:, 5], sm[:, 4], neg_half[:], ALU.pow).then_inc(f_pool, 1)
            pool.wait_ge(f_pool, 1)
            for t in range(TILES):
                nc.gpsimd.tensor_scalar(o_all[:, t], acc[:, t], mv8[:, t, 0:1], sm[:, 5, t:t + 1],
                                        ALU.subtract, ALU.mult).then_inc(f_pool, 1)

        @block.scalar
        def _(act):
            def copy(dst, src):
                return nc.scalar.copy(dst, src)

            def weights_step(n):
                act.wait_ge(set_pe, 2 * n + 1)
                copy((wqqT, wpqT)[n][:], ps[:, BANK_S + n].bitcast(BF16)[:, 0:CH * D].rearrange("p (c n) -> p c n", c=CH)).then_inc(set_act, 1)
                act.wait_ge(set_pe, 2 * n + 2)
                copy((swq_b, swp_b)[n][:], ps[:, BANK_T + n, 0:D]).then_inc(set_act, 1)

            def k_hi_step(b, par, u, u_global):
                c, g = u // 4, u % 4
                act.wait_ge(unit_done, u_global + 1)
                nc.scalar.activation(k_hi[:, par, g, MC * c:MC * c + MC], ps[:, BANK_KV, 0:MC], ACT.Identity,
                                     bias=bk_sb[:, g:g + 1]).then_inc(k_hi_done, 1)

            def units(b_next, par, us):
                for u in us:
                    if u % 4 < 2:
                        k_hi_step(b_next, par, u, UNITS * b_next + u)

            def exp_step(b, par, p):
                act.wait_ge(max_done, PAIRS * b + p + 1)
                nc.scalar.activation(pr[:, p % 2].rearrange("p (c n) -> p c n", c=CHUNKS), ps[:, BANK_S:BANK_S + CHUNKS, 0:MC],
                                     ACT.Exp, bias=negmax[:, p % 2:p % 2 + 1],
                                     accum_out=sumexp[:, par, p:p + 1]).then_inc(exp_done, 1)

            def pT_step(b, p, q):
                n = (3 * p + q) % 2
                act.wait_ge(tr_done, 3 * PAIRS * b + 3 * p + q + 1)
                copy(pT[0:MT, n], ps[0:MT, BANK_T + n].rearrange("p (t n) -> p t n", t=TPC)).then_inc(pT_outer, 1)

            def oT_step(b, half):
                act.wait_ge(pv_done, PAIRS * b + 4 * half + 4)
                copy(oT_sb[:, 4 * half:4 * half + 4], ps[:, BANK_O].rearrange("p (c n) -> p c n", c=4)).then_inc(oT_done, 1)

            def a_step(k, t):
                if k == 1:
                    act.wait_ge(a_v_done, t + 1)
                    for j in range(2):
                        for hp in range(2):
                            src = ps[SP * j:SP * j + SP, BANK_A, 0:D].rearrange("p (r h d) -> p r h d", r=PAIRS, h=2)
                            copy(a_vb[SP * hp:SP * hp + SP, :, j, DH * hp:DH * hp + DH], src[:, :, hp]).then_inc(a_vb_done, 1)
                elif k == 2:
                    act.wait_ge(a_tqk_done, t + 1)
                    copy(a_qkT, ps[:, BANK_A].rearrange("p (c n) -> p c n", c=4)).then_inc(a_qkT_done, 1)
                elif k == 4:
                    act.wait_ge(a_sub_done, t + 1)
                    nc.scalar.activation(a_p, a_p, ACT.Exp).then_inc(a_exp_done, 1)
                elif k in (5, 6):
                    act.wait_ge(a_tp_done, 2 * t + k - 4)
                    copy(a_pT[:, 4 * (k - 5):4 * (k - 5) + 4], ps[:, BANK_A].rearrange("p (c n) -> p c n", c=4)).then_inc(a_pT_done, 1)
                elif k == 8:
                    act.wait_ge(a_to_done, t + 1)
                    copy(a_oT, ps[:, BANK_A, 0:D].rearrange("p (c n) -> p c n", c=CH)).then_inc(a_oT_done, 1)
                elif k == 9:
                    act.wait_ge(a_x1_done, t + 1)
                    copy(x1_all[:, bass.ds(t, 1)].rearrange("p a n -> p (a n)"), a_x1).then_inc(a_x1_kept, 1)
                elif k == 11:
                    act.wait_ge(a_txq_done, t + 1)
                    copy(a_xqT[:], ps[:, BANK_A].bitcast(BF16)[:, 0:D].rearrange("p (c n) -> p c n", c=CH)).then_inc(a_xqT_done, 1)
                elif k == 13:
                    act.wait_ge(a_tq_done, t + 1)
                    copy(qT_hi[:], ps[:, BANK_A, 0:D].rearrange("p (c n) -> p c n", c=CH)).then_inc(a_qhi_done, 1)

            def batch(b, j, t_next, units_on):
                for slot in range(1, PAIRS + 1):
                    early, late = unit_slots(slot) if units_on else ([], [])
                    if slot == PAIRS // 2 + 1:
                        oT_step(b, 0)
                    pT_step(b, slot - 1, 0)
                    hurry = early and late and late[0] % 4 == 1
                    if hurry:
                        units(b + 1, 1 - j, early)
                    if slot < PAIRS:
                        exp_step(b, j, slot)
                    elif units_on:
                        exp_step(b + 1, 1 - j, 0)
                    if not hurry:
                        units(b + 1, 1 - j, early)
                    pT_step(b, slot - 1, 2)
                    if t_next is not None:
                        a_step(A_AT.get(PAIRS * j + slot, -1), t_next)
                    units(b + 1, 1 - j, late)
                oT_step(b, 1)

            act.wait_ge(kv_in, 16 * len(FOR_KV))
            for k in range(A_STEPS):
                if k < UNITS:
                    units(0, 0, [k])
                a_step(k, 0)
                if k in (4, 6):
                    weights_step(k // 2 - 2)
            exp_step(0, 0, 0)
            with act.Fori(0, TILES - 1) as it:
                batch(2 * it, 0, it + 1, True)
                batch(2 * it + 1, 1, it + 1, True)
            batch(B - 2, 0, None, True)
            batch(B - 1, 1, None, False)

            for t in range(TILES):
                act.wait_ge(p_pe, t + 1)
                copy(f_oqT[:, t], ps[:, t % 4].bitcast(BF16)[:, 0:D].rearrange("p (c n) -> p c n", c=CH)).then_inc(p_act, 1)
            for t in range(TILES):
                act.wait_ge(p_pe, 2 * TILES + t + 1)
                copy(x2T[:, :, t], ps[:, t % 4, 0:D].rearrange("p (c n) -> p c n", c=CH)).then_inc(p_act, 1)
            act.wait_ge(p_dve, at["gaps"])
            nc.scalar.activation(sm[:, 8], sm[:, 7], ACT.Exp).then_inc(p_act, 1)

            def xgT_step(g):
                act.wait_ge(tx_done, g + 1)
                copy(xgT[:], ps[:, XG_BANK, 0:D].rearrange("p (c n) -> p c n", c=CH)).then_inc(xgT_done, 1)

            def gelu_step(g):
                act.wait_ge(hb_done, 2 * g + 2)
                nc.scalar.activation(hg[:], hb[:], ACT.Gelu_apprx_tanh).then_inc(gelu_done, 1)

            def around(g, left=GT):
                act.wait_ge(th_done, 2 * g + 1)
                copy(hT[:, 0:4], ps[:, TH_BANK].rearrange("p (f n) -> p f n", f=4)).then_inc(hT_act, 1)
                if left > 1:
                    gelu_step(g + 1)
                if left > 2:
                    xgT_step(g + 2)

            xgT_step(0)
            gelu_step(0)
            xgT_step(1)
            with act.Fori(0, GT - 3) as g:
                around(g)
            for left in (3, 2, 1):
                around(GT - left, left)

        @block.tensor
        def _(pe):
            mm = nc.tensor.matmul

            def transpose(dst, src, n):
                return nc.tensor.transpose(dst, src, (id16 if src.dtype == BF16 else id32)[0:n, 0:n])

            def weights_step(n):
                pe.wait_ge(set_pool, 6)
                pe.wait_ge(set_dve, 2 + 8 * n + 6)
                for g in range(CH):
                    for c in range(CH):
                        last = transpose(ps[:, BANK_S + n].bitcast(BF16)[:, c * D + g * P:c * D + g * P + P],
                                         w_int[n][:, g, c * P:c * P + P], P)
                last.then_inc(set_pe, 1)
                pe.wait_ge(set_dve, 2 + 8 * n + 8)
                mm(ps[:, BANK_T + n, 0:D], ones[:], w_diag[n].rearrange("p c n -> p (c n)"), start=True, stop=True).then_inc(set_pe, 1)

            SPLIT = ((0, 0), (0, 1), (1, 0))

            def unit(b, j, u, first=False):
                c, g = u // 4, u % 4
                place = (CHUNKS * j + c) % 2
                cs, ws = (ctx_hi, ctx_lo), (wkv_hi, wkv_lo)
                pe.wait_ge(ctx_lo_done, CHUNKS * b + c + 1)
                if not first:
                    pe.wait_ge(unit_out, UNITS * b + u)
                if g < 2:
                    for i, (x, w) in enumerate(SPLIT):
                        for k in range(CH):
                            last = mm(ps[:, BANK_KV, 0:MC], ws[w][:, k, P * g:P * g + P], cs[x][:, place, k, :],
                                      start=(i == 0 and k == 0), stop=(i == 2 and k == CH - 1))
                else:
                    for m in range(2):
                        a = MT * (2 * (g - 2) + m)
                        for i, (x, w) in enumerate(SPLIT):
                            for k in range(CH):
                                last = mm(ps[0:MT, BANK_KV, D * m:D * m + D], cs[x][:, place, k, a:a + MT], ws[w][:, k, D:2 * D],
                                          start=(i == 0 and k == 0), stop=(i == 2 and k == CH - 1))
                last.then_inc(unit_done, 1)

            def scores(b, j, p, first=False):
                g, r = p // (PAIRS // CH), p % (PAIRS // CH)
                if p == 0:
                    pe.wait_ge(unit_out, UNITS * b + UNITS - 2)
                    pe.wait_ge(qbd_done, 4 * (b + 1))
                if not first:
                    pe.wait_ge(exp_done, PAIRS * b + p)
                ks, qs = (k_hi, k_lo), (qbd_hi, qbd_lo)
                for i, (kk, qq) in enumerate(SPLIT):
                    q = qs[qq][:, j, g, 2 * r:2 * r + 2, :].rearrange("p h s -> p (h s)")
                    for c in range(CHUNKS):
                        last = mm(ps[:, BANK_S + c, 0:MC], q, ks[kk][:, j, g, MC * c:MC * c + MC], start=(i == 0), stop=(i == 2))
                last.then_inc(s_done, 1)

            def tr(b, p, q):
                n = 3 * p + q
                pe.wait_ge(exp_done, PAIRS * b + p + 1)
                for i in range(TPC):
                    a = MC * q + MT * i
                    last = transpose(ps[0:MT, BANK_T + n % 2, P * i:P * i + P], pr[:, p % 2, a:a + MT], P)
                last.then_inc(tr_done, 1)

            def pv(b, j, p, q):
                n = 3 * p + q
                if q == 0 and p == 0:
                    pe.wait_ge(unit_out, UNITS * (b + 1))
                    pe.wait_ge(o_done, 2 * b + 1)
                if q == 0 and p == PAIRS // 2:
                    pe.wait_ge(oT_done, 2 * b + 1)
                if q == 1:
                    pe.wait_ge(pT_inner, PAIRS * b + p + 1)
                else:
                    pe.wait_ge(pT_outer, 2 * PAIRS * b + 2 * p + q // 2 + 1)
                for i in range(TPC):
                    last = mm(ps[32 * i:32 * i + 32, BANK_O, P * (p % 4):P * (p % 4) + P],
                              v_sb[0:MT, j, TPC * q + i, 32 * p:32 * p + 32], pT[0:MT, n % 2, i],
                              start=(q == 0), stop=(q == 2))
                if q == 2:
                    last.then_inc(pv_done, 1)

            def o_back(b):
                pe.wait_ge(oT_done, 2 * b + 2)
                for p in range(PAIRS):
                    last = mm(ps[:, BANK_O, 32 * p:32 * p + 32], oT_sb[:, p], sel_sb[:], start=True, stop=True)
                last.then_inc(o_back_done, 1)

            def a_step(k, t, first=False):
                A = ps[:, BANK_A]
                if k == 0:
                    pe.wait_ge(x_in, 32 * (t + 1))
                    if not first:
                        pe.wait_ge(a_qlo_done, t)
                    for c in range(CH):
                        last = mm(A, a_xT[:, c], wqkv_sb[:, c, 0:2 * D], start=(c == 0), stop=(c == CH - 1))
                    last.then_inc(a_qk_done, 1)
                elif k == 1:
                    pe.wait_ge(a_rope_mul, 3 * t + 3)
                    for c in range(CH):
                        last = mm(A[:, 0:D], a_xT[:, c], wqkv_sb[:, c, 2 * D:3 * D], start=(c == 0), stop=(c == CH - 1))
                    last.then_inc(a_v_done, 1)
                elif k == 2:
                    pe.wait_ge(a_rope, t + 1)
                    pe.wait_ge(a_vb_done, 4 * t + 4)
                    for c in range(4):
                        last = transpose(A[:, P * c:P * c + P], a_t1[:, P * c:P * c + P], P)
                    last.then_inc(a_tqk_done, 1)
                elif k in (3, 4):
                    g = k - 3
                    pe.wait_ge(a_kbd_done, 4 * t + 4)
                    if g == 1:
                        pe.wait_ge(a_masked, 2 * t + 1)
                    for j in range(2):
                        last = mm(ps[SP * j:SP * j + SP, BANK_A], a_qkT[:, g, SP * j:SP * j + SP],
                                  a_kbd[:, j, g].rearrange("p h s -> p (h s)"), start=True, stop=True)
                    last.then_inc(a_s_done, 1)
                elif k in (5, 6):
                    pe.wait_ge(a_exp_done, t + 1)
                    if k == 6:
                        pe.wait_ge(a_pT_done, 2 * t + 1)
                    for r in range(4):
                        a = P * (4 * (k - 5) + r)
                        last = transpose(A[:, P * r:P * r + P], a_p[:, a:a + P], P)
                    last.then_inc(a_tp_done, 1)
                elif k == 7:
                    pe.wait_ge(a_pT_done, 2 * t + 2)
                    for r in range(PAIRS):
                        last = mm(A[:, 64 * r:64 * r + 64], a_pT[:, r], a_vb[:, r].rearrange("p j d -> p (j d)"), start=True, stop=True)
                    last.then_inc(a_pv_done, 1)
                elif k == 8:
                    pe.wait_ge(a_o_done, 2 * t + 2)
                    for c in range(CH):
                        last = transpose(A[:, P * c:P * c + P], a_o[:, P * c:P * c + P], P)
                    last.then_inc(a_to_done, 1)
                elif k == 9:
                    pe.wait_ge(a_oT_done, t + 1)
                    for c in range(CH):
                        last = mm(A[:, 0:D], a_oT[:, c], wout_sb[:, c], start=(c == 0), stop=(c == CH - 1))
                    last.then_inc(a_out_done, 1)
                elif k == 11:
                    pe.wait_ge(a_xq_done, t + 1)
                    for c in range(CH):
                        last = transpose(A.bitcast(BF16)[:, P * c:P * c + P], a_xq[:, P * c:P * c + P], P)
                    last.then_inc(a_txq_done, 1)
                elif k == 12:
                    pe.wait_ge(a_xqT_done, t + 1)
                    for c in range(CH):
                        last = mm(A[:, 0:D], a_xqT[:, c], wqqT[:, c], start=(c == 0), stop=(c == CH - 1))
                    last.then_inc(a_qp_done, 1)
                elif k == 13:
                    pe.wait_ge(a_q_done, t + 1)
                    for c in range(CH):
                        last = transpose(A[:, P * c:P * c + P], a_q1[:, P * c:P * c + P], P)
                    last.then_inc(a_tq_done, 1)

            def batch(b, j, t_next, units_on):
                for slot in range(1, PAIRS + 1):
                    if slot < PAIRS:
                        scores(b, j, slot)
                    elif units_on:
                        scores(b + 1, 1 - j, 0)
                    early, late = unit_slots(slot) if units_on else ([], [])
                    if slot > 1:
                        pv(b, j, slot - 2, 2)
                    tr(b, slot - 1, 0)
                    tr(b, slot - 1, 1)
                    for u in early:
                        unit(b + 1, 1 - j, u)
                    pv(b, j, slot - 1, 0)
                    tr(b, slot - 1, 2)
                    pv(b, j, slot - 1, 1)
                    if t_next is not None:
                        a_step(A_AT.get(PAIRS * j + slot, -1), t_next)
                    if slot == PAIRS:
                        pv(b, j, PAIRS - 1, 2)
                    for u in late:
                        unit(b + 1, 1 - j, u)
                o_back(b)

            pe.wait_ge(set_dve, 2)
            pe.wait_ge(set_pool, 5)
            for k in range(A_STEPS):
                if k < UNITS:
                    unit(0, 0, k, k == 0)
                if k == 0:
                    pe.wait_ge(dec_in, 16 * len(FOR_DEC))
                a_step(k, 0, True)
                if k in (4, 6):
                    weights_step(k // 2 - 2)
            pe.wait_ge(set_act, 4)
            scores(0, 0, 0, True)
            with pe.Fori(0, TILES - 1) as it:
                batch(2 * it, 0, it + 1, True)
                batch(2 * it + 1, 1, it + 1, True)
            batch(B - 2, 0, None, True)
            batch(B - 1, 1, None, False)

            pe.wait_ge(p_dve, at["integers"])
            for t in range(TILES):
                if t >= 4:
                    pe.wait_ge(p_act, t - 3)
                for c in range(CH):
                    last = transpose(ps[:, t % 4].bitcast(BF16)[:, P * c:P * c + P], f_oq[:, t, P * c:P * c + P], P)
                last.then_inc(p_pe, 1)
            for t in range(TILES):
                pe.wait_ge(p_act, t + 1)
                if t >= 4:
                    pe.wait_ge(p_dve, at["integers"] + t - 3)
                for c in range(CH):
                    last = mm(ps[:, 4 + t % 4, 0:D], f_oqT[:, t, c], wpqT[:, c], start=(c == 0), stop=(c == CH - 1))
                last.then_inc(p_pe, 1)
            for t in range(TILES):
                pe.wait_ge(p_dve, at["variances"] + t + 1)
                pe.wait_ge(p_act, TILES + max(0, t - 3))
                for c in range(CH):
                    last = transpose(ps[:, t % 4, P * c:P * c + P], acc[:, t, P * c:P * c + P], P)
                last.then_inc(p_pe, 1)
            for t in range(TILES):
                pe.wait_ge(p_act, TILES + t + 1)
                for c in range(CH):
                    last = mm(ps[:, 4, E * t:E * t + E], x2T[:, c, t], gw_sb[:, c], start=(c == 0), stop=(c == CH - 1))
                last.then_inc(p_pe, 1)
            pe.wait_ge(p_dve, at["choices"])
            choices = oh16[:].rearrange("p t e -> p (t e)")
            mm(ps[:, 5, 0:TILES * E], before16[:], choices, start=True, stop=True).then_inc(p_pe, 1)
            mm(ps[:, 6, 0:TILES * E], ones16[:], choices, start=True, stop=True).then_inc(p_pe, 1)

            def expert_of(g):
                return pe.value_load(e_tab[0:1, bass.ds(g, 1)], min_val=0, max_val=E - 1)

            def tx(g):
                pe.wait_ge(xg_in, 16 * (g + 1))
                for c in range(CH):
                    last = transpose(ps[:, XG_BANK, P * c:P * c + P], xg[:, P * c:P * c + P], P)
                last.then_inc(tx_done, 1)

            def m1(g, e, i, first=False):
                if i == 0:
                    pe.wait_ge(xgT_done, g + 1)
                if not first:
                    pe.wait_ge(hb_done, 2 * g - 1 + i)
                for c in range(CH):
                    last = mm(ps[:, H_BANK + i], xgT[:, c],
                              w1_sb[:, bass.ds(e, 1), c, 512 * i:512 * i + 512].rearrange("p a n -> p (a n)"),
                              start=(c == 0), stop=(c == CH - 1))
                last.then_inc(m1_done, 1)

            def th(g):
                pe.wait_ge(gelu_done, g + 1)
                for f in range(FT):
                    last = transpose(ps[:, TH_BANK + f // 4, P * (f % 4):P * (f % 4) + P], hg[:, P * f:P * f + P], P)
                    if f % 4 == 3:
                        last.then_inc(th_done, 1)

            def m2(g, e, first=False):
                pe.wait_ge(hT_act, g + 1)
                pe.wait_ge(hT_dve, g + 1)
                if not first:
                    pe.wait_ge(y_ready, g)
                for f in range(FT):
                    last = mm(ps[:, Y_BANK, 0:D], hT[:, f],
                              w2_sb[:, bass.ds(e, 1), f].rearrange("p a n -> p (a n)"), start=(f == 0), stop=(f == FT - 1))
                last.then_inc(m2_done, 1)

            def around(g, left=GT, first=False):
                if left > 1:
                    e_next = expert_of(g + 1)
                    m1(g + 1, e_next, 0)
                th(g)
                if left > 1:
                    m1(g + 1, e_next, 1)
                if left > 2:
                    tx(g + 2)
                m2(g, expert_of(g), first)

            pe.wait_ge(p_dve, at["tiles known"])
            pe.wait_ge(w_in, 16 * 2 * E)
            tx(0)
            e0 = expert_of(0)
            m1(0, e0, 0, True)
            m1(0, e0, 1, True)
            tx(1)
            around(0, first=True)
            with pe.Fori(1, GT - 3) as g:
                around(g)
            for left in (3, 2, 1):
                around(GT - left, left)


def dump_rows():
    row, tile, choice = np.ogrid[0:P, 0:TILES, 0:2]
    return np.where(row % SP < S, 0, DUMP + (choice * TILES + tile) * P + row).astype(np.float32)


def tables():
    pos = (np.arange(P) % SP).astype(np.float32)
    inv = (1.0 / 10000.0 ** (np.arange(0, DH, 2, dtype=np.float32) / DH)).astype(np.float32)
    freqs = np.outer(pos, inv).astype(np.float32)
    emb = np.concatenate([freqs, freqs], axis=-1)
    cos, sin = np.cos(emb).astype(np.float32), np.sin(emb).astype(np.float32)
    sin_pair = np.stack([-sin[:, 0::2], sin[:, 1::2]], axis=1)
    head = (np.arange(P)[:, None] // DH == np.arange(HG)[None, :]).astype(np.float32) * np.float32(DH ** -0.5)
    causal = np.where(np.arange(SP)[None, :] <= (np.arange(P) % SP)[:, None], 0.0, MASKED).astype(np.float32)
    return {"rope_cos": cos, "rope_sin": np.ascontiguousarray(sin_pair), "head_mask": head, "causal": causal,
            "ident": np.eye(P, dtype=np.float32), "sel": np.tile(np.eye(32, dtype=np.float32), (P // 32, 1)),
            "before": np.triu(np.ones((P, P), np.float32), 1),
            "valid": (np.arange(P) % SP < S).astype(np.float32).reshape(P, 1), "dump": dump_rows(),
            "iota_tiles": np.ascontiguousarray(np.broadcast_to(np.arange(GT, dtype=np.float32), (P, GT))),
            "iota_row": np.ascontiguousarray(np.broadcast_to(np.arange(E, dtype=np.float32), (P, E)))}


def kernel(x, ctx_2048, L0_attn_w_qkv, L0_attn_w_out, L0_attn_w_c1, L0_attn_w_c2, L0_xattn_wq, L0_xattn_bq,
           L0_xattn_wkv, L0_xattn_bkv, L0_xattn_wp, L0_xattn_bp, L0_ffn_gate_w, L0_ffn_gate_b, L0_ffn_w1, L0_ffn_b1,
           L0_ffn_w2, L0_ffn_b2):
    import concourse.bacc as bacc
    from concourse.bass_utils import run_bass_kernel_spmd

    def halves(a):
        return a.reshape(-1, P, a.shape[-1]).transpose(1, 0, 2)

    def rows(v):
        return np.broadcast_to(v.reshape(1, -1), (P, v.size))

    xp = np.zeros((B, SP, D), np.asarray(x).dtype)
    xp[:, :S] = np.asarray(x)
    xp = xp.reshape(TILES, P, D)
    ct = np.asarray(ctx_2048).reshape(B, CHUNKS, MC, CH, P).transpose(0, 1, 4, 3, 2)
    wkv, bkv = np.asarray(L0_xattn_wkv), np.asarray(L0_xattn_bkv)
    arrays = {
        "x_tok": xp, "x_T": xp.reshape(TILES, P, CH, P).transpose(0, 3, 2, 1), "ctx_T": ct,
        "w_qkv_T": halves(np.asarray(L0_attn_w_qkv).T), "w_out_T": halves(np.asarray(L0_attn_w_out).T),
        "wq": halves(np.asarray(L0_xattn_wq)), "bq_row": rows(np.asarray(L0_xattn_bq)),
        "w_kv_T": halves(wkv.T), "bk_col": bkv[:D].reshape(CH, P).T, "bv_row": rows(bkv[D:]),
        "wp": halves(np.asarray(L0_xattn_wp)), "bp_row": rows(np.asarray(L0_xattn_bp)),
        "gate_w": halves(np.asarray(L0_ffn_gate_w)), "gate_b_row": rows(np.asarray(L0_ffn_gate_b)),
        "w1": np.asarray(L0_ffn_w1).reshape(E, CH, P, F).transpose(0, 2, 1, 3),
        "b1": np.asarray(L0_ffn_b1),
        "w2": np.asarray(L0_ffn_w2).reshape(E, FT, P, D).transpose(0, 2, 1, 3), "b2": np.asarray(L0_ffn_b2),
    }
    arrays.update(tables())
    arrays = {k: np.ascontiguousarray(v) for k, v in arrays.items()}
    nc = bacc.Bacc("TRN2", target_bir_lowering=False, num_devices=1)
    args = {k: nc.dram_tensor(k, v.shape, mybir.dt.from_np(v.dtype), kind="ExternalInput").ap() for k, v in arrays.items()}
    out = nc.dram_tensor("out", (B, S, D), F32, kind="ExternalOutput").ap()
    decoder_layer(nc, **args, out=out)
    r = run_bass_kernel_spmd(nc, [arrays], core_ids=[0])
    return r.results[0]["out"]
```

```python
from contextlib import ExitStack

import numpy as np
import concourse.bass as bass
from concourse import mybir

ALU = mybir.AluOpType
ACT = mybir.ActivationFunctionType
AX = mybir.AxisListType
F32 = mybir.dt.float32
F32R = mybir.dt.float32r
BF16 = mybir.dt.bfloat16
F16 = mybir.dt.float16
U32 = mybir.dt.uint32
I32 = mybir.dt.int32

B, S, D = 16, 56, 256
M = 1500
H, DH = 16, 16
E, F = 8, 1024
P = 128
CH = D // P
SP = 64
TILES = B * SP // P
HG = P // DH
PD = 2 * DH
KS = 3 * PD
PAIRS = H // 2
CHUNKS, MC = 3, 500
MT = 125
TPC = MC // MT
UNITS = 4 * CHUNKS
FT = F // P
EARLY_W1, EARLY_W2 = 6, 3
A_STEPS = 15
GT = 2 * B * S // P + E - 1
DUMP = GT * P
EPS = 1e-5
ROUND = 12582912.0
MASKED = -1e30

BANK_S = 0
BANK_T = 3
BANK_O = 5
BANK_KV = 6
XG_BANK, Y_BANK = 0, 1
H_BANK, TH_BANK = 2, 4
BANK_A = 7


def decoder_layer(nc, x_tok, x_T, ctx_T, w_qkv_T, w_out_T, wq, bq_row, w_kv_T, bk_col, bv_row, wp, bp_row,
                  gate_w, gate_b_row, w1, b1, w2, b2, rope_cos, rope_sin, head_mask, pair_mask, causal, ident, iota_row, sel,
                  before, valid, dump, iota_tiles, out):
    with ExitStack() as ctx:
        def sb(name, shape, dt=F32):
            return ctx.enter_context(nc.sbuf_tensor(name, shape, dt))[:]

        def sem(name):
            return ctx.enter_context(nc.semaphore(name))

        ps = ctx.enter_context(nc.psum_tensor("ps", [P, 8, 512], F32))

        id32 = sb("id32", [P, P])
        id16 = sb("id16", [P, P], BF16)
        ones = sb("ones", [P, P])
        iota8 = sb("iota8", [P, E])
        swp_b = sb("swp_b", [P, D])
        wpqT = sb("wpqT", [P, CH, D], BF16)
        bp_b = sb("bp_b", [P, D])
        gw_sb = sb("gw_sb", [P, CH, E])
        gb_b = sb("gb_b", [P, E])
        before16 = sb("before16", [P, P], BF16)
        ones16 = sb("ones16", [P, P], BF16)
        valid_sb = sb("valid_sb", [P, 1])
        dump_sb = sb("dump_sb", [P, TILES, 2])
        iota_t = sb("iota_t", [P, GT])
        neg_half = sb("neg_half", [P, TILES])
        x1_all = sb("x1_all", [P, TILES, D])
        o_all = sb("o_all", [P, TILES, D])
        acc = x1_all
        comb = sb("comb", [P, 2, TILES])
        slot_gather = sb("slot_gather", [P, TILES, 2], U32)
        slot_scatter = sb("slot_scatter", [P, TILES, 2], U32)
        e_tab = sb("e_tab", [P, GT], I32)
        sm = sb("sm", [P, 16, TILES])
        zeros = sb("zeros", [P, D])
        w_mark = sb("w_mark", [P, E])
        scan_t = sb("scan_t", [P, 2, 4 + TILES, E])
        scan_e = sb("scan_e", [P, 2, 4 + E])
        lg_all = sb("lg_all", [P, TILES, E])

        whole = sb
        attention = ExitStack()

        def sb(name, shape, dt=F32):
            return attention.enter_context(nc.sbuf_tensor(name, shape, dt))[:]

        cos_sb = sb("cos_sb", [P, DH])
        sin_sb = sb("sin_sb", [P, 2, DH // 2])
        hmask = sb("hmask", [P, HG])
        causal_sb = sb("causal_sb", [P, SP])
        sel_sb = sb("sel_sb", [P, 32])
        wqkv_sb = sb("wqkv_sb", [P, CH, 3 * D])
        wout_sb = sb("wout_sb", [P, CH, D])
        wkv_hi = sb("wkv_hi", [P, CH, 2 * D], F32R)
        wkv_lo = sb("wkv_lo", [P, CH, 2 * D], F32R)
        wqqT = sb("wqqT", [P, CH, D], BF16)
        swq_b = sb("swq_b", [P, D])
        bq_b = sb("bq_b", [P, D])
        bv_b = sb("bv_b", [P, D])
        bk_sb = sb("bk_sb", [P, CH])
        ctx_raw = sb("ctx_raw", [P, 2, CH, MC])
        v_sb = sb("v_sb", [P, 2, M // MT, D])
        pr = sb("pr", [P, 2, M])
        oT_sb = sb("oT_sb", [P, PAIRS, P])
        pT = sb("pT", [P, 2, TPC, P])
        a_t1 = sb("a_t1", [P, 2 * D])
        a_t2 = sb("a_t2", [P, 2 * D])
        a_qkT = sb("a_qkT", [P, 4, P])
        a_kbd = sb("a_kbd", [P, 2, CH, HG, SP])
        a_s = sb("a_s", [P, H, SP])
        a_p = a_s[:].rearrange("p h s -> p (h s)")
        a_vb = sb("a_vb", [P, PAIRS, 2, 32])
        a_o = sb("a_o", [P, D])
        a_oT = sb("a_oT", [P, CH, P])
        a_y = sb("a_y", [P, D])
        a_x1 = sb("a_x1", [P, D])
        a_q1 = sb("a_q1", [P, D])
        a_pT = a_kbd[:, 0].rearrange("p c h s -> p (c h s)").rearrange("p (r n) -> p r n", r=PAIRS)
        ctx_hi = sb("ctx_hi", [P, 2, CH, MC], F32R)
        ctx_lo = sb("ctx_lo", [P, 2, CH, MC], F32R)
        k_two = sb("k_two", [P, CH, 2, MC], F16)
        k_st = sb("k_st", [KS, 2, PAIRS, M], F16)
        q_st = sb("q_st", [KS, PAIRS, P], F16)
        qbd = sb("qbd", [KS, 2, PAIRS, 2, SP], F16)
        pmask = sb("pmask", [KS, 2])
        a_q3 = a_s[:].rearrange("p h s -> p (h s)")[:, 0:PAIRS * KS].rearrange("p (r i d) -> p r i d", r=PAIRS, i=3)
        a_x = sb("a_x", [P, D])
        a_xT = sb("a_xT", [P, CH, P])
        a_xq = sb("a_xq", [P, D], BF16)
        a_xqT = sb("a_xqT", [P, CH, P], BF16)
        a_mx = sb("a_mx", [P, H])
        a_rs = sb("a_rs", [P, H])
        a_sum = sb("a_sum", [P, H])
        a_st = sb("a_st", [P, 6])
        a_mv = sb("a_mv", [P, 2])
        a_ve = sb("a_ve", [P, 1])
        a_pace = sb("a_pace", [P, 1])
        a_rstd = sb("a_rstd", [P, 1])
        a_am = sb("a_am", [P, 1])
        a_sx = sb("a_sx", [P, 1])
        a_rsx = sb("a_rsx", [P, 1])
        negmax = sb("negmax", [P, 2])
        sumexp = sb("sumexp", [P, 2, PAIRS])
        rsum = sb("rsum", [P, 2, PAIRS])
        b_am = sb("b_am", [P, 1])
        b_s = sb("b_s", [P, 1])
        b_rs = sb("b_rs", [P, 1])
        b_st = sb("b_st", [P, 6])
        b_mv = sb("b_mv", [P, 2])
        b_ve = sb("b_ve", [P, 1])
        b_rstd = sb("b_rstd", [P, 1])
        b_pace = sb("b_pace", [P, 1])
        b_q, b_oq, b_y, b_x2 = a_q1, a_xq, a_y, a_x1
        b_x2T = a_t2[:, 0:D].rearrange("p (c n) -> p c n", c=CH)
        b_oqT = a_t2[:, D:D + P].bitcast(BF16).rearrange("p (c n) -> p c n", c=CH)
        wkv_raw = pr[:].rearrange("p a b -> p (a b)")[:, 0:CH * 2 * D].rearrange("p (c n) -> p c n", c=CH)
        spare = v_sb[:, 1].rearrange("p b c -> p (b c)")
        w_nat = [spare[:, 512 * n:512 * n + 512].rearrange("p (c n) -> p c n", c=CH) for n in (0, 1)]
        w_t = [spare[:, 512 * n:512 * n + 512].rearrange("p (c n) -> p c n", c=CH) for n in (2, 3)]
        w_int = [spare[:, 256 * n:256 * n + 256].bitcast(BF16).rearrange("p (c n) -> p c n", c=CH) for n in (8, 9)]
        w_diag = [spare[:, 256 * n:256 * n + 256].rearrange("p (c n) -> p c n", c=CH) for n in (10, 11)]
        before32 = pr[:].rearrange("p a b -> p (a b)")[:, CH * 2 * D:CH * 2 * D + P]
        w_am = sm[:, 0:CH, 0:2]
        w_s = sm[:, CH:2 * CH, 0:2]
        w_rs = sm[:, 2 * CH:3 * CH, 0:2]

        attention.close()
        sb = whole
        w1_sb = sb("w1_sb", [P, E, CH, F])
        w2_sb = sb("w2_sb", [P, E, FT, D])
        hT = sb("hT", [P, FT, P])
        sm8 = sb("sm8", [P, 16, TILES, E])
        e_cmp = sb("e_cmp", [P, GT, E])
        e_sum = sb("e_sum", [P, GT])
        oh16 = sb("oh16", [P, TILES, E], BF16)
        idx8 = sb("idx8", [P, TILES, E], U32)
        st8 = sb("st8", [P, TILES, 6])
        mv8 = sb("mv8", [P, TILES, 2])
        xg = sb("xg", [P, D])
        xgT = sb("xgT", [P, CH, P])
        b1_row = sb("b1_row", [P, F])
        b2_row = sb("b2_row", [P, D])
        hb = sb("hb", [P, F])
        hg = sb("hg", [P, F])
        y_sb = sb("y_sb", [P, D])
        got = w1_sb[:, 0:2].rearrange("p e c f -> p (e c f)").rearrange("p (k t n) -> p k t n", k=2, t=TILES)

        kv_in = sem("kv_in")
        dec_in = sem("dec_in")
        small_in = sem("small_in")
        x_in = sem("x_in")
        ctx_in = [sem(f"ctx_in{k}") for k in range(2)]
        out_done = sem("out_done")
        set_dve = sem("set_dve")
        set_pe = sem("set_pe")
        set_act = sem("set_act")
        set_pool = sem("set_pool")
        ctx_hi_done = sem("ctx_hi_done")
        ctx_lo_done = sem("ctx_lo_done")
        unit_done = sem("unit_done")
        k_hi_done = sem("k_hi_done")
        unit_out = sem("unit_out")
        s_done = sem("s_done")
        max_done = sem("max_done")
        exp_done = sem("exp_done")
        tr_done = sem("tr_done")
        pT_outer = sem("pT_outer")
        pT_inner = sem("pT_inner")
        pv_done = sem("pv_done")
        rsum_done = sem("rsum_done")
        oT_done = sem("oT_done")
        o_back_done = sem("o_back_done")
        o_done = sem("o_done")
        k_out = [sem(f"k_out{g}") for g in range(CH)]
        k_in = [sem(f"k_in{g}") for g in range(CH)]
        qbd_done = sem("qbd_done")
        a_qk_done = sem("a_qk_done")
        a_rope_mul = sem("a_rope_mul")
        a_rope = sem("a_rope")
        a_v_done = sem("a_v_done")
        a_vb_done = sem("a_vb_done")
        a_tqk_done = sem("a_tqk_done")
        a_qkT_done = sem("a_qkT_done")
        a_kbd_done = sem("a_kbd_done")
        a_s_done = sem("a_s_done")
        a_masked = sem("a_masked")
        a_max_done = sem("a_max_done")
        a_sub_done = sem("a_sub_done")
        a_exp_done = sem("a_exp_done")
        a_sum_done = sem("a_sum_done")
        a_rs_done = sem("a_rs_done")
        a_tp_done = sem("a_tp_done")
        a_pT_done = sem("a_pT_done")
        a_pv_done = sem("a_pv_done")
        a_o_done = sem("a_o_done")
        a_to_done = sem("a_to_done")
        a_oT_done = sem("a_oT_done")
        a_out_done = sem("a_out_done")
        a_y_done = sem("a_y_done")
        a_ln = sem("a_ln")
        a_rstd_done = sem("a_rstd_done")
        a_x1_done = sem("a_x1_done")
        a_x1_kept = sem("a_x1_kept")
        a_quant = sem("a_quant")
        a_xq_done = sem("a_xq_done")
        a_txq_done = sem("a_txq_done")
        a_xqT_done = sem("a_xqT_done")
        a_qp_done = sem("a_qp_done")
        a_q1_done = sem("a_q1_done")
        a_q_done = sem("a_q_done")
        a_tq_done = sem("a_tq_done")
        a_qhi_done = sem("a_qhi_done")
        a_qlo_done = sem("a_qlo_done")
        b_grid = sem("b_grid")
        b_oq_done = sem("b_oq_done")
        b_toq_done = sem("b_toq_done")
        b_oqT_done = sem("b_oqT_done")
        b_p_done = sem("b_p_done")
        b_sum = sem("b_sum")
        b_ln = sem("b_ln")
        b_rstd_done = sem("b_rstd_done")
        b_x2_done = sem("b_x2_done")
        b_x2_kept = sem("b_x2_kept")
        b_tx2_done = sem("b_tx2_done")
        b_x2T_done = sem("b_x2T_done")
        b_gate_done = sem("b_gate_done")
        b_lg_done = sem("b_lg_done")
        p_dve = sem("p_dve")
        p_pe = sem("p_pe")
        p_act = sem("p_act")
        w_in = [sem(f"w_in{e}") for e in range(E)]
        w_late = [sem(f"w_late{e}") for e in range(E)]
        w_ready = sem("w_ready")
        zeroed = sem("zeroed")
        scattered = sem("scattered")
        xg_in = sem("xg_in")
        b1_in = sem("b1_in")
        b2_in = sem("b2_in")
        y_out = sem("y_out")
        tx_done = sem("tx_done")
        xgT_done = sem("xgT_done")
        m1_done = sem("m1_done")
        hb_done = sem("hb_done")
        gelu_done = sem("gelu_done")
        th_done = sem("th_done")
        hT_act = sem("hT_act")
        hT_dve = sem("hT_dve")
        m2_done = sem("m2_done")
        y_ready = sem("y_ready")
        gathered = [sem(f"gathered{t}") for t in range(TILES)]
        f_sum = sem("f_sum")
        f_stat = sem("f_stat")
        f_var = sem("f_var")
        f_rstd = sem("f_rstd")
        f_out = sem("f_out")

        k_dram = nc.dram_tensor("k_dram", (CH, P, 2, MC), F16).ap()
        xs = nc.dram_tensor("xs", (DUMP + 2 * TILES * P, D), F32).ap()
        ys = nc.dram_tensor("ys", (GT * P, D), F32).ap()
        xs_tiles = xs[0:DUMP].rearrange("(g p) n -> g p n", p=P)
        ys_tiles = ys.rearrange("(g p) n -> g p n", p=P)

        FOR_KV = [(wkv_raw, w_kv_T), (bk_sb[:], bk_col), (bv_b[:], bv_row)]
        FOR_DEC = [(wqkv_sb[:], w_qkv_T), (cos_sb[:], rope_cos), (sin_sb[:], rope_sin), (id32[:], ident),
                   (hmask[:], head_mask), (pmask[:], pair_mask), (causal_sb[:], causal), (wout_sb[:], w_out_T)]
        SMALL = [(w_nat[0], wq), (w_nat[1], wp), (bq_b[:], bq_row), (bp_b[:], bp_row), (gw_sb[:], gate_w),
                 (gb_b[:], gate_b_row), (sel_sb[:], sel), (before32, before), (valid_sb[:], valid),
                 (dump_sb[:], dump), (iota_t[:], iota_tiles), (iota8[:], iota_row)]

        def unit_slots(slot):
            edges = [0, 2, 4, 6, 8, 10, 11, 11, UNITS]
            us = list(range(edges[slot - 1], edges[slot]))
            return (us[:1], us[1:]) if slot < PAIRS else ([], us)

        B_SLOTS = {1: 0, 3: 1, 4: 2, 7: 3, 8: 4, 9: 5}
        A_AT = {s: s - 1 for s in range(1, 1 + A_STEPS)}

        block = ctx.enter_context(nc.Block())
        at = {}

        @block.vector
        def _(dve):
            V = nc.vector

            def quantise(src, am, s, rs, t1, dst, own, n, rows):
                shape = [P, rows, D]
                V.tensor_reduce(am, src, AX.X, ALU.max, apply_absolute_value=True).then_inc(own, 1)
                dve.wait_ge(own, n + 1)
                V.tensor_scalar(s, am, 1.0 / 127.0, 1e-8, ALU.mult, ALU.max).then_inc(own, 1)
                dve.wait_ge(own, n + 2)
                V.reciprocal(rs, s).then_inc(own, 1)
                dve.wait_ge(own, n + 3)
                V.tensor_tensor(t1, src, rs.unsqueeze(2).to_broadcast(shape), ALU.mult).then_inc(own, 1)
                dve.wait_ge(own, n + 4)
                V.tensor_scalar(t1, t1, ROUND, ROUND - 127.0, ALU.add, ALU.max).then_inc(own, 1)
                dve.wait_ge(own, n + 5)
                V.tensor_scalar(dst, t1, ROUND + 127.0, ROUND, ALU.min, ALU.subtract).then_inc(own, 1)

            V.memset(a_pace[:], 0.0).then_inc(o_done, 1)
            dve.wait_ge(kv_in, 16 * len(FOR_KV))
            V.tensor_copy(wkv_hi[:], wkv_raw).then_inc(set_dve, 1)
            dve.wait_ge(set_dve, 1)
            V.tensor_tensor(wkv_lo[:], wkv_raw, wkv_hi[:].bitcast(F32), ALU.subtract).then_inc(set_dve, 1)

            def weights_to_int8(n):
                quantise(w_nat[n], w_am[:, :, n], w_s[:, :, n], w_rs[:, :, n], w_t[n], w_int[n], set_dve, 2 + 8 * n, CH)
                for c in range(CH):
                    V.tensor_scalar(w_diag[n][:, c], id32[:], w_s[:, c, n:n + 1], None, ALU.mult).then_inc(set_dve, 1)

            def ctx_hi_step(b, j, c, first=False):
                k = (CHUNKS * j + c) % 2
                dve.wait_ge(ctx_in[k], 8 * (CHUNKS * b + c - k) + 16)
                if not first:
                    dve.wait_ge(unit_done, 4 * (CHUNKS * b + c - 1))
                V.tensor_copy(ctx_hi[:, k], ctx_raw[:, k]).then_inc(ctx_hi_done, 1)

            def unit_step(b, par, u):
                c, g = u // 4, u % 4
                dve.wait_ge(unit_done, UNITS * b + u + 1)
                if g < 2:
                    dve.wait_ge(k_hi_done, 2 * (CHUNKS * b + c) + g + 1)
                    V.scalar_tensor_tensor(k_two[:, g, 1], ps[:, BANK_KV, 0:MC], bk_sb[:, g:g + 1], k_two[:, g, 0],
                                           ALU.add, ALU.subtract).then_inc(unit_out, 1)
                else:
                    m = TPC * c + 2 * (g - 2)
                    V.tensor_tensor(v_sb[0:MT, par, m:m + 2], ps[0:MT, BANK_KV].rearrange("p (t n) -> p t n", t=2),
                                    bv_b[0:MT].unsqueeze(1).to_broadcast([MT, 2, D]), ALU.add).then_inc(unit_out, 1)

            def max_step(b, p):
                dve.wait_ge(s_done, PAIRS * b + p + 1)
                V.tensor_reduce(negmax[:, p % 2:p % 2 + 1], ps[:, BANK_S:BANK_S + CHUNKS, 0:MC], AX.XY, ALU.max,
                                negate=True).then_inc(max_done, 1)

            def pT_step(b, p):
                n = (3 * p + 1) % 2
                dve.wait_ge(tr_done, 3 * PAIRS * b + 3 * p + 2)
                V.tensor_copy(pT[0:MT, n], ps[0:MT, BANK_T + n].rearrange("p (t n) -> p t n", t=TPC)).then_inc(pT_inner, 1)

            def o_step(b, par, t):
                dve.wait_ge(exp_done, PAIRS * (b + 1))
                V.reciprocal(rsum[:, par], sumexp[:, par]).then_inc(rsum_done, 1)
                dve.wait_ge(rsum_done, b + 1)
                dve.wait_ge(o_back_done, b + 1)
                for hp in range(2):
                    dst = o_all[SP * par:SP * par + SP, bass.ds(t, 1)].rearrange("p a (r h d) -> p (a r) h d", r=PAIRS, h=2)[:, :, hp]
                    src = ps[SP * hp:SP * hp + SP, BANK_O, 0:D].rearrange("p (r h d) -> p r h d", r=PAIRS, h=2)[:, :, hp]
                    V.tensor_tensor(dst, src, rsum[SP * hp:SP * hp + SP, par].unsqueeze(2).to_broadcast([SP, PAIRS, DH]),
                                    ALU.mult).then_inc(o_done, 1)

            def a_step(k, t):
                if k == 0:
                    dve.wait_ge(a_qk_done, t + 1)
                    qk = ps[:, BANK_A].rearrange("p (h d) -> p h d", d=DH)
                    V.tensor_tensor(a_t1.rearrange("p (h d) -> p h d", d=DH), qk,
                                    cos_sb[:].unsqueeze(1).to_broadcast([P, 2 * H, DH]), ALU.mult).then_inc(a_rope_mul, 1)
                    qk2 = ps[:, BANK_A].rearrange("p (h i e) -> p h i e", i=DH // 2, e=2)
                    t2 = a_t2.rearrange("p (h i e) -> p h i e", i=DH // 2, e=2)
                    for e in range(2):
                        V.tensor_tensor(t2[:, :, :, e], qk2[:, :, :, 1 - e],
                                        sin_sb[:, e].unsqueeze(1).to_broadcast([P, 2 * H, DH // 2]), ALU.mult).then_inc(a_rope_mul, 1)
                    dve.wait_ge(a_rope_mul, 3 * t + 3)
                    V.tensor_tensor(a_t1, a_t1, a_t2, ALU.add).then_inc(a_rope, 1)
                elif k in (3, 4):
                    g = k - 3
                    dve.wait_ge(a_s_done, 2 * t + g + 1)
                    V.tensor_tensor(a_s[:, HG * g:HG * g + HG], ps[:, BANK_A].rearrange("p (h s) -> p h s", h=HG),
                                    causal_sb[:].unsqueeze(1).to_broadcast([P, HG, SP]), ALU.add).then_inc(a_masked, 1)
                    if g == 1:
                        dve.wait_ge(a_masked, 2 * t + 2)
                        V.tensor_reduce(a_mx[:], a_s, AX.X, ALU.max).then_inc(a_max_done, 1)
                        dve.wait_ge(a_max_done, t + 1)
                        V.tensor_tensor(a_s, a_s, a_mx[:].unsqueeze(2).to_broadcast([P, H, SP]), ALU.subtract).then_inc(a_sub_done, 1)
                elif k == 5:
                    dve.wait_ge(a_exp_done, t + 1)
                    V.tensor_reduce(a_sum[:], a_p.rearrange("p (h s) -> p h s", h=H), AX.X, ALU.add).then_inc(a_sum_done, 1)
                    dve.wait_ge(a_sum_done, t + 1)
                    V.reciprocal(a_rs[:], a_sum[:]).then_inc(a_rs_done, 1)
                elif k == 7:
                    dve.wait_ge(a_rs_done, t + 1)
                    dve.wait_ge(a_pv_done, t + 1)
                    for j in range(2):
                        rows = slice(SP * j, SP * j + SP)
                        src = ps[rows, BANK_A].rearrange("p (r j x) -> p r j x", r=PAIRS, j=2)[:, :, j]
                        V.tensor_tensor(a_o[rows].rearrange("p (r h d) -> p r h d", r=PAIRS, h=2),
                                        src.rearrange("p r (h d) -> p r h d", h=2),
                                        a_rs[rows].rearrange("p (r h) -> p r h", h=2).unsqueeze(3).to_broadcast([SP, PAIRS, 2, DH]),
                                        ALU.mult).then_inc(a_o_done, 1)
                elif k == 9:
                    dve.wait_ge(a_out_done, t + 1)
                    V.tensor_tensor(a_y, ps[:, BANK_A, 0:D], a_x[:], ALU.add).then_inc(a_y_done, 1)
                    dve.wait_ge(a_y_done, t + 1)
                    V.bn_stats(a_st[:], a_y).then_inc(a_ln, 1)
                    dve.wait_ge(a_ln, 3 * t + 1)
                    V.memset(a_pace[:], 0.0)
                    V.bn_aggr(a_mv[:], a_st[:]).then_inc(a_ln, 1)
                    dve.wait_ge(a_ln, 3 * t + 2)
                    V.tensor_scalar(a_ve[:], a_mv[:, 1:2], EPS, None, ALU.add).then_inc(a_ln, 1)
                    if not (isinstance(t, int) and t == 0):
                        dve.wait_ge(a_x1_kept, t)
                    dve.wait_ge(a_rstd_done, t + 1)
                    V.tensor_scalar(a_x1, a_y, a_mv[:, 0:1], a_rstd[:], ALU.subtract, ALU.mult).then_inc(a_x1_done, 1)
                elif k == 10:
                    dve.wait_ge(a_x1_done, t + 1)
                    V.tensor_reduce(a_am[:], a_x1, AX.X, ALU.max, apply_absolute_value=True).then_inc(a_quant, 1)
                    dve.wait_ge(a_quant, 5 * t + 1)
                    V.tensor_scalar(a_sx[:], a_am[:], 1.0 / 127.0, 1e-8, ALU.mult, ALU.max).then_inc(a_quant, 1)
                    dve.wait_ge(a_quant, 5 * t + 2)
                    V.reciprocal(a_rsx[:], a_sx[:]).then_inc(a_quant, 1)
                    dve.wait_ge(a_quant, 5 * t + 3)
                    V.tensor_scalar(a_q1, a_x1, a_rsx[:], ROUND, ALU.mult, ALU.add).then_inc(a_quant, 1)
                    dve.wait_ge(a_quant, 5 * t + 4)
                    V.tensor_scalar(a_q1, a_q1, ROUND - 127.0, ROUND + 127.0, ALU.max, ALU.min).then_inc(a_quant, 1)
                    dve.wait_ge(a_quant, 5 * t + 5)
                    V.tensor_scalar(a_xq[:], a_q1, ROUND, None, ALU.subtract).then_inc(a_xq_done, 1)
                elif k == 12:
                    dve.wait_ge(a_qp_done, t + 1)
                    V.scalar_tensor_tensor(a_q1, ps[:, BANK_A, 0:D], a_sx[:], swq_b[:], ALU.mult, ALU.mult).then_inc(a_q1_done, 1)
                    dve.wait_ge(a_q1_done, t + 1)
                    V.tensor_tensor(a_q3, a_q1.rearrange("p (r d) -> p r d", r=PAIRS).unsqueeze(2).to_broadcast([P, PAIRS, 3, PD]),
                                    bq_b[:].rearrange("p (r d) -> p r d", r=PAIRS).unsqueeze(2).to_broadcast([P, PAIRS, 3, PD]),
                                    ALU.add).then_inc(a_q_done, 1)
                elif k in (13, 14):
                    h = k - 13
                    dve.wait_ge(a_qhi_done, 2 * t + h + 1)
                    low = q_st[2 * PD:KS, 4 * h:4 * h + 4]
                    V.tensor_tensor(low, ps[2 * PD:KS, BANK_A].rearrange("p (r n) -> p r n", r=4), low,
                                    ALU.subtract).then_inc(a_qlo_done, 1)

            def kbd_part(j):
                dve.wait_ge(a_qkT_done, 1)
                for g in range(CH):
                    V.tensor_tensor(a_kbd[:, j, g], a_qkT[:, CH + g, SP * j:SP * j + SP].unsqueeze(1).to_broadcast([P, HG, SP]),
                                    hmask[:].unsqueeze(2).to_broadcast([P, HG, SP]), ALU.mult).then_inc(a_kbd_done, 1)

            def b_step(k, t):
                if k == 2:
                    dve.wait_ge(b_p_done, t + 1)
                    V.scalar_tensor_tensor(b_y, ps[:, BANK_A, 0:D], b_s[:], swp_b[:], ALU.mult, ALU.mult).then_inc(b_sum, 1)
                elif k == 5:
                    dve.wait_ge(b_gate_done, t + 1)
                    V.tensor_tensor(lg_all[:, bass.ds(t, 1)].rearrange("p a e -> p (a e)"), ps[:, BANK_A, 0:E], gb_b[:],
                                    ALU.add).then_inc(b_lg_done, 1)
                    dve.wait_ge(b_x2_kept, t + 1)

            def b_tail(k, t):
                if k == 0:
                    dve.wait_ge(o_done, 1 + 4 * (t + 1))
                    o = o_all[:, bass.ds(t, 1)].rearrange("p a n -> p (a n)")
                    V.tensor_reduce(b_am[:], o, AX.X, ALU.max, apply_absolute_value=True).then_inc(b_grid, 1)
                    dve.wait_ge(b_grid, 5 * t + 1)
                    V.tensor_scalar(b_s[:], b_am[:], 1.0 / 127.0, 1e-8, ALU.mult, ALU.max).then_inc(b_grid, 1)
                    dve.wait_ge(b_grid, 5 * t + 2)
                    V.reciprocal(b_rs[:], b_s[:]).then_inc(b_grid, 1)
                    dve.wait_ge(b_grid, 5 * t + 3)
                    V.tensor_scalar(b_q, o, b_rs[:], ROUND, ALU.mult, ALU.add).then_inc(b_grid, 1)
                    dve.wait_ge(b_grid, 5 * t + 4)
                    V.tensor_scalar(b_q, b_q, ROUND - 127.0, ROUND + 127.0, ALU.max, ALU.min).then_inc(b_grid, 1)
                    dve.wait_ge(b_grid, 5 * t + 5)
                    V.tensor_scalar(b_oq[:], b_q, ROUND, None, ALU.subtract).then_inc(b_oq_done, 1)
                elif k == 2:
                    dve.wait_ge(b_sum, 3 * t + 1)
                    V.tensor_tensor(b_y, b_y, bp_b[:], ALU.add).then_inc(b_sum, 1)
                    dve.wait_ge(b_sum, 3 * t + 2)
                    V.tensor_tensor(b_y, b_y, x1_all[:, bass.ds(t, 1)].rearrange("p a n -> p (a n)"), ALU.add).then_inc(b_sum, 1)
                    dve.wait_ge(b_sum, 3 * t + 3)
                    V.bn_stats(b_st[:], b_y).then_inc(b_ln, 1)
                    dve.wait_ge(b_ln, 3 * t + 1)
                    V.memset(b_pace[:], 0.0)
                    V.bn_aggr(b_mv[:], b_st[:]).then_inc(b_ln, 1)
                    dve.wait_ge(b_ln, 3 * t + 2)
                    V.tensor_scalar(b_ve[:], b_mv[:, 1:2], EPS, None, ALU.add).then_inc(b_ln, 1)
                elif k == 3:
                    dve.wait_ge(b_rstd_done, t + 1)
                    V.tensor_scalar(b_x2, b_y, b_mv[:, 0:1], b_rstd[:], ALU.subtract, ALU.mult).then_inc(b_x2_done, 1)

            def unit_steps(b, j, us, ctx_on):
                for u in us:
                    unit_step(b, j, u)
                    if u % 4 == 3:
                        c = u // 4
                        if c == 0:
                            ctx_hi_step(b, j, 2)
                        elif ctx_on:
                            ctx_hi_step(b + 1, 1 - j, c - 1)

            def batch(b, j, t, t_next, units_on, t_before):
                ctx_on = t_next is not None
                for slot in range(1, PAIRS + 1):
                    early, late = unit_slots(slot) if units_on else ([], [])
                    if slot < PAIRS:
                        max_step(b, slot)
                    elif units_on:
                        max_step(b + 1, 0)
                    pT_step(b, slot - 1)
                    bk = B_SLOTS.get(PAIRS * j + slot, -1)
                    if t_before is not None:
                        b_step(bk, t_before)
                    unit_steps(b + 1, 1 - j, early, ctx_on)
                    if t_next is not None:
                        a_step(A_AT.get(PAIRS * j + slot, -1), t_next)
                    if t_before is not None:
                        b_tail(bk, t_before)
                    unit_steps(b + 1, 1 - j, late, ctx_on)
                o_step(b, j, t)

            ctx_hi_step(0, 0, 0, True)
            dve.wait_ge(ctx_hi_done, 1)
            V.tensor_tensor(ctx_lo[:, 0], ctx_raw[:, 0], ctx_hi[:, 0].bitcast(F32), ALU.subtract).then_inc(ctx_lo_done, 1)
            ctx_hi_step(0, 0, 1, True)
            dve.wait_ge(dec_in, 16 * len(FOR_DEC))
            for k in range(A_STEPS):
                if k < UNITS:
                    unit_steps(0, 0, [k], True)
                a_step(k, 0)
                if k == 2:
                    kbd_part(0)
                elif k == 3:
                    dve.wait_ge(small_in, 16 * len(SMALL))
                    weights_to_int8(0)
                elif k == 5:
                    weights_to_int8(1)
                elif k == 7:
                    dve.wait_ge(set_dve, 18)
                    dve.wait_ge(set_act, 4)
                    dve.wait_ge(set_pool, 9)
                    V.tensor_scalar(swq_b[:], swq_b[:], DH ** -0.5, None, ALU.mult).then_inc(set_dve, 1)
                    V.tensor_scalar(bq_b[:], bq_b[:], DH ** -0.5, None, ALU.mult).then_inc(set_dve, 1)
                    dve.wait_ge(set_dve, 20)
            max_step(0, 0)
            batch(0, 0, 0, 1, True, None)
            batch(1, 1, 0, 1, True, None)
            with dve.Fori(1, TILES - 1) as it:
                batch(2 * it, 0, it, it + 1, True, it - 1)
                batch(2 * it + 1, 1, it, it + 1, True, it - 1)
            batch(B - 2, 0, TILES - 1, None, True, TILES - 2)
            batch(B - 1, 1, TILES - 1, None, False, TILES - 2)
            for k in range(6):
                b_step(k, TILES - 1)
                b_tail(k, TILES - 1)

            n = [0]

            def own(ins):
                ins.then_inc(p_dve, 1)
                n[0] += 1

            def settle():
                dve.wait_ge(p_dve, n[0])

            dve.wait_ge(b_lg_done, TILES)
            lg, top, sel1, sel2, slots = lg_all, sm8[:, 1], sm8[:, 3], sm8[:, 4], sm8[:, 5]
            for t in range(TILES):
                own(V.max(top[:, t], lg[:, t]))
            settle()
            for t in range(TILES):
                own(V.max_index(idx8[:, t], top[:, t], lg[:, t]))
            own(V.tensor_tensor(sm[:, 7], top[:, :, 1], top[:, :, 0], ALU.subtract))
            at["gaps"] = n[0]
            settle()
            own(V.tensor_copy(sm8[:, 2], idx8[:]))
            settle()
            for i, dst in enumerate((sel1, sel2)):
                own(V.tensor_tensor(dst, iota8[:].unsqueeze(1).to_broadcast([P, TILES, E]),
                                    sm8[:, 2, :, i:i + 1].to_broadcast([P, TILES, E]), ALU.is_equal))
            settle()
            for dst in (sel1, sel2):
                own(V.tensor_scalar(dst, dst, valid_sb[:], None, ALU.mult))
            settle()
            own(V.tensor_tensor(oh16[:], sel1, sel2, ALU.add))
            at["choices"] = n[0]
            dve.wait_ge(p_act, 1)
            own(V.tensor_scalar(sm[:, 10], sm[:, 8], 1.0, None, ALU.add))
            settle()
            own(V.reciprocal(comb[:, 0], sm[:, 10]))
            settle()
            own(V.tensor_tensor(comb[:, 1], sm[:, 8], comb[:, 0], ALU.mult))
            dve.wait_ge(p_pe, 2)
            tot = ps[:, 6, 0:TILES * E].rearrange("p (t e) -> p t e", e=E)
            rank = ps[:, 5, 0:TILES * E].rearrange("p (t e) -> p t e", e=E)
            own(V.tensor_copy(scan_t[:, 0, 4:], tot))
            settle()
            for i, step in enumerate((1, 2, 4)):
                own(V.tensor_tensor(scan_t[:, (i + 1) % 2, 4:], scan_t[:, i % 2, 4:], scan_t[:, i % 2, 4 - step:4 + TILES - step], ALU.add))
                settle()
            cum = scan_t[:, 1, 3:3 + TILES]
            count = scan_t[:, 1, 3 + TILES]
            tiles, first = sm8[:, 8, 0], sm8[:, 8, 1]
            own(V.tensor_scalar(tiles, count, 1.0 / P, (P - 1.0) / P - 0.5 + 0.5 / P, ALU.mult, ALU.add))
            settle()
            tiles = scan_e[:, 0, 4:]
            own(V.tensor_scalar(tiles, sm8[:, 8, 0], ROUND, ROUND, ALU.add, ALU.subtract))
            settle()
            own(V.tensor_copy(sm8[:, 8, 0], tiles))
            for i, step in enumerate((1, 2, 4)):
                own(V.tensor_tensor(scan_e[:, (i + 1) % 2, 4:], scan_e[:, i % 2, 4:], scan_e[:, i % 2, 4 - step:4 + E - step], ALU.add))
                settle()
            tiles, ends = sm8[:, 8, 0], scan_e[:, 1, 4:]
            own(V.tensor_tensor(first, ends, tiles, ALU.subtract))
            own(V.tensor_tensor(e_cmp[:], iota_t[:].unsqueeze(2).to_broadcast([P, GT, E]),
                                ends.unsqueeze(1).to_broadcast([P, GT, E]), ALU.is_ge))
            settle()
            own(V.tensor_reduce(e_sum[:], e_cmp[:], AX.X, ALU.add))
            own(V.tensor_scalar(first, first, float(P), None, ALU.mult))
            settle()
            own(V.tensor_scalar(e_tab[:], e_sum[:], E - 1.0, None, ALU.min))
            at["tiles known"] = n[0]
            own(V.tensor_tensor(slots, rank, cum, ALU.add))
            settle()
            own(V.tensor_tensor(slots, slots, first.unsqueeze(1).to_broadcast([P, TILES, E]), ALU.add))
            settle()
            for i, dst in enumerate((sel1, sel2)):
                own(V.tensor_tensor(dst, dst, slots, ALU.mult))
            settle()
            slot_f = sm8[:, 9].rearrange("p t e -> p (t e)")[:, 0:2 * TILES].rearrange("p (t k) -> p t k", k=2)
            for i, src in enumerate((sel1, sel2)):
                own(V.tensor_reduce(slot_f[:, :, i], src, AX.X, ALU.add))
            settle()
            own(V.tensor_tensor(slot_scatter[:], slot_f, dump_sb[:], ALU.add))
            at["slots"] = n[0]
            own(V.tensor_copy(slot_gather[:], slot_f))

            def bias_step(g, first=False):
                for i in range(2):
                    dve.wait_ge(m1_done, 2 * g + i + 1)
                    if i == 0:
                        dve.wait_ge(b1_in, 16 * (g + 1))
                        if not first:
                            dve.wait_ge(gelu_done, g)
                    V.tensor_tensor(hb[:, 512 * i:512 * i + 512], ps[:, H_BANK + i], b1_row[:, 512 * i:512 * i + 512],
                                    ALU.add).then_inc(hb_done, 1)

            def around(g, left=GT, first=False):
                dve.wait_ge(th_done, 2 * g + 2)
                V.tensor_copy(hT[:, 4:8], ps[:, TH_BANK + 1].rearrange("p (f n) -> p f n", f=4)).then_inc(hT_dve, 1)
                if left > 1:
                    bias_step(g + 1)
                dve.wait_ge(m2_done, g + 1)
                dve.wait_ge(b2_in, 16 * (g + 1))
                if not first:
                    dve.wait_ge(y_out, 16 * g)
                V.tensor_tensor(y_sb[:], ps[:, Y_BANK, 0:D], b2_row[:], ALU.add).then_inc(y_ready, 1)

            bias_step(0, True)
            around(0, first=True)
            with dve.Fori(1, GT - 3) as g:
                around(g)
            for left in (3, 2, 1):
                around(GT - left, left)

            def normalise(t):
                dve.wait_ge(f_rstd, t + 1)
                V.tensor_scalar(o_all[:, t], acc[:, t], mv8[:, t, 0:1], sm[:, 5, t:t + 1],
                                ALU.subtract, ALU.mult).then_inc(f_out, 1)

            for t in range(TILES):
                dve.wait_ge(gathered[t], 32)
                for k in range(2):
                    V.scalar_tensor_tensor(acc[:, t], got[:, k, t], comb[:, k, t:t + 1], acc[:, t], ALU.mult, ALU.add).then_inc(f_sum, 1)
                    dve.wait_ge(f_sum, 2 * t + k + 1)
                V.bn_stats(st8[:, t], acc[:, t]).then_inc(f_stat, 1)
                dve.wait_ge(f_stat, 2 * t + 1)
                V.bn_aggr(mv8[:, t], st8[:, t]).then_inc(f_stat, 1)
                dve.wait_ge(f_stat, 2 * t + 2)
                V.tensor_scalar(sm[:, 4, t:t + 1], mv8[:, t, 1:2], EPS, None, ALU.add).then_inc(f_var, 1)
                if t >= 3:
                    normalise(t - 3)
            for t in range(TILES - 3, TILES):
                normalise(t)

        @block.sync
        def _(sp):
            for dst, src in FOR_KV:
                sp.dma_start(dst, src[:]).then_inc(kv_in, 16)

            def load_x(t, first=False):
                if not first:
                    sp.wait_ge(a_y_done, t)
                sp.dma_start(a_x[:], x_tok[bass.ds(t, 1)].rearrange("a p n -> (a p) n")).then_inc(x_in, 16)
                sp.dma_start(a_xT[:], x_T[bass.ds(t, 1)].rearrange("a p c n -> (a p) c n")).then_inc(x_in, 16)

            def load_ctx(b, j, c, first=False):
                if not first:
                    sp.wait_ge(ctx_lo_done, CHUNKS * b + c - 1)
                sp.dma_start(ctx_raw[:, (CHUNKS * j + c) % 2], ctx_T[bass.ds(b, 1), c].rearrange("a p c n -> (a p) c n")).then_inc(ctx_in[(CHUNKS * j + c) % 2], 16)

            def k_chunk(b, par, c, ctx_next):
                for g in range(CH):
                    sp.wait_ge(unit_out, UNITS * b + 4 * c + g + 1)
                    sp.dma_start(k_dram[g], k_two[:, g]).then_inc(k_out[g], 16)
                    sp.wait_ge(k_out[g], 16 * (CHUNKS * b + c + 1))
                    for i, part in enumerate((0, 1, 0)):
                        sp.dma_start(k_st[PD * i:PD * i + PD, par, 4 * g:4 * g + 4, MC * c:MC * c + MC],
                                     k_dram[g, :, part].rearrange("(r d) n -> d r n", r=4)).then_inc(k_in[g], 16)
                    if g == 0 and ctx_next is not None:
                        load_ctx(ctx_next[0], ctx_next[1], c)

            load_ctx(0, 0, 0, True)
            load_x(0, True)
            for dst, src in FOR_DEC:
                sp.dma_start(dst, src[:]).then_inc(dec_in, 16)
            load_ctx(0, 0, 1, True)
            for dst, src in SMALL:
                sp.dma_start(dst, src[:]).then_inc(small_in, 16)
            load_ctx(0, 0, 2)
            k_chunk(0, 0, 0, (1, 1))
            sp.wait_ge(set_pool, 5)
            sp.dma_start(xs_tiles.rearrange("g p n -> p g n"), zeros[:].unsqueeze(1).to_broadcast([P, GT, D])).then_inc(zeroed, 16)
            k_chunk(0, 0, 1, (1, 1))
            k_chunk(0, 0, 2, (1, 1))
            with sp.Fori(0, TILES - 1) as it:
                load_x(it + 1)
                for j in range(2):
                    for c in range(CHUNKS):
                        k_chunk(2 * it + 1 + j, 1 - j, c, (2 * it + 2 + j, j))
            for c in range(CHUNKS):
                k_chunk(B - 1, 1, c, None)

            sp.wait_ge(o_done, 1 + 2 * B)
            for e in range(EARLY_W1):
                sp.dma_start(w1_sb[:, e], w1[e]).then_inc(w_in[e], 16)
            sp.wait_ge(b_lg_done, TILES)
            sp.wait_ge(b_x2_kept, TILES)
            for e in range(EARLY_W2):
                sp.dma_start(w2_sb[:, e], w2[e]).then_inc(w_in[e], 16)

            def load_xg(g):
                sp.dma_start(xg[:], xs_tiles[bass.ds(g, 1)].rearrange("a p n -> (a p) n")).then_inc(xg_in, 16)

            def load_b1(g):
                e = sp.value_load(e_tab[0:1, bass.ds(g, 1)], min_val=0, max_val=E - 1)
                sp.dma_start(b1_row[:], b1[bass.ds(e, 1)].to_broadcast([P, F])).then_inc(b1_in, 16)

            def load_b2(g):
                e = sp.value_load(e_tab[0:1, bass.ds(g, 1)], min_val=0, max_val=E - 1)
                sp.dma_start(b2_row[:], b2[bass.ds(e, 1)].to_broadcast([P, D])).then_inc(b2_in, 16)

            sp.wait_ge(p_dve, at["tiles known"])
            load_b1(0)
            load_b2(0)
            sp.wait_ge(scattered, 16 * 2 * TILES)
            load_xg(0)
            sp.wait_ge(tx_done, 1)
            load_xg(1)
            sp.wait_ge(hb_done, 2)
            load_b1(1)
            sp.wait_ge(tx_done, 2)
            load_xg(2)

            def around(g, left=GT):
                if left > 2:
                    sp.wait_ge(hb_done, 2 * g + 4)
                    load_b1(g + 2)
                if left > 3:
                    sp.wait_ge(tx_done, g + 3)
                    load_xg(g + 3)
                sp.wait_ge(y_ready, g + 1)
                sp.dma_start(ys_tiles[bass.ds(g, 1)].rearrange("a p n -> (a p) n"), y_sb[:]).then_inc(y_out, 16)
                if left > 1:
                    load_b2(g + 1)

            with sp.Fori(0, GT - 3) as g:
                around(g)
            for left in (3, 2, 1):
                around(GT - left, left)

            for t in range(TILES):
                sp.wait_ge(f_out, t + 1)
                for j in range(2):
                    sp.dma_start(out[2 * t + j], o_all[SP * j:SP * j + S, t]).then_inc(out_done, 16)
            sp.wait_ge(out_done, 16 * B)

        @block.gpsimd
        def _(pool):
            nc.gpsimd.memset(ones[:], 1.0).then_inc(set_pool, 1)
            nc.gpsimd.memset(neg_half[:], -0.5).then_inc(set_pool, 1)
            nc.gpsimd.memset(a_vb[:], 0.0).then_inc(set_pool, 1)
            nc.gpsimd.memset(ones16[:], 1.0).then_inc(set_pool, 1)
            nc.gpsimd.memset(zeros[:], 0.0).then_inc(set_pool, 1)
            nc.gpsimd.memset(scan_t[:, :, 0:4], 0.0).then_inc(set_pool, 1)
            nc.gpsimd.memset(scan_e[:, :, 0:4], 0.0).then_inc(set_pool, 1)

            def ctx_lo_step(b, j, c, first=False):
                if not first:
                    pool.wait_ge(unit_done, 4 * (CHUNKS * b + c - 1))
                k = (CHUNKS * j + c) % 2
                pool.wait_ge(ctx_hi_done, CHUNKS * b + c + 1)
                nc.gpsimd.tensor_tensor(ctx_lo[:, k], ctx_raw[:, k], ctx_hi[:, k].bitcast(F32),
                                        ALU.subtract).then_inc(ctx_lo_done, 1)

            def kbd_step(t, batches=(0, 1)):
                pool.wait_ge(a_qkT_done, t + 1)
                for j in batches:
                    for g in range(CH):
                        nc.gpsimd.tensor_tensor(
                            a_kbd[:, j, g],
                            a_qkT[:, CH + g, SP * j:SP * j + SP].unsqueeze(1).to_broadcast([P, HG, SP]),
                            hmask[:].unsqueeze(2).to_broadcast([P, HG, SP]), ALU.mult).then_inc(a_kbd_done, 1)

            def rstd_step(t):
                pool.wait_ge(a_ln, 3 * t + 3)
                nc.gpsimd.tensor_tensor(a_rstd[:], a_ve[:], neg_half[:, 0:1], ALU.pow).then_inc(a_rstd_done, 1)

            def b_rstd_step(t):
                pool.wait_ge(b_ln, 3 * t + 3)
                nc.gpsimd.tensor_tensor(b_rstd[:], b_ve[:], neg_half[:, 0:1], ALU.pow).then_inc(b_rstd_done, 1)

            def qbd_step(t, j, h, first=False):
                if j == 0:
                    pool.wait_ge(a_qlo_done, 2 * t + h + 1)
                if not first and h == 0:
                    pool.wait_ge(s_done, PAIRS * (2 * t + j - 1))
                nc.gpsimd.tensor_tensor(
                    qbd[:, j, 4 * h:4 * h + 4],
                    q_st[:, 4 * h:4 * h + 4, SP * j:SP * j + SP].unsqueeze(2).to_broadcast([KS, 4, 2, SP]),
                    pmask[:].unsqueeze(1).unsqueeze(3).to_broadcast([KS, 4, 2, SP]), ALU.mult).then_inc(qbd_done, 1)

            ctx_lo_step(0, 0, 1, True)
            pool.wait_ge(dec_in, 16 * len(FOR_DEC))
            nc.gpsimd.tensor_copy(id16[:], id32[:]).then_inc(set_pool, 1)
            kbd_step(0, (1,))
            pool.wait_ge(small_in, 16 * len(SMALL))
            nc.gpsimd.tensor_copy(before16[:], before32).then_inc(set_pool, 1)
            ctx_lo_step(0, 0, 2)
            ctx_lo_step(1, 1, 0)
            rstd_step(0)
            for j in range(2):
                for h in range(2):
                    qbd_step(0, j, h, True)
            def iteration(it, t_before):
                ctx_lo_step(2 * it + 1, 1, 1)
                kbd_step(it + 1)
                ctx_lo_step(2 * it + 1, 1, 2)
                if t_before is not None:
                    b_rstd_step(t_before)
                ctx_lo_step(2 * it + 2, 0, 0)
                ctx_lo_step(2 * it + 2, 0, 1)
                rstd_step(it + 1)
                ctx_lo_step(2 * it + 2, 0, 2)
                ctx_lo_step(2 * it + 3, 1, 0)
                for j in range(2):
                    for h in range(2):
                        qbd_step(it + 1, j, h)

            iteration(0, None)
            with pool.Fori(1, TILES - 1) as it:
                iteration(it, it - 1)
            ctx_lo_step(B - 1, 1, 1)
            ctx_lo_step(B - 1, 1, 2)
            b_rstd_step(TILES - 2)
            b_rstd_step(TILES - 1)

            pool.wait_ge(zeroed, 16)
            pool.wait_ge(p_dve, at["slots"])
            for t in range(TILES):
                for k in range(2):
                    nc.gpsimd.indirect_dma_start(
                        out=xs, out_offset=bass.IndirectOffsetOnAxis(ap=slot_scatter[:, t, k:k + 1], axis=0),
                        in_=acc[:, t], in_offset=None).then_inc(scattered, 16)
            for e in range(E):
                ahead = e + 1
                if EARLY_W2 <= ahead < E:
                    if ahead >= EARLY_W1:
                        nc.gpsimd.dma_start(w1_sb[:, ahead], w1[ahead]).then_inc(w_late[ahead], 16)
                    nc.gpsimd.dma_start(w2_sb[:, ahead], w2[ahead]).then_inc(w_late[ahead], 16)
                early = (e < EARLY_W1) + (e < EARLY_W2)
                if early:
                    pool.wait_ge(w_in[e], 16 * early)
                if early < 2:
                    pool.wait_ge(w_late[e], 16 * (2 - early))
                nc.gpsimd.memset(w_mark[:, e:e + 1], 0.0).then_inc(w_ready, 1)
            pool.wait_ge(y_out, 16 * GT)
            def last_rstd(t):
                pool.wait_ge(f_var, t + 1)
                nc.gpsimd.tensor_tensor(sm[:, 5, t:t + 1], sm[:, 4, t:t + 1], neg_half[:, 0:1], ALU.pow).then_inc(f_rstd, 1)

            for t in range(TILES):
                for k in range(2):
                    nc.gpsimd.indirect_dma_start(
                        out=got[:, k, t], out_offset=None, in_=ys,
                        in_offset=bass.IndirectOffsetOnAxis(ap=slot_gather[:, t, k:k + 1], axis=0)).then_inc(gathered[t], 16)
                if t >= 3:
                    last_rstd(t - 3)
            for t in range(TILES - 3, TILES):
                last_rstd(t)

        @block.scalar
        def _(act):
            def copy(dst, src):
                return nc.scalar.copy(dst, src)

            def weights_step(n):
                act.wait_ge(set_pe, 2 * n + 1)
                copy((wqqT, wpqT)[n][:], ps[:, BANK_S + n].bitcast(BF16)[:, 0:CH * D].rearrange("p (c n) -> p c n", c=CH)).then_inc(set_act, 1)
                act.wait_ge(set_pe, 2 * n + 2)
                copy((swq_b, swp_b)[n][:], ps[:, BANK_T + n, 0:D]).then_inc(set_act, 1)

            def k_hi_step(b, u):
                c, g = u // 4, u % 4
                if not (isinstance(b, int) and b == 0 and c == 0):
                    act.wait_ge(k_in[g], 48 * (CHUNKS * b + c))
                act.wait_ge(unit_done, UNITS * b + u + 1)
                nc.scalar.activation(k_two[:, g, 0], ps[:, BANK_KV, 0:MC], ACT.Identity,
                                     bias=bk_sb[:, g:g + 1]).then_inc(k_hi_done, 1)

            def units(b_next, par, us):
                for u in us:
                    if u % 4 < 2:
                        k_hi_step(b_next, u)

            def exp_step(b, par, p):
                act.wait_ge(max_done, PAIRS * b + p + 1)
                nc.scalar.activation(pr[:, p % 2].rearrange("p (c n) -> p c n", c=CHUNKS), ps[:, BANK_S:BANK_S + CHUNKS, 0:MC],
                                     ACT.Exp, bias=negmax[:, p % 2:p % 2 + 1],
                                     accum_out=sumexp[:, par, p:p + 1]).then_inc(exp_done, 1)

            def pT_step(b, p, q):
                n = (3 * p + q) % 2
                act.wait_ge(tr_done, 3 * PAIRS * b + 3 * p + q + 1)
                copy(pT[0:MT, n], ps[0:MT, BANK_T + n].rearrange("p (t n) -> p t n", t=TPC)).then_inc(pT_outer, 1)

            def oT_step(b, half):
                act.wait_ge(pv_done, PAIRS * b + 4 * half + 4)
                copy(oT_sb[:, 4 * half:4 * half + 4], ps[:, BANK_O].rearrange("p (c n) -> p c n", c=4)).then_inc(oT_done, 1)

            def a_step(k, t):
                if k == 1:
                    act.wait_ge(a_v_done, t + 1)
                    for j in range(2):
                        for hp in range(2):
                            src = ps[SP * j:SP * j + SP, BANK_A, 0:D].rearrange("p (r h d) -> p r h d", r=PAIRS, h=2)
                            copy(a_vb[SP * hp:SP * hp + SP, :, j, DH * hp:DH * hp + DH], src[:, :, hp]).then_inc(a_vb_done, 1)
                elif k == 2:
                    act.wait_ge(a_tqk_done, t + 1)
                    copy(a_qkT, ps[:, BANK_A].rearrange("p (c n) -> p c n", c=4)).then_inc(a_qkT_done, 1)
                elif k == 4:
                    act.wait_ge(a_sub_done, t + 1)
                    nc.scalar.activation(a_p, a_p, ACT.Exp).then_inc(a_exp_done, 1)
                elif k in (5, 6):
                    act.wait_ge(a_tp_done, 2 * t + k - 4)
                    copy(a_pT[:, 4 * (k - 5):4 * (k - 5) + 4], ps[:, BANK_A].rearrange("p (c n) -> p c n", c=4)).then_inc(a_pT_done, 1)
                elif k == 8:
                    act.wait_ge(a_to_done, t + 1)
                    copy(a_oT, ps[:, BANK_A, 0:D].rearrange("p (c n) -> p c n", c=CH)).then_inc(a_oT_done, 1)
                elif k == 9:
                    act.wait_ge(a_x1_done, t + 1)
                    copy(x1_all[:, bass.ds(t, 1)].rearrange("p a n -> p (a n)"), a_x1).then_inc(a_x1_kept, 1)
                elif k == 11:
                    act.wait_ge(a_txq_done, t + 1)
                    copy(a_xqT[:], ps[:, BANK_A].bitcast(BF16)[:, 0:D].rearrange("p (c n) -> p c n", c=CH)).then_inc(a_xqT_done, 1)
                elif k in (13, 14):
                    h = k - 13
                    act.wait_ge(a_tq_done, 2 * t + h + 1)
                    copy(q_st[:, 4 * h:4 * h + 4], ps[0:KS, BANK_A].rearrange("p (r n) -> p r n", r=4)).then_inc(a_qhi_done, 1)

            def b_step(k, t):
                if k == 1:
                    act.wait_ge(b_toq_done, t + 1)
                    copy(b_oqT, ps[:, BANK_A].bitcast(BF16)[:, 0:D].rearrange("p (c n) -> p c n", c=CH)).then_inc(b_oqT_done, 1)
                elif k == 4:
                    act.wait_ge(b_tx2_done, t + 1)
                    copy(b_x2T, ps[:, BANK_A, 0:D].rearrange("p (c n) -> p c n", c=CH)).then_inc(b_x2T_done, 1)
                    copy(acc[:, bass.ds(t, 1)].rearrange("p a n -> p (a n)"), b_x2).then_inc(b_x2_kept, 1)

            def batch(b, j, t_next, units_on, t_before):
                for slot in range(1, PAIRS + 1):
                    early, late = unit_slots(slot) if units_on else ([], [])
                    if slot == PAIRS // 2 + 1:
                        oT_step(b, 0)
                    pT_step(b, slot - 1, 0)
                    if t_before is not None:
                        b_step(B_SLOTS.get(PAIRS * j + slot, -1), t_before)
                    hurry = early and late and late[0] % 4 == 1
                    if hurry:
                        units(b + 1, 1 - j, early)
                    if slot < PAIRS:
                        exp_step(b, j, slot)
                    elif units_on:
                        exp_step(b + 1, 1 - j, 0)
                    if not hurry:
                        units(b + 1, 1 - j, early)
                    pT_step(b, slot - 1, 2)
                    if t_next is not None:
                        a_step(A_AT.get(PAIRS * j + slot, -1), t_next)
                    units(b + 1, 1 - j, late)
                oT_step(b, 1)

            act.wait_ge(kv_in, 16 * len(FOR_KV))
            for k in range(A_STEPS):
                if k < UNITS:
                    units(0, 0, [k])
                a_step(k, 0)
                if k in (4, 6):
                    weights_step(k // 2 - 2)
            exp_step(0, 0, 0)
            batch(0, 0, 1, True, None)
            batch(1, 1, 1, True, None)
            with act.Fori(1, TILES - 1) as it:
                batch(2 * it, 0, it + 1, True, it - 1)
                batch(2 * it + 1, 1, it + 1, True, it - 1)
            batch(B - 2, 0, None, True, TILES - 2)
            batch(B - 1, 1, None, False, TILES - 2)
            for k in range(6):
                b_step(k, TILES - 1)

            act.wait_ge(p_dve, at["gaps"])
            nc.scalar.activation(sm[:, 8], sm[:, 7], ACT.Exp).then_inc(p_act, 1)

            def xgT_step(g):
                act.wait_ge(tx_done, g + 1)
                copy(xgT[:], ps[:, XG_BANK, 0:D].rearrange("p (c n) -> p c n", c=CH)).then_inc(xgT_done, 1)

            def gelu_step(g):
                act.wait_ge(hb_done, 2 * g + 2)
                nc.scalar.activation(hg[:], hb[:], ACT.Gelu_apprx_tanh).then_inc(gelu_done, 1)

            def around(g, left=GT):
                act.wait_ge(th_done, 2 * g + 1)
                copy(hT[:, 0:4], ps[:, TH_BANK].rearrange("p (f n) -> p f n", f=4)).then_inc(hT_act, 1)
                if left > 1:
                    gelu_step(g + 1)
                if left > 2:
                    xgT_step(g + 2)

            xgT_step(0)
            gelu_step(0)
            xgT_step(1)
            with act.Fori(0, GT - 3) as g:
                around(g)
            for left in (3, 2, 1):
                around(GT - left, left)

        @block.tensor
        def _(pe):
            mm = nc.tensor.matmul

            def transpose(dst, src, n):
                return nc.tensor.transpose(dst, src, (id16 if src.dtype == BF16 else id32)[0:n, 0:n])

            def weights_step(n):
                pe.wait_ge(set_pool, 8)
                pe.wait_ge(set_dve, 2 + 8 * n + 6)
                for g in range(CH):
                    for c in range(CH):
                        last = transpose(ps[:, BANK_S + n].bitcast(BF16)[:, c * D + g * P:c * D + g * P + P],
                                         w_int[n][:, g, c * P:c * P + P], P)
                last.then_inc(set_pe, 1)
                pe.wait_ge(set_dve, 2 + 8 * n + 8)
                mm(ps[:, BANK_T + n, 0:D], ones[:], w_diag[n].rearrange("p c n -> p (c n)"), start=True, stop=True).then_inc(set_pe, 1)

            SPLIT = ((0, 0), (0, 1), (1, 0))

            def unit(b, j, u, first=False):
                c, g = u // 4, u % 4
                place = (CHUNKS * j + c) % 2
                cs, ws = (ctx_hi, ctx_lo), (wkv_hi, wkv_lo)
                pe.wait_ge(ctx_lo_done, CHUNKS * b + c + 1)
                if not first:
                    pe.wait_ge(unit_out, UNITS * b + u)
                if g < 2:
                    for i, (x, w) in enumerate(SPLIT):
                        for k in range(CH):
                            last = mm(ps[:, BANK_KV, 0:MC], ws[w][:, k, P * g:P * g + P], cs[x][:, place, k, :],
                                      start=(i == 0 and k == 0), stop=(i == 2 and k == CH - 1))
                else:
                    for m in range(2):
                        a = MT * (2 * (g - 2) + m)
                        for i, (x, w) in enumerate(SPLIT):
                            for k in range(CH):
                                last = mm(ps[0:MT, BANK_KV, D * m:D * m + D], cs[x][:, place, k, a:a + MT], ws[w][:, k, D:2 * D],
                                          start=(i == 0 and k == 0), stop=(i == 2 and k == CH - 1))
                last.then_inc(unit_done, 1)

            def scores(b, j, p, first=False):
                if p == 0:
                    for g in range(CH):
                        pe.wait_ge(k_in[g], 48 * CHUNKS * (b + 1))
                if p % 4 == 0:
                    pe.wait_ge(qbd_done, 2 * b + p // 4 + 1)
                if not first:
                    pe.wait_ge(exp_done, PAIRS * b + p)
                for c in range(CHUNKS):
                    last = mm(ps[:, BANK_S + c, 0:MC], qbd[:, j, p].rearrange("p h s -> p (h s)"),
                              k_st[:, j, p, MC * c:MC * c + MC], start=True, stop=True)
                last.then_inc(s_done, 1)

            def tr(b, p, q):
                n = 3 * p + q
                pe.wait_ge(exp_done, PAIRS * b + p + 1)
                for i in range(TPC):
                    a = MC * q + MT * i
                    last = transpose(ps[0:MT, BANK_T + n % 2, P * i:P * i + P], pr[:, p % 2, a:a + MT], P)
                last.then_inc(tr_done, 1)

            def pv(b, j, p, q):
                n = 3 * p + q
                if q == 0 and p == 0:
                    pe.wait_ge(unit_out, UNITS * (b + 1))
                    pe.wait_ge(o_done, 2 * b + 1)
                if q == 0 and p == PAIRS // 2:
                    pe.wait_ge(oT_done, 2 * b + 1)
                if q == 1:
                    pe.wait_ge(pT_inner, PAIRS * b + p + 1)
                else:
                    pe.wait_ge(pT_outer, 2 * PAIRS * b + 2 * p + q // 2 + 1)
                for i in range(TPC):
                    last = mm(ps[32 * i:32 * i + 32, BANK_O, P * (p % 4):P * (p % 4) + P],
                              v_sb[0:MT, j, TPC * q + i, 32 * p:32 * p + 32], pT[0:MT, n % 2, i],
                              start=(q == 0), stop=(q == 2))
                if q == 2:
                    last.then_inc(pv_done, 1)

            def o_back(b):
                pe.wait_ge(oT_done, 2 * b + 2)
                for p in range(PAIRS):
                    last = mm(ps[:, BANK_O, 32 * p:32 * p + 32], oT_sb[:, p], sel_sb[:], start=True, stop=True)
                last.then_inc(o_back_done, 1)

            def a_step(k, t, first=False):
                A = ps[:, BANK_A]
                if k == 0:
                    pe.wait_ge(x_in, 32 * (t + 1))
                    if not first:
                        pe.wait_ge(a_qlo_done, 2 * t)
                    for c in range(CH):
                        last = mm(A, a_xT[:, c], wqkv_sb[:, c, 0:2 * D], start=(c == 0), stop=(c == CH - 1))
                    last.then_inc(a_qk_done, 1)
                elif k == 1:
                    pe.wait_ge(a_rope_mul, 3 * t + 3)
                    for c in range(CH):
                        last = mm(A[:, 0:D], a_xT[:, c], wqkv_sb[:, c, 2 * D:3 * D], start=(c == 0), stop=(c == CH - 1))
                    last.then_inc(a_v_done, 1)
                elif k == 2:
                    pe.wait_ge(a_rope, t + 1)
                    pe.wait_ge(a_vb_done, 4 * t + 4)
                    for c in range(4):
                        last = transpose(A[:, P * c:P * c + P], a_t1[:, P * c:P * c + P], P)
                    last.then_inc(a_tqk_done, 1)
                elif k in (3, 4):
                    g = k - 3
                    pe.wait_ge(a_kbd_done, 4 * t + 4)
                    if g == 1:
                        pe.wait_ge(a_masked, 2 * t + 1)
                    for j in range(2):
                        last = mm(ps[SP * j:SP * j + SP, BANK_A], a_qkT[:, g, SP * j:SP * j + SP],
                                  a_kbd[:, j, g].rearrange("p h s -> p (h s)"), start=True, stop=True)
                    last.then_inc(a_s_done, 1)
                elif k in (5, 6):
                    pe.wait_ge(a_exp_done, t + 1)
                    if k == 6:
                        pe.wait_ge(a_pT_done, 2 * t + 1)
                    for r in range(4):
                        a = P * (4 * (k - 5) + r)
                        last = transpose(A[:, P * r:P * r + P], a_p[:, a:a + P], P)
                    last.then_inc(a_tp_done, 1)
                elif k == 7:
                    pe.wait_ge(a_pT_done, 2 * t + 2)
                    for r in range(PAIRS):
                        last = mm(A[:, 64 * r:64 * r + 64], a_pT[:, r], a_vb[:, r].rearrange("p j d -> p (j d)"), start=True, stop=True)
                    last.then_inc(a_pv_done, 1)
                elif k == 8:
                    pe.wait_ge(a_o_done, 2 * t + 2)
                    for c in range(CH):
                        last = transpose(A[:, P * c:P * c + P], a_o[:, P * c:P * c + P], P)
                    last.then_inc(a_to_done, 1)
                elif k == 9:
                    pe.wait_ge(a_oT_done, t + 1)
                    for c in range(CH):
                        last = mm(A[:, 0:D], a_oT[:, c], wout_sb[:, c], start=(c == 0), stop=(c == CH - 1))
                    last.then_inc(a_out_done, 1)
                elif k == 11:
                    pe.wait_ge(a_xq_done, t + 1)
                    for c in range(CH):
                        last = transpose(A.bitcast(BF16)[:, P * c:P * c + P], a_xq[:, P * c:P * c + P], P)
                    last.then_inc(a_txq_done, 1)
                elif k == 12:
                    pe.wait_ge(a_xqT_done, t + 1)
                    for c in range(CH):
                        last = mm(A[:, 0:D], a_xqT[:, c], wqqT[:, c], start=(c == 0), stop=(c == CH - 1))
                    last.then_inc(a_qp_done, 1)
                elif k in (13, 14):
                    h = k - 13
                    if h == 0:
                        pe.wait_ge(a_q_done, t + 1)
                    else:
                        pe.wait_ge(a_qlo_done, 2 * t + 1)
                    for r in range(4):
                        last = transpose(A[0:KS, P * r:P * r + P], a_q3[:, 4 * h + r].rearrange("p i d -> p (i d)"), P)
                    last.then_inc(a_tq_done, 1)

            def b_step(k, t, beside=False):
                A = ps[:, BANK_A]
                if k == 1:
                    if beside:
                        pe.wait_ge(a_rope, t + 3)
                        pe.wait_ge(a_vb_done, 4 * t + 12)
                    pe.wait_ge(b_oq_done, t + 1)
                    for c in range(CH):
                        last = transpose(A.bitcast(BF16)[:, P * c:P * c + P], b_oq[:, P * c:P * c + P], P)
                    last.then_inc(b_toq_done, 1)
                elif k == 2:
                    if beside:
                        pe.wait_ge(a_qkT_done, t + 3)
                    pe.wait_ge(b_oqT_done, t + 1)
                    for c in range(CH):
                        last = mm(A[:, 0:D], b_oqT[:, c], wpqT[:, c], start=(c == 0), stop=(c == CH - 1))
                    last.then_inc(b_p_done, 1)
                elif k == 4:
                    if beside:
                        pe.wait_ge(a_pT_done, 2 * t + 6)
                    pe.wait_ge(b_x2_done, t + 1)
                    for c in range(CH):
                        last = transpose(A[:, P * c:P * c + P], b_x2[:, P * c:P * c + P], P)
                    last.then_inc(b_tx2_done, 1)
                elif k == 5:
                    if beside:
                        pe.wait_ge(a_o_done, 2 * t + 6)
                    pe.wait_ge(b_x2T_done, t + 1)
                    for c in range(CH):
                        last = mm(A[:, 0:E], b_x2T[:, c], gw_sb[:, c], start=(c == 0), stop=(c == CH - 1))
                    last.then_inc(b_gate_done, 1)

            def b_over(k, t):
                if k in (1, 2, 4, 5):
                    pe.wait_ge({1: b_oqT_done, 2: b_sum, 4: b_x2T_done, 5: b_lg_done}[k], 3 * t + 1 if k == 2 else t + 1)

            def batch(b, j, t_next, units_on, t_before):
                for slot in range(1, PAIRS + 1):
                    if slot < PAIRS:
                        scores(b, j, slot)
                    elif units_on:
                        scores(b + 1, 1 - j, 0)
                    early, late = unit_slots(slot) if units_on else ([], [])
                    if slot > 1:
                        pv(b, j, slot - 2, 2)
                    tr(b, slot - 1, 0)
                    tr(b, slot - 1, 1)
                    bk = B_SLOTS.get(PAIRS * j + slot, -1)
                    if t_before is not None:
                        b_step(bk, t_before, t_next is not None)
                    for u in early:
                        unit(b + 1, 1 - j, u)
                    pv(b, j, slot - 1, 0)
                    tr(b, slot - 1, 2)
                    pv(b, j, slot - 1, 1)
                    if t_next is not None:
                        if t_before is not None:
                            b_over(bk, t_before)
                        a_step(A_AT.get(PAIRS * j + slot, -1), t_next)
                    if slot == PAIRS:
                        pv(b, j, PAIRS - 1, 2)
                    for u in late:
                        unit(b + 1, 1 - j, u)
                o_back(b)

            pe.wait_ge(set_dve, 2)
            pe.wait_ge(set_pool, 5)
            for k in range(A_STEPS):
                if k < UNITS:
                    unit(0, 0, k, k == 0)
                if k == 0:
                    pe.wait_ge(dec_in, 16 * len(FOR_DEC))
                a_step(k, 0, True)
                if k in (4, 6):
                    weights_step(k // 2 - 2)
            pe.wait_ge(set_act, 4)
            scores(0, 0, 0, True)
            batch(0, 0, 1, True, None)
            batch(1, 1, 1, True, None)
            with pe.Fori(1, TILES - 1) as it:
                batch(2 * it, 0, it + 1, True, it - 1)
                batch(2 * it + 1, 1, it + 1, True, it - 1)
            batch(B - 2, 0, None, True, TILES - 2)
            batch(B - 1, 1, None, False, TILES - 2)
            for k in range(6):
                b_step(k, TILES - 1)

            pe.wait_ge(p_dve, at["choices"])
            choices = oh16[:].rearrange("p t e -> p (t e)")
            mm(ps[:, 5, 0:TILES * E], before16[:], choices, start=True, stop=True).then_inc(p_pe, 1)
            mm(ps[:, 6, 0:TILES * E], ones16[:], choices, start=True, stop=True).then_inc(p_pe, 1)

            def expert_of(g):
                e = pe.value_load(e_tab[0:1, bass.ds(g, 1)], min_val=0, max_val=E - 1)
                pe.wait_ge(w_ready, e + 1)
                return e

            def tx(g):
                pe.wait_ge(xg_in, 16 * (g + 1))
                for c in range(CH):
                    last = transpose(ps[:, XG_BANK, P * c:P * c + P], xg[:, P * c:P * c + P], P)
                last.then_inc(tx_done, 1)

            def m1(g, e, i, first=False):
                if i == 0:
                    pe.wait_ge(xgT_done, g + 1)
                if not first:
                    pe.wait_ge(hb_done, 2 * g - 1 + i)
                for c in range(CH):
                    last = mm(ps[:, H_BANK + i], xgT[:, c],
                              w1_sb[:, bass.ds(e, 1), c, 512 * i:512 * i + 512].rearrange("p a n -> p (a n)"),
                              start=(c == 0), stop=(c == CH - 1))
                last.then_inc(m1_done, 1)

            def th(g):
                pe.wait_ge(gelu_done, g + 1)
                for f in range(FT):
                    last = transpose(ps[:, TH_BANK + f // 4, P * (f % 4):P * (f % 4) + P], hg[:, P * f:P * f + P], P)
                    if f % 4 == 3:
                        last.then_inc(th_done, 1)

            def m2(g, e, first=False):
                pe.wait_ge(hT_act, g + 1)
                pe.wait_ge(hT_dve, g + 1)
                if not first:
                    pe.wait_ge(y_ready, g)
                for f in range(FT):
                    last = mm(ps[:, Y_BANK, 0:D], hT[:, f],
                              w2_sb[:, bass.ds(e, 1), f].rearrange("p a n -> p (a n)"), start=(f == 0), stop=(f == FT - 1))
                last.then_inc(m2_done, 1)

            def around(g, left=GT, first=False):
                if left > 1:
                    e_next = expert_of(g + 1)
                    m1(g + 1, e_next, 0)
                th(g)
                if left > 1:
                    m1(g + 1, e_next, 1)
                if left > 2:
                    tx(g + 2)
                m2(g, expert_of(g), first)

            pe.wait_ge(p_dve, at["tiles known"])
            tx(0)
            e0 = expert_of(0)
            m1(0, e0, 0, True)
            m1(0, e0, 1, True)
            tx(1)
            around(0, first=True)
            with pe.Fori(1, GT - 3) as g:
                around(g)
            for left in (3, 2, 1):
                around(GT - left, left)


def dump_rows():
    row, tile, choice = np.ogrid[0:P, 0:TILES, 0:2]
    return np.where(row % SP < S, 0, DUMP + (choice * TILES + tile) * P + row).astype(np.float32)


def tables():
    pos = (np.arange(P) % SP).astype(np.float32)
    inv = (1.0 / 10000.0 ** (np.arange(0, DH, 2, dtype=np.float32) / DH)).astype(np.float32)
    freqs = np.outer(pos, inv).astype(np.float32)
    emb = np.concatenate([freqs, freqs], axis=-1)
    cos, sin = np.cos(emb).astype(np.float32), np.sin(emb).astype(np.float32)
    sin_pair = np.stack([-sin[:, 0::2], sin[:, 1::2]], axis=1)
    head = (np.arange(P)[:, None] // DH == np.arange(HG)[None, :]).astype(np.float32) * np.float32(DH ** -0.5)
    pair = (np.arange(KS)[:, None] % PD // DH == np.arange(2)[None, :]).astype(np.float32)
    causal = np.where(np.arange(SP)[None, :] <= (np.arange(P) % SP)[:, None], 0.0, MASKED).astype(np.float32)
    return {"rope_cos": cos, "rope_sin": np.ascontiguousarray(sin_pair), "head_mask": head, "pair_mask": pair, "causal": causal,
            "ident": np.eye(P, dtype=np.float32), "sel": np.tile(np.eye(32, dtype=np.float32), (P // 32, 1)),
            "before": np.triu(np.ones((P, P), np.float32), 1),
            "valid": (np.arange(P) % SP < S).astype(np.float32).reshape(P, 1), "dump": dump_rows(),
            "iota_tiles": np.ascontiguousarray(np.broadcast_to(np.arange(GT, dtype=np.float32), (P, GT))),
            "iota_row": np.ascontiguousarray(np.broadcast_to(np.arange(E, dtype=np.float32), (P, E)))}


def kernel(x, ctx_2048, L0_attn_w_qkv, L0_attn_w_out, L0_attn_w_c1, L0_attn_w_c2, L0_xattn_wq, L0_xattn_bq,
           L0_xattn_wkv, L0_xattn_bkv, L0_xattn_wp, L0_xattn_bp, L0_ffn_gate_w, L0_ffn_gate_b, L0_ffn_w1, L0_ffn_b1,
           L0_ffn_w2, L0_ffn_b2):
    import concourse.bacc as bacc
    from concourse.bass_utils import run_bass_kernel_spmd

    def halves(a):
        return a.reshape(-1, P, a.shape[-1]).transpose(1, 0, 2)

    def rows(v):
        return np.broadcast_to(v.reshape(1, -1), (P, v.size))

    xp = np.zeros((B, SP, D), np.asarray(x).dtype)
    xp[:, :S] = np.asarray(x)
    xp = xp.reshape(TILES, P, D)
    ct = np.asarray(ctx_2048).reshape(B, CHUNKS, MC, CH, P).transpose(0, 1, 4, 3, 2)
    wkv, bkv = np.asarray(L0_xattn_wkv), np.asarray(L0_xattn_bkv)
    arrays = {
        "x_tok": xp, "x_T": xp.reshape(TILES, P, CH, P).transpose(0, 3, 2, 1), "ctx_T": ct,
        "w_qkv_T": halves(np.asarray(L0_attn_w_qkv).T), "w_out_T": halves(np.asarray(L0_attn_w_out).T),
        "wq": halves(np.asarray(L0_xattn_wq)), "bq_row": rows(np.asarray(L0_xattn_bq)),
        "w_kv_T": halves(wkv.T), "bk_col": bkv[:D].reshape(CH, P).T, "bv_row": rows(bkv[D:]),
        "wp": halves(np.asarray(L0_xattn_wp)), "bp_row": rows(np.asarray(L0_xattn_bp)),
        "gate_w": halves(np.asarray(L0_ffn_gate_w)), "gate_b_row": rows(np.asarray(L0_ffn_gate_b)),
        "w1": np.asarray(L0_ffn_w1).reshape(E, CH, P, F).transpose(0, 2, 1, 3),
        "b1": np.asarray(L0_ffn_b1),
        "w2": np.asarray(L0_ffn_w2).reshape(E, FT, P, D).transpose(0, 2, 1, 3), "b2": np.asarray(L0_ffn_b2),
    }
    arrays.update(tables())
    arrays = {k: np.ascontiguousarray(v) for k, v in arrays.items()}
    nc = bacc.Bacc("TRN2", target_bir_lowering=False, num_devices=1)
    args = {k: nc.dram_tensor(k, v.shape, mybir.dt.from_np(v.dtype), kind="ExternalInput").ap() for k, v in arrays.items()}
    out = nc.dram_tensor("out", (B, S, D), F32, kind="ExternalOutput").ap()
    decoder_layer(nc, **args, out=out)
    r = run_bass_kernel_spmd(nc, [arrays], core_ids=[0])
    return r.results[0]["out"]
```
